# Optimizing a Trainium2 kernel written in Bass

```python
import numpy as np
import jax
import jax.numpy as jnp

def _softmax(x, axis=-1):
    return jax.nn.softmax(x, axis=axis)

def _gelu(x):
    return jax.nn.gelu(x, approximate=True)

def _silu(x):
    return jax.nn.silu(x)

def _sigmoid(x):
    return jax.nn.sigmoid(x)

def _layernorm(x, axis=-1, eps=1e-05):
    m = jnp.mean(x, axis=axis, keepdims=True)
    v = jnp.var(x, axis=axis, keepdims=True)
    return (x - m) / jnp.sqrt(v + eps)

def _scatter_add(tgt, idx, src, axis=0):
    return tgt.at[idx].add(src)

def _segment_sum(src, seg, n):
    return jax.ops.segment_sum(src, seg, n)
kernel_name = 'mk_adaln_d1_jaxref_r4_e2a5cf'

def setup_inputs(seed: int=0):
    np.random.seed(seed)
    _w = jnp.asarray

    def _L0_attn_setup():
        import jax, jax.numpy as jnp
        import numpy as np
        D = 256
        H = 16
        DH = 64
        K = 4
        C = H * DH

        def _causal_conv(x, w, b):
            y = jax.lax.conv_general_dilated(x, w, window_strides=(1,), padding=[(K - 1, 0)], feature_group_count=C, dimension_numbers=('NCH', 'OIH', 'NCH'))
            return y + b[None, :, None]
        key = jax.random.key(seed)
        ks = jax.random.split(key, 16)
        s = 0.02
        w = lambda k, shape: jax.random.normal(k, shape, jnp.float32) * s
        return {'hidden_states': jax.random.normal(ks[0], (4, 512, D), jnp.float32), 'Wq': w(ks[1], (C, D)), 'Wk': w(ks[2], (C, D)), 'Wv': w(ks[3], (C, D)), 'Wa': w(ks[4], (H, D)), 'ba': jnp.zeros((H,), jnp.float32), 'Wb': w(ks[5], (H, D)), 'bb': jnp.zeros((H,), jnp.float32), 'conv_q_w': w(ks[6], (C, 1, K)), 'conv_q_b': jnp.zeros((C,), jnp.float32), 'conv_k_w': w(ks[7], (C, 1, K)), 'conv_k_b': jnp.zeros((C,), jnp.float32), 'conv_v_w': w(ks[8], (C, 1, K)), 'conv_v_b': jnp.zeros((C,), jnp.float32), 'Wg': w(ks[9], (C, D)), 'bg': jnp.zeros((C,), jnp.float32), 'Wo': w(ks[10], (D, C))}
    _L0_attn_in = _L0_attn_setup()

    def _L0_ffn_setup():
        import jax, jax.numpy as jnp
        import numpy as np
        S, B, H, F, E, K = (512, 2, 256, 512, 8, 2)

        def _moe_forward(hidden_states, router_w, w1, b1, w2, b2):
            s, b, h = hidden_states.shape
            T = s * b
            x = hidden_states.reshape(T, h)
            logits = jnp.einsum('th,eh->te', x, router_w)
            topk_logits, topk_idx = jax.lax.top_k(logits, K)
            probs = jax.nn.softmax(topk_logits, axis=-1)
            combine = jnp.zeros((T, E), dtype=x.dtype)
            combine = combine.at[jnp.arange(T)[:, None], topk_idx].add(probs.astype(x.dtype))
            hmid = jnp.einsum('th,efh->etf', x, w1) + b1[:, None, :]
            hmid = jax.nn.gelu(hmid, approximate=False)
            y = jnp.einsum('etf,ehf->eth', hmid, w2) + b2[:, None, :]
            out = jnp.einsum('eth,te->th', y, combine)
            return out.reshape(s, b, h)
        key = jax.random.key(seed)
        ks = jax.random.split(key, 6)
        std = 0.02
        return {'hidden_states': jax.random.normal(ks[0], (S, B, H), dtype=jnp.float32), 'router_w': jax.random.normal(ks[1], (E, H), dtype=jnp.float32) * std, 'w1': jax.random.normal(ks[2], (E, F, H), dtype=jnp.float32) * (1.0 / np.sqrt(H)), 'b1': jnp.zeros((E, F), dtype=jnp.float32), 'w2': jax.random.normal(ks[3], (E, H, F), dtype=jnp.float32) * (1.0 / np.sqrt(F)), 'b2': jnp.zeros((E, H), dtype=jnp.float32)}
    _L0_ffn_in = _L0_ffn_setup()
    _L0_c = _w((lambda *s: np.random.randn(*s).astype(np.float32) * 0.05)(4, 256))
    _L0_wmod = _w((lambda *s: np.random.randn(*s).astype(np.float32) * 0.05)(256, 6 * 256) * 256 ** (-0.5))
    _d = {'L0_attn_hidden_states': _L0_attn_in['hidden_states'], 'L0_attn_Wq': _L0_attn_in['Wq'], 'L0_attn_Wk': _L0_attn_in['Wk'], 'L0_attn_Wv': _L0_attn_in['Wv'], 'L0_attn_Wa': _L0_attn_in['Wa'], 'L0_attn_ba': _L0_attn_in['ba'], 'L0_attn_Wb': _L0_attn_in['Wb'], 'L0_attn_bb': _L0_attn_in['bb'], 'L0_attn_conv_q_w': _L0_attn_in['conv_q_w'], 'L0_attn_conv_q_b': _L0_attn_in['conv_q_b'], 'L0_attn_conv_k_w': _L0_attn_in['conv_k_w'], 'L0_attn_conv_k_b': _L0_attn_in['conv_k_b'], 'L0_attn_conv_v_w': _L0_attn_in['conv_v_w'], 'L0_attn_conv_v_b': _L0_attn_in['conv_v_b'], 'L0_attn_Wg': _L0_attn_in['Wg'], 'L0_attn_bg': _L0_attn_in['bg'], 'L0_attn_Wo': _L0_attn_in['Wo'], 'L0_ffn_router_w': _L0_ffn_in['router_w'], 'L0_ffn_w1': _L0_ffn_in['w1'], 'L0_ffn_b1': _L0_ffn_in['b1'], 'L0_ffn_w2': _L0_ffn_in['w2'], 'L0_ffn_b2': _L0_ffn_in['b2'], 'L0_c': _L0_c, 'L0_wmod': _L0_wmod}
    _x0 = _d['L0_attn_hidden_states']
    _d['L0_attn_hidden_states'] = jax.random.normal(jax.random.fold_in(jax.random.key(seed), 1), (4, 1024, 256), dtype=_x0.dtype)
    del _x0
    return _d

def reference(L0_attn_hidden_states, L0_attn_Wq, L0_attn_Wk, L0_attn_Wv, L0_attn_Wa, L0_attn_ba, L0_attn_Wb, L0_attn_bb, L0_attn_conv_q_w, L0_attn_conv_q_b, L0_attn_conv_k_w, L0_attn_conv_k_b, L0_attn_conv_v_w, L0_attn_conv_v_b, L0_attn_Wg, L0_attn_bg, L0_attn_Wo, L0_ffn_router_w, L0_ffn_w1, L0_ffn_b1, L0_ffn_w2, L0_ffn_b2, L0_c, L0_wmod):

    def _L0_attn_ref(hidden_states, Wq, Wk, Wv, Wa, ba, Wb, bb, conv_q_w, conv_q_b, conv_k_w, conv_k_b, conv_v_w, conv_v_b, Wg, bg, Wo):
        import jax, jax.numpy as jnp
        import numpy as np
        D = 256
        H = 16
        DH = 64
        K = 4
        C = H * DH

        def _causal_conv(x, w, b):
            y = jax.lax.conv_general_dilated(x, w, window_strides=(1,), padding=[(K - 1, 0)], feature_group_count=C, dimension_numbers=('NCH', 'OIH', 'NCH'))
            return y + b[None, :, None]
        B, T, _ = hidden_states.shape
        q = jnp.einsum('btd,cd->bct', hidden_states, Wq)
        k = jnp.einsum('btd,cd->bct', hidden_states, Wk)
        v = jnp.einsum('btd,cd->bct', hidden_states, Wv)
        q = jax.nn.silu(_causal_conv(q, conv_q_w, conv_q_b))
        k = jax.nn.silu(_causal_conv(k, conv_k_w, conv_k_b))
        v = jax.nn.silu(_causal_conv(v, conv_v_w, conv_v_b))
        q = q.transpose(0, 2, 1).reshape(B, T, H, DH)
        k = k.transpose(0, 2, 1).reshape(B, T, H, DH)
        v = v.transpose(0, 2, 1).reshape(B, T, H, DH)
        k = k / jnp.maximum(jnp.linalg.norm(k, axis=-1, keepdims=True), 1e-12)
        alpha = jax.nn.sigmoid(jnp.einsum('btd,hd->bth', hidden_states, Wa) + ba)
        beta = jax.nn.sigmoid(jnp.einsum('btd,hd->bth', hidden_states, Wb) + bb)

        def step(S, xs):
            kt, vt, qt, at, bt = xs
            v_old = jnp.einsum('bhij,bhj->bhi', S, kt)
            upd = vt - at[..., None] * v_old
            dS = upd[..., :, None] * kt[..., None, :]
            S = jnp.clip(at[..., None, None] * S + bt[..., None, None] * dS, -5.0, 5.0)
            ot = jnp.einsum('bhij,bhj->bhi', S, qt)
            return (S, ot)
        S0 = jnp.zeros((B, H, DH, DH), hidden_states.dtype)
        xs = (k.transpose(1, 0, 2, 3), v.transpose(1, 0, 2, 3), q.transpose(1, 0, 2, 3), alpha.transpose(1, 0, 2), beta.transpose(1, 0, 2))
        _, ys = jax.lax.scan(step, S0, xs)
        y = ys.transpose(1, 0, 2, 3).reshape(B, T, C)
        g = jax.nn.silu(jnp.einsum('btd,cd->btc', hidden_states, Wg) + bg)
        y = y * g
        out = jnp.einsum('btc,dc->btd', y, Wo)
        return out

    def _L0_ffn_ref(hidden_states, router_w, w1, b1, w2, b2):
        import jax, jax.numpy as jnp
        import numpy as np
        S, B, H, F, E, K = (512, 2, 256, 512, 8, 2)

        def _moe_forward(hidden_states, router_w, w1, b1, w2, b2):
            s, b, h = hidden_states.shape
            T = s * b
            x = hidden_states.reshape(T, h)
            logits = jnp.einsum('th,eh->te', x, router_w)
            topk_logits, topk_idx = jax.lax.top_k(logits, K)
            probs = jax.nn.softmax(topk_logits, axis=-1)
            combine = jnp.zeros((T, E), dtype=x.dtype)
            combine = combine.at[jnp.arange(T)[:, None], topk_idx].add(probs.astype(x.dtype))
            hmid = jnp.einsum('th,efh->etf', x, w1) + b1[:, None, :]
            hmid = jax.nn.gelu(hmid, approximate=False)
            y = jnp.einsum('etf,ehf->eth', hmid, w2) + b2[:, None, :]
            out = jnp.einsum('eth,te->th', y, combine)
            return out.reshape(s, b, h)
        return _moe_forward(hidden_states, router_w, w1, b1, w2, b2)
    x = L0_attn_hidden_states
    mod = (_silu(L0_c) @ L0_wmod).reshape(L0_c.shape[0], 6, 1, -1)
    sa, ca, ga, sb, cb, gb = (mod[:, 0], mod[:, 1], mod[:, 2], mod[:, 3], mod[:, 4], mod[:, 5])
    ga = (2 * (ga >= 0) - 1) * jnp.maximum(jnp.abs(ga), 0.25)
    gb = (2 * (gb >= 0) - 1) * jnp.maximum(jnp.abs(gb), 0.25)
    h = _layernorm(x, axis=-1) * (1 + ca) + sa
    x = x + ga * _L0_attn_ref(h, L0_attn_Wq, L0_attn_Wk, L0_attn_Wv, L0_attn_Wa, L0_attn_ba, L0_attn_Wb, L0_attn_bb, L0_attn_conv_q_w, L0_attn_conv_q_b, L0_attn_conv_k_w, L0_attn_conv_k_b, L0_attn_conv_v_w, L0_attn_conv_v_b, L0_attn_Wg, L0_attn_bg, L0_attn_Wo)
    h = _layernorm(x, axis=-1) * (1 + cb) + sb
    x = x + gb * _L0_ffn_ref(h, L0_ffn_router_w, L0_ffn_w1, L0_ffn_b1, L0_ffn_w2, L0_ffn_b2)
    return x

_drawn_inputs = setup_inputs


def setup_inputs(seed=0):
    import zlib

    import numpy as np

    out = dict(_drawn_inputs(seed))
    spreads = {'L0_attn_ba': (0.0, 0.8),
     'L0_attn_bb': (0.0, 0.8),
     'L0_attn_conv_q_b': (0.0, 0.8),
     'L0_attn_conv_k_b': (0.0, 0.8),
     'L0_attn_conv_v_b': (0.0, 0.8),
     'L0_attn_bg': (0.0, 0.8),
     'L0_ffn_b1': (0.0, 0.66),
     'L0_ffn_b2': (0.0, 0.452)}
    factors = {'L0_attn_Wq': 8.0,
     'L0_attn_Wk': 8.0,
     'L0_attn_Wv': 8.0,
     'L0_attn_Wa': 8.0,
     'L0_attn_Wb': 8.0,
     'L0_attn_conv_q_w': 8.0,
     'L0_attn_conv_k_w': 8.0,
     'L0_attn_conv_v_w': 8.0,
     'L0_attn_Wg': 8.0,
     'L0_attn_Wo': 8.0}
    for name, (base, spread) in spreads.items():
        noise = np.random.default_rng([zlib.crc32(name.encode()), seed]).standard_normal(out[name].shape)
        drawn = base * np.exp(spread * noise) if base else spread * noise
        out[name] = jnp.asarray(drawn.astype(out[name].dtype))
    for name, factor in factors.items():
        out[name] = (out[name] * factor).astype(out[name].dtype)
    return out
```

```python
from contextlib import ExitStack

import concourse.bass as bass
from concourse import mybir

ALU = mybir.AluOpType
ACT = mybir.ActivationFunctionType
F32 = mybir.dt.float32
AX_X = mybir.AxisListType.X

P = 128
B, T, D = 4, 1024, 256
H, DH = 16, 64
C = H * DH
E, F = 8, 512
DC = D // P
M = C // P
FC = F // P
NT = T // P
G = 512
GH = T // G
GT = G // P
CLIP = 5.0
LN_EPS = 1e-5
NORM_EPS = 1e-12
SA, CA, GA, SB, CB, GB = range(6)


def adaln_delta_moe(nc, x, cT, wmod, wqkv, convp, wg, bg, wab, bab, wo, rw, w1, b1, w2, b2,
                    ident_d, ones2_d, out, qkv_s, ab_s, y_s):
    with ExitStack() as top:
        def sb_in(stack):
            return lambda name, shape: stack.enter_context(nc.sbuf_tensor(name, shape, F32))

        def ps_in(stack):
            return lambda name, shape: stack.enter_context(nc.psum_tensor(name, shape, F32))

        def sem(name):
            return top.enter_context(nc.semaphore(name))

        sb = sb_in(top)
        ident = sb("ident", [P, P])
        ones2 = sb("ones2", [P, P])
        modT = sb("modT", [P, 12, B])
        gates = sb("gates", [P, 2, B, D])
        rw_sb = sb("rw_sb", [P, DC, E])
        x1 = sb("x1", [P, B * NT, D])

        modulation(nc, top, sem, cT, wmod, rw, ident_d, ones2_d, ident, ones2, modT, gates, rw_sb)

        with ExitStack() as attn:
            asb = sb_in(attn)
            hT = asb("hT", [P, DC, B * T])
            norm_first(nc, sem, x, ident, modT, hT)
            gate_scalars(nc, sem, wab, bab, hT, ab_s)
            project(nc, sem, wqkv, convp, ones2, hT, qkv_s)
            scan(nc, sem, ones2, qkv_s, ab_s, y_s)
            attn_out(nc, sem, x, y_s, wg, bg, wo, hT, gates, x1)
        h2T = sb("h2T", [P, DC, B * T])
        comb = sb("comb", [P, B * NT, E])
        acc = sb("acc", [P, B * NT, D])
        norm_second(nc, sem, ident, modT, rw_sb, b2, x1, h2T, comb, acc)
        experts(nc, sem, w1, b1, w2, h2T, comb, acc)
        finish(nc, sem, gates, x1, acc, out)


def modulation(nc, top, sem, cT, wmod, rw, ident_d, ones2_d, ident, ones2, modT, gates, rw_sb):
    s_load, s_silu, s_bc = sem("mod_loaded"), sem("mod_silu"), sem("mod_spread")
    s_col, s_row, s_v = sem("mod_columns"), sem("mod_rows"), sem("mod_vector")
    with ExitStack() as st:
        c_sb = st.enter_context(nc.sbuf_tensor("c_sb", [P, DC, B], F32))
        sc = st.enter_context(nc.sbuf_tensor("silu_c", [P, DC, B], F32))
        scb = st.enter_context(nc.sbuf_tensor("silu_c_spread", [P, DC, B, P], F32))
        wm = st.enter_context(nc.sbuf_tensor("wmod_sb", [P, DC, 6 * D], F32))
        absg = st.enter_context(nc.sbuf_tensor("gate_size", [P, 2 * B * D], F32))
        sgn = st.enter_context(nc.sbuf_tensor("gate_sign", [P, 2 * B * D], F32))
        raw = st.enter_context(nc.sbuf_tensor("gate_raw", [P, 2 * B * D], F32))
        ones = st.enter_context(nc.sbuf_tensor("ones_row", [P, P], F32))
        pm = st.enter_context(nc.psum_tensor("pm", [P, 12, B], F32))
        pg = st.enter_context(nc.psum_tensor("pg", [P, 2 * B, D], F32))
        block = st.enter_context(nc.Block())

        @block.sync
        def _(sp):
            sp.dma_start(c_sb[:], cT).then_inc(s_load, 16)
            sp.dma_start(wm[:], wmod).then_inc(s_load, 16)
            sp.dma_start(ident[:], ident_d).then_inc(s_load, 16)
            sp.dma_start(ones2[:], ones2_d).then_inc(s_load, 16)
            sp.dma_start(rw_sb[:], rw).then_inc(s_load, 16)
            sp.wait_ge(s_load, 80)

        @block.scalar
        def _(act):
            act.wait_ge(s_load, 80)
            nc.scalar.activation(sc[:], c_sb[:], ACT.Silu).then_inc(s_silu, 1)

        @block.vector
        def _(dve):
            nc.vector.memset(ones[:], 1.0).then_inc(s_v, 1)
            dve.wait_ge(s_v, 1)
            dve.wait_ge(s_silu, 1)
            for dc in range(DC):
                for b in range(B):
                    last = nc.vector.tensor_scalar(scb[:, dc, b, :], ones[:], sc[:, dc, b:b + 1], None, ALU.mult)
            last.then_inc(s_bc, 1)
            dve.wait_ge(s_col, 1)
            nc.vector.tensor_copy(modT[:], pm[:]).then_inc(s_v, 1)
            dve.wait_ge(s_v, 2)
            for part in (CA, CB):
                nc.vector.tensor_scalar(modT[:, 2 * part:2 * part + 2, :], modT[:, 2 * part:2 * part + 2, :], 1.0, None,
                                        ALU.add).then_inc(s_v, 1)
            dve.wait_ge(s_row, 1)
            nc.vector.tensor_copy(raw[:], pg[:].rearrange("p a d -> p (a d)")).then_inc(s_v, 1)
            dve.wait_ge(s_v, 5)
            nc.vector.tensor_scalar(sgn[:], raw[:], 0.0, 2.0, ALU.is_ge, ALU.mult).then_inc(s_v, 1)
            nc.vector.tensor_scalar(absg[:], raw[:], -1.0, None, ALU.mult).then_inc(s_v, 1)
            dve.wait_ge(s_v, 7)
            nc.vector.tensor_tensor(absg[:], absg[:], raw[:], ALU.max).then_inc(s_v, 1)
            nc.vector.tensor_scalar(sgn[:], sgn[:], -1.0, None, ALU.add).then_inc(s_v, 1)
            dve.wait_ge(s_v, 9)
            nc.vector.tensor_scalar(absg[:], absg[:], 0.25, None, ALU.max).then_inc(s_v, 1)
            dve.wait_ge(s_v, 10)
            nc.vector.tensor_tensor(gates[:].rearrange("p a b d -> p (a b d)"), absg[:], sgn[:],
                                    ALU.mult).then_inc(s_v, 1)
            dve.wait_ge(s_v, 11)

        @block.tensor
        def _(pe):
            pe.wait_ge(s_load, 80)
            pe.wait_ge(s_silu, 1)
            for j in range(12):
                for dc in range(DC):
                    last = nc.tensor.matmul(pm[:, j, :], wm[:, dc, j * P:(j + 1) * P], sc[:, dc, :],
                                            start=(dc == 0), stop=(dc == DC - 1))
            last.then_inc(s_col, 1)
            pe.wait_ge(s_bc, 1)
            for g, part in enumerate((GA, GB)):
                for b in range(B):
                    for dc in range(DC):
                        last = nc.tensor.matmul(pg[:, g * B + b, :], scb[:, dc, b, :],
                                                wm[:, dc, part * D:(part + 1) * D],
                                                start=(dc == 0), stop=(dc == DC - 1))
            last.then_inc(s_row, 1)


def norm_first(nc, sem, x, ident, modT, hT):
    s_x, s_st, s_ag, s_sq = sem("x_loaded"), sem("x_stats"), sem("x_moments"), sem("x_root")
    s_rs, s_n, s_t, s_e = sem("x_rstd"), sem("x_normed"), sem("x_turned"), sem("x_kept")
    with ExitStack() as st:
        xs = st.enter_context(nc.sbuf_tensor("xs", [P, B * NT, D], F32))
        stats = st.enter_context(nc.sbuf_tensor("stats", [P, B * NT, 6], F32))
        mv = st.enter_context(nc.sbuf_tensor("mv", [P, B * NT, 2], F32))
        eps = st.enter_context(nc.sbuf_tensor("eps", [P, 1], F32))
        sd = st.enter_context(nc.sbuf_tensor("sd", [P, B * NT], F32))
        rstd = st.enter_context(nc.sbuf_tensor("rstd", [P, B * NT], F32))
        pt = st.enter_context(nc.psum_tensor("pt", [P, 2, DC, G], F32))
        block = st.enter_context(nc.Block())

        @block.sync
        def _(sp):
            for b in range(B):
                sp.dma_start(xs[:, b * NT:(b + 1) * NT, :], x[:, b * NT:(b + 1) * NT, :]).then_inc(s_x, 16)

        @block.scalar
        def _(act):
            act.wait_ge(s_ag, B * NT + 1)
            nc.scalar.activation(sd[:], mv[:, :, 1], ACT.Sqrt, bias=eps[:, 0:1]).then_inc(s_sq, 1)

        @block.vector
        def _(dve):
            nc.vector.memset(eps[:], LN_EPS).then_inc(s_ag, 1)
            dve.wait_ge(s_x, 16 * B)
            with dve.Fori(0, B * NT) as i:
                nc.vector.bn_stats(stats[:, bass.ds(i, 1), :], xs[:, bass.ds(i, 1), :]).then_inc(s_st, 1)
            dve.wait_ge(s_st, B * NT)
            for i in range(B * NT):
                nc.vector.bn_aggr(mv[:, i, :], stats[:, i, :]).then_inc(s_ag, 1)
            dve.wait_ge(s_sq, 1)
            nc.vector.reciprocal(rstd[:], sd[:]).then_inc(s_rs, 1)
            dve.wait_ge(s_rs, 1)
            with dve.Fori(0, B * NT) as i:
                nc.vector.tensor_scalar(xs[:, bass.ds(i, 1), :], xs[:, bass.ds(i, 1), :], mv[:, bass.ds(i, 1), 0],
                                        rstd[:, bass.ds(i, 1)], ALU.subtract, ALU.mult).then_inc(s_n, 1)
            for g in range(B * GH):
                dve.wait_ge(s_t, g + 1)
                b = g // GH
                for dc in range(DC):
                    nc.vector.tensor_scalar(hT[:, dc, g * G:(g + 1) * G], pt[:, g % 2, dc, :],
                                            modT[:, 2 * CA + dc, b:b + 1], modT[:, 2 * SA + dc, b:b + 1],
                                            ALU.mult, ALU.add).then_inc(s_e, 1)
            dve.wait_ge(s_e, DC * B * GH)

        @block.tensor
        def _(pe):
            for g in range(B * GH):
                pe.wait_ge(s_n, (g + 1) * GT)
                if g >= 2:
                    pe.wait_ge(s_e, DC * (g - 1))
                for j in range(GT):
                    for dc in range(DC):
                        last = nc.tensor.transpose(pt[:, g % 2, dc, j * P:(j + 1) * P],
                                                   xs[:, g * GT + j, dc * P:(dc + 1) * P], ident[:])
                last.then_inc(s_t, 1)


def gate_scalars(nc, sem, wab, bab, hT, ab_s):
    s_w, s_p, s_a, s_o = sem("ab_weights"), sem("ab_product"), sem("ab_sigmoid"), sem("ab_stored")
    with ExitStack() as st:
        w = st.enter_context(nc.sbuf_tensor("wab_sb", [P, DC, 2 * H], F32))
        bias = st.enter_context(nc.sbuf_tensor("bab_sb", [2 * H, 1], F32))
        ab = st.enter_context(nc.sbuf_tensor("ab", [2 * H, B, T], F32))
        pa = st.enter_context(nc.psum_tensor("pa", [P, 2, G], F32))
        block = st.enter_context(nc.Block())

        @block.sync
        def _(sp):
            sp.dma_start(w[:], wab).then_inc(s_w, 16)
            sp.dma_start(bias[:], bab).then_inc(s_w, 16)
            sp.wait_ge(s_a, B * GH)
            sp.dma_start(ab_s, ab[:]).then_inc(s_o, 16)
            sp.wait_ge(s_o, 16)

        @block.scalar
        def _(act):
            act.wait_ge(s_w, 32)
            for g in range(B * GH):
                act.wait_ge(s_p, g + 1)
                nc.scalar.activation(ab[:].rearrange("h b t -> h (b t)")[:, g * G:(g + 1) * G],
                                     pa[0:2 * H, g % 2, :], ACT.Sigmoid, bias=bias[:, 0:1]).then_inc(s_a, 1)

        @block.tensor
        def _(pe):
            pe.wait_ge(s_w, 32)
            for g in range(B * GH):
                if g >= 2:
                    pe.wait_ge(s_a, g - 1)
                for dc in range(DC):
                    last = nc.tensor.matmul(pa[0:2 * H, g % 2, :], w[:, dc, :], hT[:, dc, g * G:(g + 1) * G],
                                            start=(dc == 0), stop=(dc == DC - 1))
                last.then_inc(s_p, 1)


def project(nc, sem, wqkv, convp, ones2, hT, qkv_s):
    s_w, s_p, s_raw, s_tap = sem("p_weights"), sem("p_product"), sem("p_raw"), sem("p_taps")
    s_silu, s_sq, s_nn, s_rt = sem("p_silu"), sem("p_square"), sem("p_norm2"), sem("p_norm")
    s_k, s_o, s_z = sem("p_kn"), sem("p_stored"), sem("p_zero")
    s_r, s_tick, s_st = sem("p_recip"), sem("p_tick"), sem("p_unit_stored")
    with ExitStack() as st:
        w = st.enter_context(nc.sbuf_tensor("wqkv_sb", [P, 2, 3, DC, P], F32))
        cw = st.enter_context(nc.sbuf_tensor("convp_sb", [P, 2, 3, 5], F32))
        raw = st.enter_context(nc.sbuf_tensor("raw", [P, 4 + T], F32))
        tap = st.enter_context(nc.sbuf_tensor("tap", [P, T], F32))
        res = st.enter_context(nc.sbuf_tensor("res", [P, 3, T], F32))
        sq = st.enter_context(nc.sbuf_tensor("sq", [P, T], F32))
        tick2 = st.enter_context(nc.sbuf_tensor("p_tick2", [P, 8], F32))
        tick = st.enter_context(nc.sbuf_tensor("p_tick", [P, 8], F32))
        pp = st.enter_context(nc.psum_tensor("pp", [P, 2, T], F32))
        pn = st.enter_context(nc.psum_tensor("pn", [P, T], F32))
        block = st.enter_context(nc.Block())
        NB = M * B

        @block.gpsimd
        def _(pool):

            with pool.Fori(0, M) as m:
                pool.wait_ge(s_tap, 1 + m * (B * 3))
                pool.wait_ge(s_tick, 1 + m * (2 * B + 1))
                nc.gpsimd.tensor_tensor(tick[:], ones2[:, 0:8], ones2[:, 0:8], ALU.add).then_inc(s_tick, 1)
                pool.dma_start(w[:, 0], wqkv[bass.ds(m, 1)].rearrange("a p n c k -> (a p) n c k")).then_inc(s_w, 16)
                pool.dma_start(cw[:, 0], convp[bass.ds(m, 1)].rearrange("a p n k -> (a p) n k")).then_inc(s_w, 16)
                for b in range(B):
                    pool.wait_ge(s_silu, 1 + m * (3 * B) + 3 * (b + 1))
                    pool.wait_ge(s_k, 1 + m * B + (b + 1))
                    pool.wait_ge(s_tick, 1 + m * (2 * B + 1) + (2 * b + 1))
                    nc.gpsimd.tensor_tensor(tick[:], ones2[:, 0:8], ones2[:, 0:8], ALU.add).then_inc(s_tick, 1)
                    for n in range(3):
                        pool.dma_start(qkv_s[n, b, bass.ds(m, 1)].rearrange("a p t -> (a p) t"),
                                     res[:, n, :]).then_inc(s_o, 16)
                    pool.wait_ge(s_o, m * (48 * B) + 48 * (b + 1))
                    pool.wait_ge(s_tick, 1 + m * (2 * B + 1) + (2 * b + 2))
                    nc.gpsimd.tensor_tensor(tick[:], ones2[:, 0:8], ones2[:, 0:8], ALU.add).then_inc(s_tick, 1)
                    pool.wait_ge(s_tick, 1 + m * (2 * B + 1) + (2 * b + 3))
                    nc.gpsimd.tensor_tensor(tick2[:], ones2[:, 0:8], ones2[:, 0:8], ALU.add).then_inc(s_st, 1)

        @block.scalar
        def _(act):
            with act.Fori(0, M) as m:
                act.wait_ge(s_w, m * 32 + 32)
                for b in range(B):
                    for n in range(3):
                        u = 3 * b + n
                        act.wait_ge(s_p, m * (3 * B) + (u + 1))
                        if u == 0:
                            act.wait_ge(s_z, m * 1 + 1)
                        else:
                            act.wait_ge(s_tap, 1 + m * (3 * B) + u)
                        act.wait_ge(s_silu, 1 + m * (3 * B) + u)
                        nc.scalar.activation(raw[:, 4:], pp[:, u % 2, :], ACT.Identity).then_inc(s_raw, 1)
                        nc.scalar.activation(tap[:], pp[:, u % 2, :], ACT.Identity, bias=cw[:, 0, n, 4:5],
                                             scale=cw[:, 0, n, 3:4]).then_inc(s_raw, 1)
                        act.wait_ge(s_tap, 1 + m * (3 * B) + (u + 1))
                        if n == 0:
                            act.wait_ge(s_st, 1 + m * B + b)
                        nc.scalar.activation(res[:, n, :], tap[:], ACT.Silu).then_inc(s_silu, 1)
                        if n == 1:
                            act.wait_ge(s_silu, 1 + m * (3 * B) + (u + 1))
                            act.wait_ge(s_k, 1 + m * B + b)
                            nc.scalar.activation(sq[:], res[:, 1, :], ACT.Square).then_inc(s_sq, 1)
                            act.wait_ge(s_nn, m * B + (b + 1))
                            nc.scalar.activation(sq[:], pn[:], ACT.Sqrt).then_inc(s_rt, 1)

        @block.vector
        def _(dve):
            nc.vector.memset(raw[:, 0:4], 0.0).then_inc(s_z, 1)
            with dve.Fori(0, M) as m:
                dve.wait_ge(s_w, m * 32 + 32)
                for b in range(B):
                    for n in range(3):
                        u = 3 * b + n
                        dve.wait_ge(s_raw, 1 + m * (6 * B) + (2 * u + 2))
                        for i, k in enumerate((2, 1, 0)):
                            ins = nc.vector.scalar_tensor_tensor(
                                out=tap[:], in0=raw[:, 1 + k:1 + k + T], scalar=cw[:, 0, n, k:k + 1],
                                in1=tap[:], op0=ALU.mult, op1=ALU.add)
                            if i < 2:
                                ins.then_inc(s_r, 1)
                                dve.wait_ge(s_r, m * (3 * B * 2 + 2 * B) + (6 + 2) * b + 2 * n + (2 if n == 2 else 0)
                                            + i + 1)
                            elif u == 3 * B - 1:
                                ins.then_inc(s_tap, 1)
                            else:
                                ins.then_inc(s_tap, 1)
                        if n == 1:
                            dve.wait_ge(s_rt, m * B + (b + 1))
                            nc.vector.tensor_scalar(sq[:], sq[:], NORM_EPS, None, ALU.max).then_inc(s_r, 1)
                            dve.wait_ge(s_r, m * (8 * B) + (8 * b + 5))
                            nc.vector.reciprocal(sq[:], sq[:]).then_inc(s_r, 1)
                            dve.wait_ge(s_r, m * (8 * B) + (8 * b + 6))
                            nc.vector.tensor_tensor(res[:, 1, :], res[:, 1, :], sq[:], ALU.mult).then_inc(s_k, 1)
                dve.wait_ge(s_tap, 1 + m * (3 * B) + 3 * B)
                dve.wait_ge(s_k, 1 + m * B + B)
                nc.vector.memset(raw[:, 0:4], 0.0).then_inc(s_z, 1)

        @block.tensor
        def _(pe):
            pe.sem_inc(s_tap, 1)
            pe.sem_inc(s_silu, 1)
            pe.sem_inc(s_st, 1)
            pe.sem_inc(s_k, 1)
            pe.sem_inc(s_raw, 1)
            pe.sem_inc(s_tick, 1)
            with pe.Fori(0, M) as m:
                pe.wait_ge(s_w, m * 32 + 32)
                for b in range(B):
                    for n in range(3):
                        u = 3 * b + n
                        if u < 2:
                            pe.wait_ge(s_raw, 1 + m * (6 * B))
                        else:
                            pe.wait_ge(s_raw, 1 + m * (6 * B) + 2 * (u - 1))
                        for g in range(GH):
                            for dc in range(DC):
                                last = nc.tensor.matmul(pp[:, u % 2, g * G:(g + 1) * G], w[:, 0, n, dc, :],
                                                        hT[:, dc, b * T + g * G:b * T + (g + 1) * G],
                                                        start=(dc == 0), stop=(dc == DC - 1))
                        last.then_inc(s_p, 1)
                    pe.wait_ge(s_sq, m * B + (b + 1))
                    if b:
                        pe.wait_ge(s_rt, m * B + b)
                    for g in range(GH):
                        last = nc.tensor.matmul(pn[:, g * G:(g + 1) * G], ones2[:], sq[:, g * G:(g + 1) * G],
                                                start=True, stop=True)
                    last.then_inc(s_nn, 1)


def scan(nc, sem, ones2, qkv_s, ab_s, y_s):
    TB, HI = 64, DH // 2
    NBK = T // TB
    s_tick, s_st = sem("s_tick"), sem("s_block_stored")
    s_ab, s_in, s_d, s_y, s_o = sem("s_ab"), sem("s_in"), sem("s_step"), sem("s_y"), sem("s_out")
    with ExitStack() as st:
        al = st.enter_context(nc.sbuf_tensor("alpha", [P, T], F32))
        be = st.enter_context(nc.sbuf_tensor("beta", [P, T], F32))
        S = st.enter_context(nc.sbuf_tensor("state", [P, HI, DH], F32))
        W = st.enter_context(nc.sbuf_tensor("outer", [P, HI, DH], F32))
        r = st.enter_context(nc.sbuf_tensor("seen", [P, HI], F32))
        u = st.enter_context(nc.sbuf_tensor("update", [P, HI], F32))
        qb = st.enter_context(nc.sbuf_tensor("q_blk", [P, DH, TB], F32))
        kb = st.enter_context(nc.sbuf_tensor("k_blk", [P, DH, TB], F32))
        vb = st.enter_context(nc.sbuf_tensor("v_blk", [P, HI, TB], F32))
        yb = st.enter_context(nc.sbuf_tensor("y_blk", [P, HI, TB], F32))
        tick2 = st.enter_context(nc.sbuf_tensor("s_tick2", [P, 8], F32))
        tick = st.enter_context(nc.sbuf_tensor("s_tick", [P, 8], F32))
        block = st.enter_context(nc.Block())
        NS = 9

        @block.gpsimd
        def _(pool):
            for half in range(2):
                rows = slice(half * 64, half * 64 + 64)
                for b in range(B):
                    pr = slice(half * 64 + b * H, half * 64 + (b + 1) * H)
                    pool.dma_start(al[pr, :], ab_s[0:H, b, :]).then_inc(s_ab, 16)
                    pool.dma_start(be[pr, :], ab_s[H:2 * H, b, :]).then_inc(s_ab, 16)

            with pool.Fori(0, NBK) as n:
                pool.wait_ge(s_y, 1 + n)
                pool.wait_ge(s_tick, 1 + n * 3)
                nc.gpsimd.tensor_tensor(tick[:], ones2[:, 0:8], ones2[:, 0:8], ALU.add).then_inc(s_tick, 1)
                for half in range(2):
                    for b in range(B):
                        pr = slice(half * 64 + b * H, half * 64 + (b + 1) * H)
                        for dst, i in ((qb, 0), (kb, 1)):
                            pool.dma_start(dst[pr], qkv_s[i, b].rearrange("m (a j) t -> (m a) j t", a=2)
                                         [:, :, bass.ds(n * TB, TB)]).then_inc(s_in, 16)
                        pool.dma_start(vb[pr], qkv_s[2, b].rearrange("m (a j) t -> (m a) j t", a=2)
                                     [:, half * HI:(half + 1) * HI, bass.ds(n * TB, TB)]).then_inc(s_in, 16)
                pool.wait_ge(s_y, 1 + n + 1)
                pool.wait_ge(s_tick, 1 + n * 3 + 1)
                nc.gpsimd.tensor_tensor(tick[:], ones2[:, 0:8], ones2[:, 0:8], ALU.add).then_inc(s_tick, 1)
                for half in range(2):
                    for b in range(B):
                        pr = slice(half * 64 + b * H, half * 64 + (b + 1) * H)
                        pool.dma_start(y_s[b].rearrange("m (a j) t -> (m a) j t", a=2)
                                     [:, half * HI:(half + 1) * HI, bass.ds(n * TB, TB)], yb[pr]).then_inc(s_o, 16)
                pool.wait_ge(s_o, n * 128 + 128)
                pool.wait_ge(s_tick, 1 + n * 3 + 2)
                nc.gpsimd.tensor_tensor(tick[:], ones2[:, 0:8], ones2[:, 0:8], ALU.add).then_inc(s_tick, 1)
                pool.wait_ge(s_tick, 1 + n * 3 + 3)
                nc.gpsimd.tensor_tensor(tick2[:], ones2[:, 0:8], ones2[:, 0:8], ALU.add).then_inc(s_st, 1)

        @block.vector
        def _(dve):
            dve.sem_inc(s_y, 1)
            dve.sem_inc(s_st, 1)
            dve.sem_inc(s_tick, 1)
            nc.vector.memset(S[:], 0.0).then_inc(s_d, 1)
            dve.wait_ge(s_ab, 16 * 16)
            with dve.Fori(0, NBK) as n:
                dve.wait_ge(s_in, n * (24 * 16) + 24 * 16)
                dve.wait_ge(s_st, 1 + n)
                nc.vector.memset(r[:], 0.0)
                with dve.Fori(0, TB) as t:
                    tok = n * TB + t
                    base = (n * TB + t) * NS + 1
                    k_row = kb[:, :, bass.ds(t, 1)].rearrange("p j a -> p a j").broadcast_to([P, HI, DH])
                    q_row = qb[:, :, bass.ds(t, 1)].rearrange("p j a -> p a j").broadcast_to([P, HI, DH])
                    u_col = u[:, :].rearrange("p (i a) -> p i a", a=1).broadcast_to([P, HI, DH])
                    dve.wait_ge(s_d, base)
                    nc.vector.tensor_tensor(W[:], S[:], k_row, ALU.mult).then_inc(s_d, 1)
                    dve.wait_ge(s_d, base + 1)
                    nc.vector.tensor_reduce(r[:], W[:], AX_X, ALU.add).then_inc(s_d, 1)
                    dve.wait_ge(s_d, base + 2)
                    nc.vector.scalar_tensor_tensor(out=u[:], in0=r[:], scalar=al[:, bass.ds(tok, 1)],
                                                   in1=vb[:, :, bass.ds(t, 1)].rearrange("p i a -> p (i a)"),
                                                   op0=ALU.mult, op1=ALU.subtract).then_inc(s_d, 1)
                    dve.wait_ge(s_d, base + 3)
                    nc.vector.tensor_scalar(u[:], u[:], be[:, bass.ds(tok, 1)], -1.0, ALU.mult,
                                            ALU.mult).then_inc(s_d, 1)
                    dve.wait_ge(s_d, base + 4)
                    nc.vector.tensor_tensor(W[:], u_col, k_row, ALU.mult).then_inc(s_d, 1)
                    dve.wait_ge(s_d, base + 5)
                    nc.vector.scalar_tensor_tensor(out=S[:].rearrange("p i j -> p (i j)"),
                                                   in0=S[:].rearrange("p i j -> p (i j)"),
                                                   scalar=al[:, bass.ds(tok, 1)],
                                                   in1=W[:].rearrange("p i j -> p (i j)"), op0=ALU.mult,
                                                   op1=ALU.add).then_inc(s_d, 1)
                    dve.wait_ge(s_d, base + 6)
                    nc.vector.tensor_scalar(S[:], S[:], CLIP, -CLIP, ALU.min, ALU.max).then_inc(s_d, 1)
                    dve.wait_ge(s_d, base + 7)
                    nc.vector.tensor_tensor(W[:], S[:], q_row, ALU.mult).then_inc(s_d, 1)
                    dve.wait_ge(s_d, base + 8)
                    nc.vector.tensor_reduce(yb[:, :, bass.ds(t, 1)].rearrange("p i a -> p (i a)"), W[:], AX_X,
                                            ALU.add).then_inc(s_d, 1)
                dve.wait_ge(s_d, n * (TB * NS) + (TB * NS + 1))
                nc.vector.tensor_copy(r[:], u[:]).then_inc(s_y, 1)


def attn_out(nc, sem, x, y_s, wg, bg, wo, hT, gates, x1):
    s_y = [sem("o_y_even"), sem("o_y_odd")]
    s_w, s_gp, s_g = sem("o_weights"), sem("o_gate_product"), sem("o_gate")
    s_m, s_op, s_t, s_x1 = sem("o_gated"), sem("o_product"), sem("o_scaled"), sem("o_x1")
    with ExitStack() as st:
        wg_sb = st.enter_context(nc.sbuf_tensor("wg_sb", [P, DC, C], F32))
        bg_sb = st.enter_context(nc.sbuf_tensor("bg_sb", [P, M], F32))
        wo_sb = st.enter_context(nc.sbuf_tensor("wo_sb", [P, M, D], F32))
        y = st.enter_context(nc.sbuf_tensor("y", [P, 2, M, G], F32))
        g_sb = st.enter_context(nc.sbuf_tensor("g_sb", [P, 2, G], F32))
        tmp = st.enter_context(nc.sbuf_tensor("o_tmp", [P, 2, D], F32))
        pg = st.enter_context(nc.psum_tensor("o_pg", [P, 2, G], F32))
        po = st.enter_context(nc.psum_tensor("o_po", [P, 2, G], F32))
        block = st.enter_context(nc.Block())
        NG = B * GH

        @block.sync
        def _(sp):
            sp.dma_start(wg_sb[:], wg).then_inc(s_w, 16)
            sp.dma_start(bg_sb[:], bg).then_inc(s_w, 16)
            sp.dma_start(wo_sb[:], wo).then_inc(s_w, 16)
            sp.dma_start(x1[:], x).then_inc(s_w, 16)
            for g in range(NG):
                if g >= 2:
                    sp.wait_ge(s_op, GT * (g - 1))
                sp.dma_start(y[:, g % 2], y_s[g // GH].rearrange("m p t -> p m t")
                             [:, :, (g % GH) * G:(g % GH + 1) * G]).then_inc(s_y[g % 2], 16)

        @block.scalar
        def _(act):
            act.wait_ge(s_w, 64)
            for i in range(NG * M):
                act.wait_ge(s_gp, i + 1)
                if i >= 2:
                    act.wait_ge(s_m, i - 1)
                nc.scalar.activation(g_sb[:, i % 2, :], pg[:, i % 2, :], ACT.Silu,
                                     bias=bg_sb[:, i % M:i % M + 1]).then_inc(s_g, 1)

        @block.vector
        def _(dve):
            dve.wait_ge(s_w, 64)
            for g in range(NG):
                dve.wait_ge(s_y[g % 2], 16 * (g // 2 + 1))
                for m in range(M):
                    i = g * M + m
                    dve.wait_ge(s_g, i + 1)
                    nc.vector.tensor_tensor(y[:, g % 2, m, :], y[:, g % 2, m, :], g_sb[:, i % 2, :],
                                            ALU.mult).then_inc(s_m, 1)
                for j in range(GT):
                    i = g * GT + j
                    dve.wait_ge(s_op, i + 1)
                    if i >= 2:
                        dve.wait_ge(s_x1, i - 1)
                    nc.vector.tensor_tensor(tmp[:, i % 2, :], po[:, i % 2, 0:D], gates[:, 0, g // GH, :],
                                            ALU.mult).then_inc(s_t, 1)
                    dve.wait_ge(s_t, i + 1)
                    nc.vector.tensor_tensor(x1[:, i, :], x1[:, i, :], tmp[:, i % 2, :], ALU.add).then_inc(s_x1, 1)
            dve.wait_ge(s_x1, NG * GT)

        @block.tensor
        def _(pe):
            pe.wait_ge(s_w, 64)
            for g in range(NG):
                for m in range(M):
                    i = g * M + m
                    if i >= 2:
                        pe.wait_ge(s_g, i - 1)
                    for dc in range(DC):
                        last = nc.tensor.matmul(pg[:, i % 2, :], wg_sb[:, dc, m * P:(m + 1) * P],
                                                hT[:, dc, g * G:(g + 1) * G], start=(dc == 0), stop=(dc == DC - 1))
                    last.then_inc(s_gp, 1)
                pe.wait_ge(s_m, M * (g + 1))
                for j in range(GT):
                    i = g * GT + j
                    if i >= 2:
                        pe.wait_ge(s_t, i - 1)
                    for m in range(M):
                        last = nc.tensor.matmul(po[:, i % 2, 0:D], y[:, g % 2, m, j * P:(j + 1) * P], wo_sb[:, m, :],
                                                start=(m == 0), stop=(m == M - 1))
                    last.then_inc(s_op, 1)


def norm_second(nc, sem, ident, modT, rw_sb, b2, x1, h2T, comb, acc):
    N = B * NT
    s_b, s_st, s_ag, s_sq = sem("n_loaded"), sem("n_stats"), sem("n_moments"), sem("n_root")
    s_n, s_t, s_e, s_l = sem("n_normed"), sem("n_turned"), sem("n_kept"), sem("n_logits")
    s_v, s_x, s_c, s_cc = sem("n_vector"), sem("n_exp"), sem("n_comb_turned"), sem("n_comb_kept")
    s_b2, s_a = sem("n_bias"), sem("n_acc")
    with ExitStack() as st:
        stats = st.enter_context(nc.sbuf_tensor("stats2", [P, N, 6], F32))
        mv = st.enter_context(nc.sbuf_tensor("mv2", [P, N, 2], F32))
        eps = st.enter_context(nc.sbuf_tensor("eps2", [P, 1], F32))
        sd = st.enter_context(nc.sbuf_tensor("sd2", [P, N], F32))
        rstd = st.enter_context(nc.sbuf_tensor("rstd2", [P, N], F32))
        b2_sb = st.enter_context(nc.sbuf_tensor("b2_sb", [E, D], F32))
        lg = st.enter_context(nc.sbuf_tensor("logits", [P, N, E], F32))
        rank = st.enter_context(nc.sbuf_tensor("rank", [P, N, E], F32))
        hit = st.enter_context(nc.sbuf_tensor("hit", [P, N, E], F32))
        one1 = st.enter_context(nc.sbuf_tensor("first", [P, N, E], F32))
        one2 = st.enter_context(nc.sbuf_tensor("second", [P, N, E], F32))
        best = st.enter_context(nc.sbuf_tensor("best", [P, 2, N], F32))
        pos = st.enter_context(nc.sbuf_tensor("pos", [P, N], F32))
        ex = st.enter_context(nc.sbuf_tensor("ex", [P, 4, N], F32))
        combT = st.enter_context(nc.sbuf_tensor("combT", [E, N * P], F32))
        pt = st.enter_context(nc.psum_tensor("pt2", [P, 2, DC, G], F32))
        pl = st.enter_context(nc.psum_tensor("pl2", [P, N, E], F32))
        block = st.enter_context(nc.Block())
        NG = B * GH

        def wide(ap):
            return ap.rearrange("p (n a) -> p n a", a=1).broadcast_to([P, N, E])

        @block.sync
        def _(sp):
            sp.dma_start(b2_sb[:], b2).then_inc(s_b, 16)

        @block.scalar
        def _(act):
            act.wait_ge(s_ag, N + 1)
            nc.scalar.activation(sd[:], mv[:, :, 1], ACT.Sqrt, bias=eps[:, 0:1]).then_inc(s_sq, 1)
            act.wait_ge(s_v, E + 11)
            nc.scalar.activation(ex[:, 1, :], ex[:, 0, :], ACT.Exp).then_inc(s_x, 1)

        @block.vector
        def _(dve):
            nc.vector.memset(eps[:], LN_EPS).then_inc(s_ag, 1)
            for i in range(N):
                nc.vector.bn_stats(stats[:, i, :], x1[:, i, :]).then_inc(s_st, 1)
            dve.wait_ge(s_st, N)
            for i in range(N):
                nc.vector.bn_aggr(mv[:, i, :], stats[:, i, :]).then_inc(s_ag, 1)
            dve.wait_ge(s_sq, 1)
            v = 0

            def step(ins):
                nonlocal v
                v += 1
                ins.then_inc(s_v, 1)
                dve.wait_ge(s_v, v)

            step(nc.vector.reciprocal(rstd[:], sd[:]))
            for i in range(N):
                nc.vector.tensor_scalar(acc[:, i, :], x1[:, i, :], mv[:, i, 0:1],
                                        rstd[:, i:i + 1], ALU.subtract, ALU.mult).then_inc(s_n, 1)
            for g in range(NG):
                dve.wait_ge(s_t, g + 1)
                b = g // GH
                for dc in range(DC):
                    nc.vector.tensor_scalar(h2T[:, dc, g * G:(g + 1) * G], pt[:, g % 2, dc, :],
                                            modT[:, 2 * CB + dc, b:b + 1], modT[:, 2 * SB + dc, b:b + 1],
                                            ALU.mult, ALU.add).then_inc(s_e, 1)
            for e in range(E):
                step(nc.vector.memset(rank[:, :, e], float(E - e)))
            dve.wait_ge(s_l, 1)
            step(nc.vector.tensor_copy(lg[:], pl[:]))
            for n, (one, m) in enumerate(((one1, best[:, 0, :]), (one2, best[:, 1, :]))):
                step(nc.vector.tensor_reduce(m, lg[:], AX_X, ALU.max))
                if n == 1:
                    step(nc.vector.tensor_tensor(ex[:, 0, :], best[:, 1, :], best[:, 0, :], ALU.subtract))
                step(nc.vector.tensor_tensor(hit[:], lg[:], wide(m), ALU.is_equal))
                step(nc.vector.tensor_tensor(hit[:], hit[:], rank[:], ALU.mult))
                step(nc.vector.tensor_reduce(pos[:], hit[:], AX_X, ALU.max))
                step(nc.vector.tensor_tensor(one[:], hit[:], wide(pos[:]), ALU.is_equal))
                if n == 0:
                    step(nc.vector.tensor_scalar(hit[:], one[:], -3.0e38, None, ALU.mult))
                    step(nc.vector.tensor_tensor(lg[:], lg[:], hit[:], ALU.add))
            dve.wait_ge(s_x, 1)
            step(nc.vector.tensor_scalar(ex[:, 2, :], ex[:, 1, :], 1.0, None, ALU.add))
            step(nc.vector.reciprocal(ex[:, 3, :], ex[:, 2, :]))
            step(nc.vector.tensor_tensor(ex[:, 2, :], ex[:, 1, :], ex[:, 3, :], ALU.mult))
            step(nc.vector.tensor_tensor(one1[:], one1[:], wide(ex[:, 3, :]), ALU.mult))
            step(nc.vector.tensor_tensor(one2[:], one2[:], wide(ex[:, 2, :]), ALU.mult))
            nc.vector.tensor_tensor(comb[:], one1[:], one2[:], ALU.add).then_inc(s_a, 1)
            dve.wait_ge(s_a, 1)
            for g in range(NG):
                dve.wait_ge(s_c, g + 1)
                nc.vector.tensor_copy(combT[:, g * G:(g + 1) * G], pt[0:E, g % 2, 0, :]).then_inc(s_cc, 1)
            for g in range(N // 2):
                dve.wait_ge(s_b2, g + 1)
                nc.vector.tensor_copy(acc[:, 2 * g:2 * g + 2, :],
                                      pt[:, g % 2, 1, :].rearrange("p (j d) -> p j d", j=2)).then_inc(s_a, 1)
            dve.wait_ge(s_a, 1 + N // 2)

        @block.tensor
        def _(pe):
            for g in range(NG):
                pe.wait_ge(s_n, (g + 1) * GT)
                if g >= 2:
                    pe.wait_ge(s_e, DC * (g - 1))
                for j in range(GT):
                    for dc in range(DC):
                        last = nc.tensor.transpose(pt[:, g % 2, dc, j * P:(j + 1) * P],
                                                   acc[:, g * GT + j, dc * P:(dc + 1) * P], ident[:])
                last.then_inc(s_t, 1)
            for g in range(NG):
                pe.wait_ge(s_e, DC * (g + 1))
                for j in range(g * GT, (g + 1) * GT):
                    for dc in range(DC):
                        last = nc.tensor.matmul(pl[:, j, :], h2T[:, dc, j * P:(j + 1) * P], rw_sb[:, dc, :],
                                                start=(dc == 0), stop=(dc == DC - 1))
            last.then_inc(s_l, 1)
            pe.wait_ge(s_a, 1)
            for g in range(NG):
                if g >= 2:
                    pe.wait_ge(s_cc, g - 1)
                for j in range(GT):
                    last = nc.tensor.transpose(pt[0:E, g % 2, 0, j * P:(j + 1) * P], comb[:, g * GT + j, :], ident[:])
                last.then_inc(s_c, 1)
            pe.wait_ge(s_b, 16)
            for g in range(N // 2):
                pe.wait_ge(s_cc, g // 2 + 1)
                if g >= 2:
                    pe.wait_ge(s_a, g)
                for j in range(2):
                    last = nc.tensor.matmul(pt[:, g % 2, 1, j * D:(j + 1) * D],
                                            combT[:, (2 * g + j) * P:(2 * g + j + 1) * P], b2_sb[:],
                                            start=True, stop=True)
                last.then_inc(s_b2, 1)


def experts(nc, sem, w1, b1, w2, h2T, comb, acc):
    s_w = [sem("e_weights_even"), sem("e_weights_odd")]
    s_h, s_g, s_y, s_a = sem("e_up"), sem("e_gelu"), sem("e_down"), sem("e_acc")
    with ExitStack() as st:
        w1_sb = st.enter_context(nc.sbuf_tensor("w1_sb", [P, 2, DC, F], F32))
        w2_sb = st.enter_context(nc.sbuf_tensor("w2_sb", [P, 2, FC, D], F32))
        b1_sb = st.enter_context(nc.sbuf_tensor("b1_sb", [P, 2, FC], F32))
        hm = st.enter_context(nc.sbuf_tensor("hm", [P, 2, FC, G], F32))
        ph = st.enter_context(nc.psum_tensor("ph", [P, 4, G], F32))
        py = st.enter_context(nc.psum_tensor("py", [P, 4, G], F32))
        block = st.enter_context(nc.Block())
        NG = B * GH

        @block.sync
        def _(sp):
            for e in range(E):
                if e >= 2:
                    sp.wait_ge(s_y, 1 + (e - 1) * NG * GT)
                sp.dma_start(w1_sb[:, e % 2], w1[e]).then_inc(s_w[e % 2], 16)
                sp.dma_start(w2_sb[:, e % 2], w2[e]).then_inc(s_w[e % 2], 16)
                sp.dma_start(b1_sb[:, e % 2], b1[e]).then_inc(s_w[e % 2], 16)

        @block.scalar
        def _(act):
            with act.Fori(0, E // 2) as e2:
                for p in range(2):
                    act.wait_ge(s_w[p], e2 * 48 + 48)
                    for g in range(NG):
                        i = p * NG + g
                        if i >= 2:
                            act.wait_ge(s_y, 1 + e2 * (2 * NG * GT) + (i - 1) * GT)
                        else:
                            act.wait_ge(s_y, 1 + e2 * (2 * NG * GT) + 0)
                        for f in range(FC):
                            act.wait_ge(s_h, e2 * (2 * NG * FC) + (i * FC + f + 1))
                            nc.scalar.activation(hm[:, i % 2, f, :], ph[:, f % 4, :], ACT.Gelu,
                                                 bias=b1_sb[:, p, f:f + 1]).then_inc(s_g, 1)

        @block.vector
        def _(dve):
            with dve.Fori(0, E // 2) as e2:
                for p in range(2):
                    for g in range(NG):
                        i = p * NG + g
                        for j in range(GT):
                            dve.wait_ge(s_y, 1 + e2 * (2 * NG * GT) + (i * GT + j + 1))
                            if g == 0 and j == 0:
                                dve.wait_ge(s_a, 1 + e2 * (2 * NG * GT) + i * GT)
                            nc.vector.scalar_tensor_tensor(
                                out=acc[:, g * GT + j, :], in0=py[:, j, 0:D],
                                scalar=comb[:, g * GT + j, bass.ds(e2 * 2 + p, 1)], in1=acc[:, g * GT + j, :],
                                op0=ALU.mult, op1=ALU.add).then_inc(s_a, 1)
            dve.wait_ge(s_a, 1 + E * NG * GT)

        @block.tensor
        def _(pe):
            pe.sem_inc(s_y, 1)
            pe.sem_inc(s_a, 1)
            pe.sem_inc(s_g, 1)
            def up(e2, i, p, g):
                if g == 0:
                    pe.wait_ge(s_w[p], e2 * 48 + 48)
                for f in range(FC):
                    pe.wait_ge(s_g, 1 + e2 * (2 * NG * FC) + max((i - 1) * FC + f + 1, 0))
                    for dc in range(DC):
                        last = nc.tensor.matmul(ph[:, f, :], w1_sb[:, p, dc, f * P:(f + 1) * P],
                                                h2T[:, dc, g * G:(g + 1) * G], start=(dc == 0), stop=(dc == DC - 1))
                    last.then_inc(s_h, 1)

            def down(e2, i, p, g):
                pe.wait_ge(s_g, 1 + e2 * (2 * NG * FC) + (i + 1) * FC)
                for j in range(GT):
                    pe.wait_ge(s_a, 1 + e2 * (2 * NG * GT) + max((i - 1) * GT + j + 1, 0))
                    for f in range(FC):
                        last = nc.tensor.matmul(py[:, j, 0:D], hm[:, i % 2, f, j * P:(j + 1) * P], w2_sb[:, p, f, :],
                                                start=(f == 0), stop=(f == FC - 1))
                    last.then_inc(s_y, 1)

            with pe.Fori(0, E // 2) as e2:
                for i in range(2 * NG + 1):
                    if i < 2 * NG:
                        up(e2, i, i // NG, i % NG)
                    if i >= 1:
                        down(e2, i - 1, (i - 1) // NG, (i - 1) % NG)


def finish(nc, sem, gates, x1, acc, out):
    s_m, s_a, s_o = sem("f_scaled"), sem("f_sum"), sem("f_stored")
    with ExitStack() as st:
        block = st.enter_context(nc.Block())

        @block.sync
        def _(sp):
            for b in range(B):
                sp.wait_ge(s_a, (b + 1) * NT)
                sp.dma_start(out[:, b * NT:(b + 1) * NT, :], acc[:, b * NT:(b + 1) * NT, :]).then_inc(s_o, 16)
            sp.wait_ge(s_o, 16 * B)

        @block.vector
        def _(dve):
            for i in range(B * NT):
                nc.vector.tensor_tensor(acc[:, i, :], acc[:, i, :], gates[:, 1, i // NT, :], ALU.mult).then_inc(s_m, 1)
            for i in range(B * NT):
                dve.wait_ge(s_m, i + 1)
                nc.vector.tensor_tensor(acc[:, i, :], acc[:, i, :], x1[:, i, :], ALU.add).then_inc(s_a, 1)


def kernel(**inputs):
    import numpy as np
    import concourse.bacc as bacc
    from concourse.bass_utils import run_bass_kernel_spmd

    a = {k[3:]: np.asarray(v) for k, v in inputs.items()}

    def cols(w):
        return w.T.reshape(w.shape[1] // P, P, w.shape[0]).transpose(1, 0, 2)

    wqkv = np.stack([cols(a["attn_W" + n]).reshape(P, DC, M, P) for n in "qkv"])
    convp = np.stack([np.concatenate([a[f"attn_conv_{n}_w"].reshape(C, 4), a[f"attn_conv_{n}_b"].reshape(C, 1)], 1)
                      .reshape(M, P, 5) for n in "qkv"])
    ident = np.eye(P, dtype=np.float32)
    ones2 = np.kron(np.eye(2, dtype=np.float32), np.ones((DH, DH), np.float32))
    tiles = lambda z: z.reshape(B * NT, P, D).transpose(1, 0, 2)
    arrays = {
        "x": tiles(a["attn_hidden_states"]),
        "cT": a["c"].T.reshape(DC, P, B).transpose(1, 0, 2),
        "wmod": a["wmod"].reshape(DC, P, 6 * D).transpose(1, 0, 2),
        "wqkv": wqkv.transpose(3, 1, 0, 2, 4),
        "convp": convp.transpose(1, 2, 0, 3),
        "wg": cols(a["attn_Wg"]),
        "bg": a["attn_bg"].reshape(M, P).T,
        "wab": cols(np.concatenate([a["attn_Wa"], a["attn_Wb"]], 0)),
        "bab": np.concatenate([a["attn_ba"], a["attn_bb"]]).reshape(2 * H, 1),
        "wo": cols(a["attn_Wo"]),
        "rw": cols(a["ffn_router_w"]),
        "w1": np.stack([cols(w) for w in a["ffn_w1"]]),
        "b1": a["ffn_b1"].reshape(E, FC, P).transpose(0, 2, 1),
        "w2": np.stack([cols(w) for w in a["ffn_w2"]]),
        "b2": a["ffn_b2"],
        "ident": ident,
        "ones2": ones2,
    }
    nc = bacc.Bacc("TRN2", target_bir_lowering=False, num_devices=1)
    feeds, args = {}, []
    for name, v in arrays.items():
        v = np.ascontiguousarray(v)
        feeds[name + "_in"] = v
        args.append(nc.dram_tensor(name + "_in", v.shape, F32, kind="ExternalInput").ap())
    args.append(nc.dram_tensor("out_0", (P, B * NT, D), F32, kind="ExternalOutput").ap())
    args.append(nc.dram_tensor("qkv_scratch", (3, B, M, P, T), F32, kind="Internal").ap())
    args.append(nc.dram_tensor("ab_scratch", (2 * H, B, T), F32, kind="Internal").ap())
    args.append(nc.dram_tensor("y_scratch", (B, M, P, T), F32, kind="Internal").ap())
    adaln_delta_moe(nc, *args)
    r = run_bass_kernel_spmd(nc, [feeds], core_ids=[0])
    got = np.asarray(r.results[0]["out_0"]).reshape(P, B * NT, D)
    return got.transpose(1, 0, 2).reshape(B, T, D)
```

```python
from contextlib import ExitStack

import concourse.bass as bass
from concourse import mybir

ALU = mybir.AluOpType
ACT = mybir.ActivationFunctionType
F32 = mybir.dt.float32
AX_X = mybir.AxisListType.X

P = 128
B, T, D = 4, 1024, 256
H, DH = 16, 64
C = H * DH
E, F = 8, 512
DC = D // P
M = C // P
FC = F // P
NT = T // P
G = 512
GH = T // G
GT = G // P
CLIP = 5.0
LN_EPS = 1e-5
NORM_EPS = 1e-12
SA, CA, GA, SB, CB, GB = range(6)


def adaln_delta_moe(nc, x, cT, wmod, wqkv, convp, wg, bg, wab, bab, wo, rw, w1, b1, w2, b2,
                    ident_d, ones2_d, tri_d, mask_d, bab_row, out, qkv_s, ab_s, y_s, gates_s):
    with ExitStack() as top:
        def sb_in(stack):
            return lambda name, shape: stack.enter_context(nc.sbuf_tensor(name, shape, F32))

        def ps_in(stack):
            return lambda name, shape: stack.enter_context(nc.psum_tensor(name, shape, F32))

        def sem(name):
            return top.enter_context(nc.semaphore(name))

        sb = sb_in(top)
        ident = sb("ident", [P, P])
        ones2 = sb("ones2", [P, P])
        modT = sb("modT", [P, 12, B])
        rw_sb = sb("rw_sb", [P, DC, E])

        modulation(nc, sem, cT, wmod, rw, ident_d, ones2_d, ident, ones2, modT, gates_s, rw_sb)

        hT = sb("hT", [P, DC, B * T])
        norm_first(nc, sem, x, ident, modT, hT)
        gate_scalars(nc, sem, wab, bab, hT, ab_s)
        fmax = sb("fmax", [P, 1])
        flag = top.enter_context(nc.sbuf_tensor("flag", [P, 1], mybir.dt.int32))
        with ExitStack() as st:
            la, bt = sb_in(st)("log_alpha", [P, B * NT, H]), sb_in(st)("beta_tok", [P, B * NT, H])
            gate_logs(nc, sem, wab, bab_row, hT, la, bt)
            delta_fast(nc, sem, ident, wqkv, convp, tri_d, mask_d, hT, la, bt, ab_s, y_s, fmax)
        judge(nc, sem, fmax, flag)
        clipped = nc.values_load(flag[0:1, 0:1], min_val=0, max_val=1)
        with nc.If(clipped > 0):
            project(nc, sem, wqkv, convp, ones2, hT, qkv_s)
            scan(nc, sem, ones2, qkv_s, ab_s, y_s)
        x1 = sb("x1", [P, B * NT, D])
        gates = sb("gates", [P, 2, B, D])
        attn_out(nc, sem, x, y_s, wg, bg, wo, gates_s, hT, gates, x1)
        h2T = hT
        comb = sb("comb", [P, B * NT, E])
        acc = sb("acc", [P, B * NT, D])
        norm_second(nc, sem, ident, modT, rw_sb, b2, x1, h2T, comb, acc)
        experts(nc, sem, w1, b1, w2, h2T, comb, acc)
        finish(nc, sem, gates, x1, acc, out)


def modulation(nc, sem, cT, wmod, rw, ident_d, ones2_d, ident, ones2, modT, gates_s, rw_sb):
    s_load, s_silu, s_bc = sem("mod_loaded"), sem("mod_silu"), sem("mod_spread")
    s_col, s_row, s_v, s_o = sem("mod_columns"), sem("mod_rows"), sem("mod_vector"), sem("mod_stored")
    with ExitStack() as st:
        gates = st.enter_context(nc.sbuf_tensor("gates_made", [P, 2 * B * D], F32))
        c_sb = st.enter_context(nc.sbuf_tensor("c_sb", [P, DC, B], F32))
        sc = st.enter_context(nc.sbuf_tensor("silu_c", [P, DC, B], F32))
        scb = st.enter_context(nc.sbuf_tensor("silu_c_spread", [P, DC, B, P], F32))
        wm = st.enter_context(nc.sbuf_tensor("wmod_sb", [P, DC, 6 * D], F32))
        absg = st.enter_context(nc.sbuf_tensor("gate_size", [P, 2 * B * D], F32))
        sgn = st.enter_context(nc.sbuf_tensor("gate_sign", [P, 2 * B * D], F32))
        raw = st.enter_context(nc.sbuf_tensor("gate_raw", [P, 2 * B * D], F32))
        ones = st.enter_context(nc.sbuf_tensor("ones_row", [P, P], F32))
        pm = st.enter_context(nc.psum_tensor("pm", [P, 12, B], F32))
        pg = st.enter_context(nc.psum_tensor("pg", [P, 2 * B, D], F32))
        block = st.enter_context(nc.Block())

        @block.sync
        def _(sp):
            sp.dma_start(c_sb[:], cT).then_inc(s_load, 16)
            sp.dma_start(wm[:], wmod).then_inc(s_load, 16)
            sp.dma_start(ident[:], ident_d).then_inc(s_load, 16)
            sp.dma_start(ones2[:], ones2_d).then_inc(s_load, 16)
            sp.dma_start(rw_sb[:], rw).then_inc(s_load, 16)
            sp.wait_ge(s_load, 80)
            sp.wait_ge(s_v, 11)
            sp.dma_start(gates_s, gates[0:1, :]).then_inc(s_o, 16)
            sp.wait_ge(s_o, 16)

        @block.scalar
        def _(act):
            act.wait_ge(s_load, 80)
            nc.scalar.activation(sc[:], c_sb[:], ACT.Silu).then_inc(s_silu, 1)

        @block.vector
        def _(dve):
            nc.vector.memset(ones[:], 1.0).then_inc(s_v, 1)
            dve.wait_ge(s_v, 1)
            dve.wait_ge(s_silu, 1)
            for dc in range(DC):
                for b in range(B):
                    last = nc.vector.tensor_scalar(scb[:, dc, b, :], ones[:], sc[:, dc, b:b + 1], None, ALU.mult)
            last.then_inc(s_bc, 1)
            dve.wait_ge(s_col, 1)
            nc.vector.tensor_copy(modT[:], pm[:]).then_inc(s_v, 1)
            dve.wait_ge(s_v, 2)
            for part in (CA, CB):
                nc.vector.tensor_scalar(modT[:, 2 * part:2 * part + 2, :], modT[:, 2 * part:2 * part + 2, :], 1.0, None,
                                        ALU.add).then_inc(s_v, 1)
            dve.wait_ge(s_row, 1)
            nc.vector.tensor_copy(raw[:], pg[:].rearrange("p a d -> p (a d)")).then_inc(s_v, 1)
            dve.wait_ge(s_v, 5)
            nc.vector.tensor_scalar(sgn[:], raw[:], 0.0, 2.0, ALU.is_ge, ALU.mult).then_inc(s_v, 1)
            nc.vector.tensor_scalar(absg[:], raw[:], -1.0, None, ALU.mult).then_inc(s_v, 1)
            dve.wait_ge(s_v, 7)
            nc.vector.tensor_tensor(absg[:], absg[:], raw[:], ALU.max).then_inc(s_v, 1)
            nc.vector.tensor_scalar(sgn[:], sgn[:], -1.0, None, ALU.add).then_inc(s_v, 1)
            dve.wait_ge(s_v, 9)
            nc.vector.tensor_scalar(absg[:], absg[:], 0.25, None, ALU.max).then_inc(s_v, 1)
            dve.wait_ge(s_v, 10)
            nc.vector.tensor_tensor(gates[:], absg[:], sgn[:], ALU.mult).then_inc(s_v, 1)
            dve.wait_ge(s_v, 11)

        @block.tensor
        def _(pe):
            pe.wait_ge(s_load, 80)
            pe.wait_ge(s_silu, 1)
            for j in range(12):
                for dc in range(DC):
                    last = nc.tensor.matmul(pm[:, j, :], wm[:, dc, j * P:(j + 1) * P], sc[:, dc, :],
                                            start=(dc == 0), stop=(dc == DC - 1))
            last.then_inc(s_col, 1)
            pe.wait_ge(s_bc, 1)
            for g, part in enumerate((GA, GB)):
                for b in range(B):
                    for dc in range(DC):
                        last = nc.tensor.matmul(pg[:, g * B + b, :], scb[:, dc, b, :],
                                                wm[:, dc, part * D:(part + 1) * D],
                                                start=(dc == 0), stop=(dc == DC - 1))
            last.then_inc(s_row, 1)


def norm_first(nc, sem, x, ident, modT, hT):
    s_x, s_st, s_ag, s_sq = sem("x_loaded"), sem("x_stats"), sem("x_moments"), sem("x_root")
    s_rs, s_n, s_t, s_e = sem("x_rstd"), sem("x_normed"), sem("x_turned"), sem("x_kept")
    with ExitStack() as st:
        xs = st.enter_context(nc.sbuf_tensor("xs", [P, B * NT, D], F32))
        stats = st.enter_context(nc.sbuf_tensor("stats", [P, B * NT, 6], F32))
        mv = st.enter_context(nc.sbuf_tensor("mv", [P, B * NT, 2], F32))
        eps = st.enter_context(nc.sbuf_tensor("eps", [P, 1], F32))
        sd = st.enter_context(nc.sbuf_tensor("sd", [P, B * NT], F32))
        rstd = st.enter_context(nc.sbuf_tensor("rstd", [P, B * NT], F32))
        pt = st.enter_context(nc.psum_tensor("pt", [P, 2, DC, G], F32))
        block = st.enter_context(nc.Block())

        @block.sync
        def _(sp):
            for b in range(B):
                sp.dma_start(xs[:, b * NT:(b + 1) * NT, :], x[:, b * NT:(b + 1) * NT, :]).then_inc(s_x, 16)

        @block.scalar
        def _(act):
            act.wait_ge(s_ag, B * NT + 1)
            nc.scalar.activation(sd[:], mv[:, :, 1], ACT.Sqrt, bias=eps[:, 0:1]).then_inc(s_sq, 1)

        @block.vector
        def _(dve):
            nc.vector.memset(eps[:], LN_EPS).then_inc(s_ag, 1)
            dve.wait_ge(s_x, 16 * B)
            with dve.Fori(0, B * NT) as i:
                nc.vector.bn_stats(stats[:, bass.ds(i, 1), :], xs[:, bass.ds(i, 1), :]).then_inc(s_st, 1)
            dve.wait_ge(s_st, B * NT)
            for i in range(B * NT):
                nc.vector.bn_aggr(mv[:, i, :], stats[:, i, :]).then_inc(s_ag, 1)
            dve.wait_ge(s_sq, 1)
            nc.vector.reciprocal(rstd[:], sd[:]).then_inc(s_rs, 1)
            dve.wait_ge(s_rs, 1)
            with dve.Fori(0, B * NT) as i:
                nc.vector.tensor_scalar(xs[:, bass.ds(i, 1), :], xs[:, bass.ds(i, 1), :], mv[:, bass.ds(i, 1), 0],
                                        rstd[:, bass.ds(i, 1)], ALU.subtract, ALU.mult).then_inc(s_n, 1)
            for g in range(B * GH):
                dve.wait_ge(s_t, g + 1)
                b = g // GH
                for dc in range(DC):
                    nc.vector.tensor_scalar(hT[:, dc, g * G:(g + 1) * G], pt[:, g % 2, dc, :],
                                            modT[:, 2 * CA + dc, b:b + 1], modT[:, 2 * SA + dc, b:b + 1],
                                            ALU.mult, ALU.add).then_inc(s_e, 1)
            dve.wait_ge(s_e, DC * B * GH)

        @block.tensor
        def _(pe):
            for g in range(B * GH):
                pe.wait_ge(s_n, (g + 1) * GT)
                if g >= 2:
                    pe.wait_ge(s_e, DC * (g - 1))
                for j in range(GT):
                    for dc in range(DC):
                        last = nc.tensor.transpose(pt[:, g % 2, dc, j * P:(j + 1) * P],
                                                   xs[:, g * GT + j, dc * P:(dc + 1) * P], ident[:])
                last.then_inc(s_t, 1)


def gate_scalars(nc, sem, wab, bab, hT, ab_s):
    s_w, s_p, s_a, s_o = sem("ab_weights"), sem("ab_product"), sem("ab_sigmoid"), sem("ab_stored")
    with ExitStack() as st:
        w = st.enter_context(nc.sbuf_tensor("wab_sb", [P, DC, 2 * H], F32))
        bias = st.enter_context(nc.sbuf_tensor("bab_sb", [2 * H, 1], F32))
        ab = st.enter_context(nc.sbuf_tensor("ab", [2 * H, B, T], F32))
        pa = st.enter_context(nc.psum_tensor("pa", [P, 2, G], F32))
        block = st.enter_context(nc.Block())

        @block.sync
        def _(sp):
            sp.dma_start(w[:], wab).then_inc(s_w, 16)
            sp.dma_start(bias[:], bab).then_inc(s_w, 16)
            sp.wait_ge(s_a, B * GH)
            sp.dma_start(ab_s, ab[:]).then_inc(s_o, 16)
            sp.wait_ge(s_o, 16)

        @block.scalar
        def _(act):
            act.wait_ge(s_w, 32)
            for g in range(B * GH):
                act.wait_ge(s_p, g + 1)
                nc.scalar.activation(ab[:].rearrange("h b t -> h (b t)")[:, g * G:(g + 1) * G],
                                     pa[0:2 * H, g % 2, :], ACT.Sigmoid, bias=bias[:, 0:1]).then_inc(s_a, 1)

        @block.tensor
        def _(pe):
            pe.wait_ge(s_w, 32)
            for g in range(B * GH):
                if g >= 2:
                    pe.wait_ge(s_a, g - 1)
                for dc in range(DC):
                    last = nc.tensor.matmul(pa[0:2 * H, g % 2, :], w[:, dc, :], hT[:, dc, g * G:(g + 1) * G],
                                            start=(dc == 0), stop=(dc == DC - 1))
                last.then_inc(s_p, 1)


def gate_logs(nc, sem, wab, bab_row, hT, la, bt):
    s_w, s_p, s_z, s_a, s_m = (sem("gl_weights"), sem("gl_product"), sem("gl_logits"), sem("gl_act"),
                               sem("gl_mins"))
    N = B * NT
    with ExitStack() as st:
        w = st.enter_context(nc.sbuf_tensor("gl_w", [P, DC, 2 * H], F32))
        bias = st.enter_context(nc.sbuf_tensor("gl_bias", [P, 2 * H], F32))
        z = st.enter_context(nc.sbuf_tensor("gl_z", [P, N, 2 * H], F32))
        az = st.enter_context(nc.sbuf_tensor("gl_abs", [P, N, H], F32))
        pz = st.enter_context(nc.psum_tensor("gl_pz", [P, N, 2 * H], F32))
        block = st.enter_context(nc.Block())

        @block.sync
        def _(sp):
            sp.dma_start(w[:], wab).then_inc(s_w, 16)
            sp.dma_start(bias[:], bab_row.broadcast_to([P, 2 * H])).then_inc(s_w, 16)

        @block.tensor
        def _(pe):
            pe.wait_ge(s_w, 32)
            for i in range(N):
                for dc in range(DC):
                    last = nc.tensor.matmul(pz[:, i, :], hT[:, dc, i * P:(i + 1) * P], w[:, dc, :],
                                            start=(dc == 0), stop=(dc == DC - 1))
            last.then_inc(s_p, 1)

        @block.vector
        def _(dve):
            dve.wait_ge(s_w, 32)
            dve.wait_ge(s_p, 1)
            brow = bias[:].rearrange("p (a h) -> p a h", a=1).broadcast_to([P, N // 2, 2 * H])
            for i in range(2):
                nc.vector.tensor_tensor(z[:, i * N // 2:(i + 1) * N // 2, :], pz[:, i * N // 2:(i + 1) * N // 2, :],
                                        brow, ALU.add).then_inc(s_z, 1)
            dve.wait_ge(s_z, 2)
            nc.vector.tensor_scalar(la[:], z[:, :, 0:H], 0.0, None, ALU.min).then_inc(s_m, 1)
            dve.wait_ge(s_a, 4)
            dve.wait_ge(s_m, 1)
            nc.vector.tensor_tensor(la[:], la[:], az[:], ALU.subtract).then_inc(s_m, 1)
            dve.wait_ge(s_m, 2)

        @block.scalar
        def _(act):
            act.wait_ge(s_z, 2)
            nc.scalar.activation(bt[:], z[:, :, H:2 * H], ACT.Sigmoid).then_inc(s_a, 1)
            nc.scalar.activation(az[:], z[:, :, 0:H], ACT.Abs).then_inc(s_a, 1)
            act.wait_ge(s_a, 2)
            nc.scalar.activation(az[:], az[:], ACT.Exp, scale=-1.0).then_inc(s_a, 1)
            act.wait_ge(s_a, 3)
            nc.scalar.activation(az[:], az[:], ACT.Ln, bias=1.0).then_inc(s_a, 1)


TRI64, TRI32, AFTER64, CHUNK0, CHUNK1 = range(5)
CH = 64
HB = 32
NCH = T // CH
NN = 2 * NT * 2
NG_K = 4
LIMIT = 4.99


def delta_fast(nc, sem, ident, wqkv, convp, tri_d, mask_d, hT, la, bt, ab_s, y_s, fmax):
    (s_turn, s_c, s_w, s_ar) = (sem("d_turn"), sem("d_const"), sem("d_weights"), sem("d_alpha_rows"))
    (s_proj, s_raw, s_tap, s_tp, s_silu) = (sem("d_proj"), sem("d_raw"), sem("d_taps"), sem("d_tap_part"),
                                            sem("d_silu"))
    (s_sel, s_lm, s_sm, s_pd, s_ex) = (sem("d_select"), sem("d_masked_logs"), sem("d_small_sums"), sem("d_log_sums"),
                                       sem("d_exp"))
    (s_kt, s_ktok, s_vt, s_v0, s_ksq) = (sem("d_k_turned"), sem("d_k_kept"), sem("d_v_turned"), sem("d_v0"),
                                         sem("d_k_square"))
    (s_n2, s_rt, s_sc, s_km) = (sem("d_norm2"), sem("d_norm"), sem("d_scalars"), sem("d_kmax"))
    (s_em, s_ec, s_y0) = (sem("d_masked_decay"), sem("d_decay_c"), sem("d_y0_khat"))
    (s_kk, s_T, s_kq, s_AT) = (sem("d_kk"), sem("d_T"), sem("d_kq"), sem("d_AT"))
    (s_x0, s_tq, s_sub, s_xt) = (sem("d_x_one"), sem("d_T_turned"), sem("d_subst"), sem("d_X_turned"))
    (s_p1, s_p1e, s_p2, s_p2e) = (sem("d_join1"), sem("d_join1_kept"), sem("d_join2"), sem("d_join2_kept"))
    (s_yk, s_yke, s_g, s_q) = (sem("d_yk"), sem("d_yk_kept"), sem("d_gamma_rows"), sem("d_q_decayed"))
    (s_U, s_Ue, s_S, s_Se, s_y, s_ye) = (sem("d_u"), sem("d_u_kept"), sem("d_s"), sem("d_s_kept"), sem("d_y"),
                                         sem("d_y_kept"))
    (s_ua, s_z, s_zt, s_m, s_r, s_end, s_o) = (sem("d_u_abs"), sem("d_z"), sem("d_z_turned"), sem("d_bound"),
                                               sem("d_bound_max"), sem("d_end"), sem("d_stored"))
    s_mx = sem("d_max")
    BP = B // 2
    TURNS = BP * M
    U6 = [(n, b2) for n in (1, 0, 2) for b2 in range(2)]

    with ExitStack() as st:
        def sb(name, *shape):
            return st.enter_context(nc.sbuf_tensor("d_" + name, [P, *shape], F32))

        tri = sb("tri", 5, P)
        msk = sb("msk", 2 * HB + CH)
        mask_d32, mask_o32, mask_t64 = msk[:, 0:HB], msk[:, HB:2 * HB], msk[:, 2 * HB:]
        w = sb("w", 3, DC, P)
        cw = sb("cw", 3, 5)
        raw = sb("raw", 6, 4 + T)
        tap = sb("tap", 2, T)
        qT, kT, vT = sb("qT", 2, T), sb("kT", 2, T), sb("vT", 2, T)
        res = [qT, kT, vT]
        lsu, bsu = sb("lsu", NN), sb("bsu", NN)
        ktok = sb("ktok", NN, DH)
        L = [sb("L0", NN, CH), sb("L1", NN, CH)]
        R = [sb("R0", NN, DH), sb("R1", NN, DH)]
        KG = [sb("KG0", NN, DH), sb("KG1", NN, DH)]
        QA = [sb("QA0", NN, CH), sb("QA1", NN, CH)]
        ksq = KG[0]
        Lm_t = R[0]
        Pp, Xn = sb("Pp", NN, HB), sb("Xn", NN, HB)
        Lm_d, Lm_o = Pp, Xn
        ex4 = sb("ex4", 4, NN)
        EX = sb("EX", 2, HB, HB)
        Ed, X, Eo = EX[:, 0], EX[:, 1], sb("Eo", NN, HB)
        Td, To = Ed, Eo
        Tq = sb("Tq", HB, HB)
        grow = EX[:].rearrange("p a n c -> p a (n c)")
        yT = grow
        Y0 = tap[:].rearrange("p a (n c) -> p (a n) c", c=DH)
        Z = KG
        Ua = ktok
        tmp = Td
        arow = sb("arow", 2, T)
        n2, rt, rn, brn, cc, yc = (sb("n2", NN), sb("rt", NN), sb("rn", NN), sb("brn", NN), sb("cc", NN),
                                   sb("yc", NN))
        kmax = sb("kmax", NN, NG_K)
        zero = sb("zero", CH)
        msc = tap
        fm = sb("fm", 8)
        fone = sb("fone", 1)
        ps = st.enter_context(nc.psum_tensor("d_ps", [P, 8, G], F32))
        SA_, SB_, SC_, SD_ = ps[:, 0:2], ps[:, 2:4], ps[:, 4:6], ps[:, 6:8]

        def nview(pair, width):
            return pair.rearrange("p a (n c) -> p (a n) c", c=width)

        half = [slice(0, CH), slice(CH, P)]

        def hview(pair):
            return pair.rearrange("p h (t c) -> p t h c", c=CH)

        def by_head(ap):
            return ap.rearrange("p (t h) c -> p t h c", h=2)

        def tile_heads(buf, rows, t8):
            return buf[rows].rearrange("p (b t h) c -> p b t (h c)", b=2, h=2)[:, :, t8, :]

        def wide(ap, n, width):
            return ap.rearrange("p (n a) -> p n a", a=1).broadcast_to([ap.shape[0], n, width])

        def mwide(ap, n):
            return ap.rearrange("p (a c) -> p a c", a=1).broadcast_to([P, n, ap.shape[1]])

        block = st.enter_context(nc.Block())

        def turns(eng, body):
            with eng.Fori(0, M) as m:
                for bp in range(BP):
                    body(bp, m, m * BP + bp)

        @block.sync
        def _(sp):
            sp.dma_start(tri[:], tri_d).then_inc(s_c, 16)
            sp.dma_start(msk[:], mask_d).then_inc(s_c, 16)
            sp.sem_inc(s_turn, 1)
            sp.dma_start(w[:], wqkv[0]).then_inc(s_w, 16)
            sp.dma_start(cw[:], convp[0]).then_inc(s_w, 16)
            for su in range(TURNS):
                m, bp = su // BP, su % BP
                if bp == BP - 1:
                    sp.dma_start(w[:], wqkv[(m + 1) % M]).then_inc(s_w, 16)
                    sp.dma_start(cw[:], convp[(m + 1) % M]).then_inc(s_w, 16)
                for b2 in range(2):
                    for h in range(2):
                        sp.dma_start(arow[h * DH:(h + 1) * DH, b2, :],
                                     ab_s[2 * m + h, 2 * bp + b2:2 * bp + b2 + 1, :].broadcast_to([DH, T])
                                     ).then_inc(s_ar, 16)
                sp.wait_ge(s_ye, 4 * (su + 1))
                for b2 in range(2):
                    sp.dma_start(y_s[2 * bp + b2, m], yT[:, b2, :]).then_inc(s_o, 16)
                sp.wait_ge(s_o, 32 * (su + 1))
                sp.wait_ge(s_end, su + 1)
                sp.sem_inc(s_turn, 1)

        @block.scalar
        def _(act):
            def keep(i, turn, pair):
                act.wait_ge(s_proj, turn * 6 + (i + 1))
                nc.scalar.activation(raw[:, i, 4:], pair.rearrange("p a c -> p (a c)"), ACT.Identity).then_inc(s_raw, 1)

            def tap_first(i, turn):
                act.wait_ge(s_raw, turn * 6 + (i + 1))
                if i >= 2:
                    act.wait_ge(s_silu, turn * 6 + (i - 1))
                nc.scalar.activation(tap[:, i % 2, :], raw[:, i, 4:], ACT.Identity, bias=cw[:, U6[i][0], 4:5],
                                     scale=cw[:, U6[i][0], 3:4]).then_inc(s_tap, 1)

            def silu(i, turn):
                act.wait_ge(s_tp, turn * 36 + 6 * (i + 1))
                nc.scalar.activation(res[U6[i][0]][:, U6[i][1], :], tap[:, i % 2, :], ACT.Silu).then_inc(s_silu, 1)

            act.wait_ge(s_w, 32)
            for i in range(6):
                keep(i, 0, (SD_, SA_)[i % 2])
            for i in range(2):
                tap_first(i, 0)
            for i in range(6):
                silu(i, 0)
                if i < 4:
                    tap_first(i + 2, 0)

            def body(bp, m, su):
                act.wait_ge(s_turn, su + 1)
                for b2, pair in enumerate((SC_, SD_)):
                    act.wait_ge(s_kt, su * 2 + (b2 + 1))
                    nc.scalar.activation(ktok[:, b2 * 16:(b2 + 1) * 16, :], nview(pair, DH),
                                         ACT.Identity).then_inc(s_ktok, 1)
                act.wait_ge(s_sm, su + 1)
                nc.scalar.activation(ex4[:].rearrange("p a n -> p (a n)"), ps[:, 0, 0:4 * NN],
                                     ACT.Exp).then_inc(s_ex, 1)
                for i, (dst, pair) in enumerate(((Ed, SB_), (Eo, SC_))):
                    act.wait_ge(s_pd, su * 4 + (i + 1))
                    nc.scalar.activation(dst[:], nview(pair, HB), ACT.Exp).then_inc(s_ex, 1)
                for b2, pair in enumerate((SD_, SA_)):
                    act.wait_ge(s_pd, su * 4 + (b2 + 3))
                    for cp in range(2):
                        last = nc.scalar.activation(QA[cp][half[cp], b2 * 16:(b2 + 1) * 16, :],
                                                    nview(pair, CH)[half[cp]], ACT.Exp)
                    last.then_inc(s_ex, 1)
                act.wait_ge(s_n2, su + 1)
                nc.scalar.activation(rt[:], n2[:], ACT.Sqrt).then_inc(s_rt, 1)
                for i in range(6):
                    keep(i, su + 1, (SD_, SA_)[i % 2])
                for b2, pair in enumerate((SD_, SA_)):
                    act.wait_ge(s_p1, su * 2 + (b2 + 1))
                    for cp in range(2):
                        rows = slice(cp * CH, cp * CH + HB)
                        last = nc.scalar.activation(Pp[rows, b2 * 16:(b2 + 1) * 16, :], nview(pair, HB)[rows, 0:16, :],
                                                    ACT.Identity)
                    last.then_inc(s_p1e, 1)
                for b2, pair in enumerate((SD_, SA_)):
                    act.wait_ge(s_p2, su * 2 + (b2 + 1))
                    for cp in range(2):
                        rows = slice(cp * CH, cp * CH + HB)
                        last = nc.scalar.activation(L[cp][rows, b2 * 16:(b2 + 1) * 16, HB:CH],
                                                    nview(pair, HB)[rows, 16:32, :], ACT.Identity, scale=-1.0)
                    last.then_inc(s_p2e, 1)
                for b2, pair in enumerate((SB_, SC_)):
                    act.wait_ge(s_yk, su * 2 + (b2 + 1))
                    for cp in range(2):
                        last = nc.scalar.activation(L[cp][half[1 - cp], b2 * 16:(b2 + 1) * 16, :],
                                                    nview(pair, CH)[half[1 - cp]], ACT.Identity)
                    last.then_inc(s_yke, 1)
                def keep_y(hf):
                    act.wait_ge(s_y, su * NCH + 8 * (hf + 1))
                    for b2 in range(2):
                        nc.scalar.activation(yT[:, b2, hf * G:(hf + 1) * G], ps[:, 2 * hf + b2, :],
                                             ACT.Identity).then_inc(s_ye, 1)

                def tiles_of(buf, cp, hf):
                    return buf[half[cp]].rearrange("p (b t h) c -> p b t (h c)", b=2, h=2)[:, :, 4 * hf:4 * hf + 4, :]

                def abs_u(hf):
                    act.wait_ge(s_Ue, su * NCH + 8 * (hf + 1))
                    for cp in range(2):
                        last = nc.scalar.activation(tiles_of(Ua, cp, hf), tiles_of(R[cp], cp, hf), ACT.Abs)
                    last.then_inc(s_ua, 1)

                if bp == BP - 1:
                    act.wait_ge(s_w, m * 32 + 64)
                for i in range(2):
                    tap_first(i, su + 1)
                act.wait_ge(s_y0, su * 5 + 5)
                act.wait_ge(s_km, su + 1)
                for i in range(6):
                    silu(i, su + 1)
                    if i < 4:
                        tap_first(i + 2, su + 1)
                    if i == 3:
                        keep_y(0)
                        abs_u(0)
                abs_u(1)
                keep_y(1)
            turns(act, body)

        @block.gpsimd
        def _(pool):
            def body(bp, m, su):
                count = pool.compute_val(su + 1)
                pool.wait_ge(s_c, 32)
                pool.wait_ge(s_turn, count)
                nc.gpsimd.memset(X[:], 0.0).then_inc(s_x0, 1)
                count = pool.compute_val(su * 2 + 1)
                pool.wait_ge(s_c, 32)
                pool.wait_ge(s_x0, count)
                nc.gpsimd.memset(X[:].rearrange("p r c -> p (r c)")[:, 0:HB * HB:HB + 1], 1.0).then_inc(s_x0, 1)
                pool.wait_ge(s_sel, su * 2 + 2)
                nc.gpsimd.tensor_tensor(Lm_d[:], wide(lsu[:], NN, HB), mwide(mask_d32, NN), ALU.mult)
                nc.gpsimd.tensor_tensor(Lm_o[:], wide(lsu[:], NN, HB), mwide(mask_o32, NN), ALU.mult)
                nc.gpsimd.tensor_tensor(Lm_t[:], wide(lsu[:], NN, CH), mwide(mask_t64, NN), ALU.mult).then_inc(s_lm, 1)
                pool.wait_ge(s_ktok, su * 2 + 2)
                nc.gpsimd.tensor_tensor(ksq[:], ktok[:], ktok[:], ALU.mult).then_inc(s_ksq, 1)
                pool.wait_ge(s_ex, su * 5 + 5)
                nc.gpsimd.tensor_tensor(Ed[:], Ed[:], mwide(mask_d32, NN), ALU.mult).then_inc(s_em, 1)
                for cp in range(2):
                    pool.wait_ge(s_em, su * 3 + (cp + 1))
                    nc.gpsimd.tensor_tensor(QA[cp][half[cp]], QA[cp][half[cp]], mwide(mask_t64, NN)[half[cp]],
                                            ALU.mult).then_inc(s_em, 1)
                pool.wait_ge(s_em, su * 3 + 3)
                pool.wait_ge(s_n2, su + 1)
                for cp in range(2):
                    if cp:
                        pool.wait_ge(s_y0, su * 5 + 2)
                    nc.gpsimd.tensor_tensor(KG[cp][half[cp]], ktok[half[cp]], wide(ex4[half[cp], 1, :], NN, DH),
                                            ALU.mult).then_inc(s_y0, 1)
                    pool.wait_ge(s_y0, su * 5 + (2 * cp + 1))
                    rows = half[1 - cp]
                    nc.gpsimd.tensor_tensor(KG[cp][rows], wide(ex4[rows, 2 + cp, :], NN, DH),
                                            mwide(ident[:, rows], NN)[rows], ALU.mult).then_inc(s_y0, 1)
                pool.wait_ge(s_y0, su * 5 + 4)
                pool.wait_ge(s_sc, su * 5 + 5)
                nc.gpsimd.tensor_tensor(Y0, ktok[:], wide(yc[:], NN, DH), ALU.mult).then_inc(s_y0, 1)
                pool.wait_ge(s_ua, su * 2 + 2)
                pool.wait_ge(s_km, su + 1)
                for g in range(NG_K):
                    if g >= 2:
                        pool.wait_ge(s_zt, su * 2 * NG_K + 2 * (g - 1))
                    nc.gpsimd.tensor_tensor(Z[g % 2][:], Ua[:], wide(kmax[:, :, g], NN, DH), ALU.mult).then_inc(s_z, 1)
            turns(pool, body)

        @block.vector
        def _(dve):
            dve.wait_ge(s_c, 32)
            nc.vector.memset(raw[:, :, 0:4], 0.0).then_inc(s_mx, 1)
            nc.vector.memset(zero[:], 0.0).then_inc(s_mx, 1)
            nc.vector.memset(L[0][HB:CH, :, 0:HB], 0.0).then_inc(s_mx, 1)
            nc.vector.memset(L[1][CH + HB:P, :, 0:HB], 0.0).then_inc(s_mx, 1)
            nc.vector.memset(fmax[:], 0.0).then_inc(s_mx, 1)
            dve.wait_ge(s_mx, 5)

            def tap_part(o, turn):
                i, j, hf = o // 6, o % 6 // 2, o % 2
                if j == 0:
                    dve.wait_ge(s_tap, turn * 6 + (i + 1))
                else:
                    dve.wait_ge(s_tp, turn * 36 + (o - 1))
                k, n = 2 - j, U6[i][0]
                hs = slice(hf * G, (hf + 1) * G)
                nc.vector.scalar_tensor_tensor(
                    out=tap[:, i % 2, hs], in0=raw[:, i, 1 + k + hf * G:1 + k + (hf + 1) * G],
                    scalar=cw[:, n, k:k + 1], in1=tap[:, i % 2, hs], op0=ALU.mult, op1=ALU.add).then_inc(s_tp, 1)

            dve.wait_ge(s_w, 32)
            for o in range(36):
                tap_part(o, 0)

            def body(bp, m, su):
                dve.wait_ge(s_turn, su + 1)
                for dst, src in ((lsu, la), (bsu, bt)):
                    nc.vector.tensor_scalar(dst[:].rearrange("p (n h) -> p n h", h=2),
                                            src[:, bp * 16:(bp + 1) * 16, bass.ds(m * 2, 2)], 1.0, None,
                                            ALU.mult).then_inc(s_sel, 1)
                dve.wait_ge(s_ksq, su + 1)
                nc.vector.tensor_reduce(n2[:], ksq[:], AX_X,
                                        ALU.add).then_inc(s_n2, 1)
                dve.wait_ge(s_rt, su + 1)
                nc.vector.tensor_scalar(rn[:], rt[:], NORM_EPS, None, ALU.max).then_inc(s_sc, 1)
                dve.wait_ge(s_sc, su * 5 + 1)
                nc.vector.reciprocal(rn[:], rn[:]).then_inc(s_sc, 1)
                dve.wait_ge(s_sc, su * 5 + 2)
                nc.vector.tensor_tensor(brn[:], bsu[:], rn[:], ALU.mult).then_inc(s_sc, 1)
                dve.wait_ge(s_sc, su * 5 + 3)
                nc.vector.tensor_tensor(cc[:], brn[:], rn[:], ALU.mult).then_inc(s_sc, 1)
                dve.wait_ge(s_sc, su * 5 + 4)
                dve.wait_ge(s_ex, su * 5 + 1)
                nc.vector.scalar_tensor_tensor(out=yc[:], in0=cc[:], scalar=-1.0, in1=ex4[:, 0, :], op0=ALU.mult,
                                               op1=ALU.mult).then_inc(s_sc, 1)
                dve.wait_ge(s_em, su * 3 + 1)
                nc.vector.tensor_tensor(Ed[:], Ed[:], wide(cc[:], NN, HB), ALU.mult).then_inc(s_ec, 1)
                nc.vector.tensor_tensor(Eo[:], Eo[:], wide(cc[:], NN, HB), ALU.mult).then_inc(s_ec, 1)
                dve.wait_ge(s_ec, su * 2 + 2)
                for b2, pair in enumerate((SD_, SA_)):
                    dve.wait_ge(s_kk, su * 2 + (b2 + 1))
                    ns = slice(b2 * 16, (b2 + 1) * 16)
                    for q4 in range(4):
                        rows = slice(q4 * HB, (q4 + 1) * HB)
                        c0 = (q4 % 2) * HB
                        ins = nc.vector.tensor_tensor(by_head(Td[rows, ns, :]), hview(pair)[rows, :, :, c0:c0 + HB],
                                                      by_head(Ed[rows, ns, :]), ALU.mult)
                        if q4 % 2:
                            ins = nc.vector.tensor_tensor(by_head(To[rows, ns, :]), hview(pair)[rows, :, :, 0:HB],
                                                          by_head(Eo[rows, ns, :]), ALU.mult)
                    ins.then_inc(s_T, 1)
                dve.wait_ge(s_T, su * 2 + 2)
                nc.vector.transpose(Tq[:], Td[:].rearrange("p n s -> p s n")).then_inc(s_tq, 1)
                dve.wait_ge(s_em, su * 3 + 3)
                for b2, pair in enumerate((SD_, SA_)):
                    dve.wait_ge(s_kq, su * 2 + (b2 + 1))
                    ns = slice(b2 * 16, (b2 + 1) * 16)
                    for cp in range(2):
                        a = by_head(QA[cp][half[cp], ns, :])
                        ins = nc.vector.tensor_tensor(a, hview(pair)[half[cp]], a, ALU.mult)
                    ins.then_inc(s_AT, 1)
                dve.wait_ge(s_x0, su * 2 + 2)
                dve.wait_ge(s_tq, su + 1)
                for s in range(HB - 1):
                    left, known = HB - 1 - s, s + 1
                    if s:
                        dve.wait_ge(s_sub, su * 62 + 2 * s)
                    tv = tmp[:].rearrange("p a b -> p (a b)")[:, 0:left * known].rearrange("p (r c) -> p r c", c=known)
                    nc.vector.tensor_tensor(
                        tv, Tq[:, s, s + 1:].rearrange("p (r a) -> p r a", a=1).broadcast_to([P, left, known]),
                        X[:, s, 0:known].rearrange("p (a c) -> p a c", a=1).broadcast_to([P, left, known]),
                        ALU.mult).then_inc(s_sub, 1)
                    dve.wait_ge(s_sub, su * 62 + (2 * s + 1))
                    nc.vector.tensor_tensor(X[:, s + 1:, 0:known], X[:, s + 1:, 0:known], tv,
                                            ALU.subtract).then_inc(s_sub, 1)
                dve.wait_ge(s_sub, su * 62 + 62)
                for q4 in range(4):
                    rows = slice(q4 * HB, (q4 + 1) * HB)
                    c0 = (q4 % 2) * HB
                    nc.vector.transpose(L[q4 // 2][rows, :, c0:c0 + HB].rearrange("p n r -> p r n"), X[rows])
                nc.vector.transpose(Xn[:].rearrange("p n c -> p c n"),
                                    X[:].rearrange("p r c -> p c r")).then_inc(s_xt, 1)
                for b2, pair in enumerate((SB_, SC_)):
                    dve.wait_ge(s_vt, su * 2 + (b2 + 1))
                    ns = slice(b2 * 16, (b2 + 1) * 16)
                    for cp in range(2):
                        ins = nc.vector.tensor_tensor(R[cp][half[cp], ns, :], nview(pair, DH)[half[cp]],
                                                      wide(brn[half[cp], ns], 16, DH), ALU.mult)
                    ins = nc.vector.memset(R[0][half[1], b2 * 16:b2 * 16 + 2, :], 0.0)
                    ins.then_inc(s_v0, 1)
                dve.wait_ge(s_ar, su * 64 + 64)
                dve.wait_ge(s_xt, su + 1)
                for b2 in range(2):
                    for c in range(NCH):
                        ins = nc.vector.tensor_tensor_scan(grow[:, b2, c * CH:(c + 1) * CH],
                                                           arow[:, b2, c * CH:(c + 1) * CH], zero[:], 1.0,
                                                           ALU.mult, ALU.add)
                ins.then_inc(s_g, 1)
                dve.wait_ge(s_g, su + 1)
                for cp in range(2):
                    for h in range(2):
                        for b2 in range(2):
                            ins = nc.vector.tensor_tensor(
                                QA[cp][half[1 - cp], b2 * 16 + h:(b2 + 1) * 16:2, :],
                                qT[half[h], b2, :].rearrange("p (t a c) -> p t a c", a=2, c=CH)[:, :, cp, :],
                                grow[half[h], b2, :].rearrange("p (t a c) -> p t a c", a=2, c=CH)[:, :, cp, :],
                                ALU.mult)
                ins.then_inc(s_q, 1)
                dve.wait_ge(s_ktok, su * 2 + 2)
                nc.vector.tensor_reduce(kmax[:].rearrange("p n g -> p (n g)"),
                                        ktok[:].rearrange("p n (g c) -> p (n g) c", g=NG_K), AX_X, ALU.max,
                                        apply_absolute_value=True).then_inc(s_km, 1)
                if bp == BP - 1:
                    dve.wait_ge(s_w, m * 32 + 64)
                for c in range(NCH):
                    t8, cp = c // 2, c % 2
                    rows = half[cp]
                    dve.wait_ge(s_U, su * NCH + (c + 1))
                    nc.vector.tensor_copy(tile_heads(R[cp], rows, t8),
                                          ps[rows, 6, 0:4 * DH].rearrange("p (b c) -> p b c", b=2)
                                          ).then_inc(s_Ue, 1)
                    tap_part(2 * c, su + 1)
                    if c < NCH - 1:
                        dve.wait_ge(s_S, su * (NCH - 1) + (c + 1))
                        nc.vector.tensor_copy(tile_heads(R[1 - cp], rows, (c + 1) // 2),
                                              ps[rows, 7, 0:4 * DH].rearrange("p (b c) -> p b c", b=2)
                                              ).then_inc(s_Se, 1)
                    tap_part(2 * c + 1, su + 1)
                for o in range(2 * NCH, 36):
                    tap_part(o, su + 1)
                dve.wait_ge(s_silu, su * 6 + 12)
                for i in range(2 * NG_K):
                    g, b2 = i // 2, i % 2
                    pair = (SC_, SD_)[i % 2]
                    dve.wait_ge(s_zt, su * 2 * NG_K + (i + 1))
                    if i >= 2:
                        dve.wait_ge(s_r, su * 2 * NG_K + (i - 1))
                    for hf in range(2):
                        hs = slice(hf * G, (hf + 1) * G)
                        nc.vector.tensor_tensor_scan(
                            msc[:, i % 2, hs], arow[:, b2, hs], pair[:, hf, :],
                            0.0 if hf == 0 else msc[:, i % 2, G - 1:G], ALU.mult, ALU.add).then_inc(s_m, 1)
                        dve.wait_ge(s_m, su * 4 * NG_K + (2 * i + hf + 1))
                    nc.vector.tensor_reduce(fm[:, i:i + 1], msc[:, i % 2, :], AX_X, ALU.max).then_inc(s_r, 1)
                dve.wait_ge(s_r, su * 2 * NG_K + 2 * NG_K)
                nc.vector.tensor_reduce(fone[:], fm[:], AX_X, ALU.max).then_inc(s_mx, 1)
                dve.wait_ge(s_mx, su * 1 + 6)
                nc.vector.tensor_tensor(fmax[:], fmax[:], fone[:], ALU.max).then_inc(s_end, 1)
            turns(dve, body)
            dve.wait_ge(s_end, TURNS)

        @block.tensor
        def _(pe):
            pe.wait_ge(s_c, 32)

            def proj(i, turn, bp):
                n, b2 = U6[i]
                if i >= 2:
                    pe.wait_ge(s_raw, turn * 6 + (i - 1))
                for g in range(GH):
                    for dc in range(DC):
                        last = nc.tensor.matmul((SD_, SA_)[i % 2][:, g, :], w[:, n, dc, :],
                                                hT[:, dc, (2 * bp + b2) * T + g * G:(2 * bp + b2) * T + (g + 1) * G],
                                                start=(dc == 0), stop=(dc == DC - 1))
                last.then_inc(s_proj, 1)

            pe.wait_ge(s_w, 32)
            for i in range(6):
                proj(i, 0, 0)

            def body(bp, m, su):
                pe.wait_ge(s_turn, su + 1)
                for b2, pair in enumerate((SC_, SD_)):
                    pe.wait_ge(s_silu, su * 6 + (b2 + 1))
                    for t8 in range(NT):
                        last = nc.tensor.transpose(nview(pair, P)[:, t8, :], kT[:, b2, t8 * P:(t8 + 1) * P],
                                                   ident[:])
                    last.then_inc(s_kt, 1)
                pe.wait_ge(s_lm, su + 1)
                for i, c in enumerate((TRI64, AFTER64, CHUNK0, CHUNK1)):
                    last = nc.tensor.matmul(ps[:, 0, i * NN:(i + 1) * NN], tri[:, c, :], lsu[:], start=True,
                                            stop=True)
                last.then_inc(s_sm, 1)
                for a in range(2):
                    last = nc.tensor.matmul(SB_[:, a, :], tri[:, TRI32, :],
                                            Lm_d[:].rearrange("p n c -> p (n c)")[:, a * G:(a + 1) * G],
                                            start=True, stop=True)
                last.then_inc(s_pd, 1)
                pe.wait_ge(s_ktok, su * 2 + 2)
                for a in range(2):
                    last = nc.tensor.matmul(SC_[:, a, :], tri[:, TRI64, :],
                                            Lm_o[:].rearrange("p n c -> p (n c)")[:, a * G:(a + 1) * G],
                                            start=True, stop=True)
                last.then_inc(s_pd, 1)
                pe.wait_ge(s_ex, su * 5 + 1)
                for b2, pair in enumerate((SD_, SA_)):
                    for a in range(2):
                        last = nc.tensor.matmul(pair[:, a, :], tri[:, AFTER64, :],
                                                Lm_t[:, b2 * 16 + 8 * a:b2 * 16 + 8 * (a + 1), :]
                                            .rearrange("p n c -> p (n c)"),
                                                start=True, stop=True)
                    last.then_inc(s_pd, 1)
                for b2, pair in enumerate((SB_, SC_)):
                    pe.wait_ge(s_silu, su * 6 + (5 + b2))
                    pe.wait_ge(s_ex, su * 5 + (2 + b2))
                    for t8 in range(NT):
                        last = nc.tensor.transpose(nview(pair, P)[:, t8, :], vT[:, b2, t8 * P:(t8 + 1) * P],
                                                   ident[:])
                    last.then_inc(s_vt, 1)
                for other, order, s_done in ((kT, (SD_, SA_), s_kk), (qT, (SD_, SA_), s_kq)):
                    for b2, pair in enumerate(order):
                        freed, kept = (s_ex, su * 5 + (4 + b2)) if other is kT else (s_T, su * 2 + (b2 + 1))
                        count = pe.compute_val(kept)
                        pe.wait_ge(s_c, 32)
                        pe.wait_ge(freed, count)
                        for t8 in range(NT):
                            for h in range(2):
                                for cp in range(2):
                                    c = 2 * t8 + cp
                                    hr, cr = slice(h * DH, (h + 1) * DH), slice(cp * CH, (cp + 1) * CH)
                                    last = nc.tensor.matmul(hview(pair)[cr, t8, h, :],
                                                            kT[hr, b2, c * CH:(c + 1) * CH],
                                                            other[hr, b2, c * CH:(c + 1) * CH],
                                                            start=True, stop=True)
                        last.then_inc(s_done, 1)
                if bp == BP - 1:
                    pe.wait_ge(s_w, m * 32 + 64)
                for i in range(6):
                    if i < 2:
                        pe.wait_ge(s_AT, su * 2 + (i + 1))
                    proj(i, su + 1, (bp + 1) % BP)
                for b2 in range(2):
                    count, count1 = pe.compute_val(su + 1), pe.compute_val(su * 6 + (11 + b2))
                    pe.wait_ge(s_c, 32)
                    pe.wait_ge(s_xt, count)
                    pe.wait_ge(s_raw, count1)
                    for n in range(b2 * 16, (b2 + 1) * 16):
                        for cp in range(2):
                            lo, hi = slice(cp * CH, cp * CH + HB), slice(cp * CH + HB, (cp + 1) * CH)
                            last = nc.tensor.matmul(nview((SD_, SA_)[b2], HB)[lo, n % 16, :], To[hi, n, :],
                                                    L[cp][hi, n, HB:CH], start=True, stop=True)
                    last.then_inc(s_p1, 1)
                for b2 in range(2):
                    count = pe.compute_val(su * 2 + (b2 + 1))
                    pe.wait_ge(s_c, 32)
                    pe.wait_ge(s_p1e, count)
                    for n in range(b2 * 16, (b2 + 1) * 16):
                        for cp in range(2):
                            lo = slice(cp * CH, cp * CH + HB)
                            last = nc.tensor.matmul(nview((SD_, SA_)[b2], HB)[lo, 16 + n % 16, :], Xn[lo, n, :],
                                                    Pp[lo, n, :], start=True, stop=True)
                    last.then_inc(s_p2, 1)
                for b2, pair in enumerate((SB_, SC_)):
                    count, count1, count2 = (pe.compute_val(su * 2 + (b2 + 1)), pe.compute_val(su * 5 + 5),
                                             pe.compute_val(su * 2 + (b2 + 1)))
                    pe.wait_ge(s_c, 32)
                    pe.wait_ge(s_p2e, count)
                    pe.wait_ge(s_y0, count1)
                    pe.wait_ge(s_v0, count2)
                    for n in range(b2 * 16, (b2 + 1) * 16):
                        for cp in range(2):
                            last = nc.tensor.matmul(nview(pair, CH)[half[1 - cp], n % 16, :], Y0[half[cp], n, :],
                                                    L[cp][half[cp], n, :], start=True, stop=True)
                    last.then_inc(s_yk, 1)
                pe.wait_ge(s_yke, su * 2 + 2)
                pe.wait_ge(s_v0, su * 2 + 2)
                pe.wait_ge(s_q, su + 1)

                def heads(c):
                    for b2 in range(2):
                        for h in range(2):
                            yield b2, h, b2 * 16 + (c // 2) * 2 + h

                def y_of(c, which):
                    for b2, h, n in heads(c):
                        if b2 == which:
                            last = nc.tensor.matmul(ps[half[h], 2 * (c // 8) + b2, (c % 8) * CH:(c % 8 + 1) * CH],
                                                    R[c % 2][:, n, :], QA[c % 2][:, n, :], start=True, stop=True)
                    if which == 1:
                        last.then_inc(s_y, 1)

                for c in range(NCH):
                    cp = c % 2
                    if c:
                        pe.wait_ge(s_Se, su * (NCH - 1) + c)
                    for b2, h, n in heads(c):
                        last = nc.tensor.matmul(ps[half[cp], 6, (2 * b2 + h) * DH:(2 * b2 + h + 1) * DH],
                                                L[cp][:, n, :], R[cp][:, n, :], start=True, stop=True)
                    last.then_inc(s_U, 1)
                    if c:
                        y_of(c - 1, 0)
                    pe.wait_ge(s_Ue, su * NCH + (c + 1))
                    if c < NCH - 1:
                        for b2, h, n in heads(c):
                            last = nc.tensor.matmul(ps[half[cp], 7, (2 * b2 + h) * DH:(2 * b2 + h + 1) * DH],
                                                    KG[cp][:, n, :], R[cp][:, n, :], start=True, stop=True)
                        last.then_inc(s_S, 1)
                    if c:
                        y_of(c - 1, 1)
                y_of(NCH - 1, 0)
                y_of(NCH - 1, 1)
                for i in range(2 * NG_K):
                    g, b2 = i // 2, i % 2
                    pe.wait_ge(s_z, su * NG_K + (g + 1))
                    if i >= 2:
                        pe.wait_ge(s_m, su * 4 * NG_K + 2 * (i - 1))
                    for t8 in range(NT):
                        last = nc.tensor.transpose(nview((SC_, SD_)[i % 2], P)[:, t8, :], Z[g % 2][:, b2 * 16 + 2 * t8:b2 * 16 + 2 * t8 + 2, :]
                                                   .rearrange("p h c -> p (h c)"),
                                                   ident[:])
                    last.then_inc(s_zt, 1)
            turns(pe, body)


def judge(nc, sem, fmax, flag):
    s_v, s_g = sem("j_vector"), sem("j_all")
    with ExitStack() as st:
        ok = st.enter_context(nc.sbuf_tensor("j_ok", [P, 1], F32))
        bad = st.enter_context(nc.sbuf_tensor("j_bad", [P, 1], F32))
        bad_all = st.enter_context(nc.sbuf_tensor("j_bad_all", [P, 1], F32))
        block = st.enter_context(nc.Block())

        @block.vector
        def _(dve):
            nc.vector.tensor_scalar(ok[:], fmax[:], LIMIT, None, ALU.is_lt).then_inc(s_v, 1)
            dve.wait_ge(s_v, 1)
            nc.vector.tensor_scalar(bad[:], ok[:], 0.5, None, ALU.is_lt).then_inc(s_v, 1)
            dve.wait_ge(s_g, 1)
            nc.vector.tensor_copy(flag[:], bad_all[:]).then_inc(s_v, 1)
            dve.wait_ge(s_v, 3)

        @block.gpsimd
        def _(pool):
            pool.wait_ge(s_v, 2)
            nc.gpsimd.partition_all_reduce(bad_all[:], bad[:], P, bass.bass_isa.ReduceOp.max).then_inc(s_g, 1)


def project(nc, sem, wqkv, convp, ones2, hT, qkv_s):
    s_w, s_p, s_raw, s_tap = sem("p_weights"), sem("p_product"), sem("p_raw"), sem("p_taps")
    s_silu, s_sq, s_nn, s_rt = sem("p_silu"), sem("p_square"), sem("p_norm2"), sem("p_norm")
    s_k, s_o, s_z = sem("p_kn"), sem("p_stored"), sem("p_zero")
    s_r, s_tick, s_st = sem("p_recip"), sem("p_tick"), sem("p_unit_stored")
    with ExitStack() as st:
        w = st.enter_context(nc.sbuf_tensor("wqkv_sb", [P, 2, 3, DC, P], F32))
        cw = st.enter_context(nc.sbuf_tensor("convp_sb", [P, 2, 3, 5], F32))
        raw = st.enter_context(nc.sbuf_tensor("raw", [P, 4 + T], F32))
        tap = st.enter_context(nc.sbuf_tensor("tap", [P, T], F32))
        res = st.enter_context(nc.sbuf_tensor("res", [P, 3, T], F32))
        sq = st.enter_context(nc.sbuf_tensor("sq", [P, T], F32))
        tick2 = st.enter_context(nc.sbuf_tensor("p_tick2", [P, 8], F32))
        tick = st.enter_context(nc.sbuf_tensor("p_tick", [P, 8], F32))
        pp = st.enter_context(nc.psum_tensor("pp", [P, 2, T], F32))
        pn = st.enter_context(nc.psum_tensor("pn", [P, T], F32))
        block = st.enter_context(nc.Block())
        NB = M * B

        @block.sync
        def _(sp):
            sp.wait_ge(s_o, M * B * 48)

        @block.gpsimd
        def _(pool):

            with pool.Fori(0, M) as m:
                pool.wait_ge(s_tap, 1 + m * (B * 3))
                pool.wait_ge(s_tick, 1 + m * (2 * B + 1))
                nc.gpsimd.tensor_tensor(tick[:], ones2[:, 0:8], ones2[:, 0:8], ALU.add).then_inc(s_tick, 1)
                pool.dma_start(w[:, 0], wqkv[bass.ds(m, 1)].rearrange("a p n c k -> (a p) n c k")).then_inc(s_w, 16)
                pool.dma_start(cw[:, 0], convp[bass.ds(m, 1)].rearrange("a p n k -> (a p) n k")).then_inc(s_w, 16)
                for b in range(B):
                    pool.wait_ge(s_silu, 1 + m * (3 * B) + 3 * (b + 1))
                    pool.wait_ge(s_k, 1 + m * B + (b + 1))
                    pool.wait_ge(s_tick, 1 + m * (2 * B + 1) + (2 * b + 1))
                    nc.gpsimd.tensor_tensor(tick[:], ones2[:, 0:8], ones2[:, 0:8], ALU.add).then_inc(s_tick, 1)
                    for n in range(3):
                        pool.dma_start(qkv_s[n, b, bass.ds(m, 1)].rearrange("a p t -> (a p) t"),
                                     res[:, n, :]).then_inc(s_o, 16)
                    pool.wait_ge(s_o, m * (48 * B) + 48 * (b + 1))
                    pool.wait_ge(s_tick, 1 + m * (2 * B + 1) + (2 * b + 2))
                    nc.gpsimd.tensor_tensor(tick[:], ones2[:, 0:8], ones2[:, 0:8], ALU.add).then_inc(s_tick, 1)
                    pool.wait_ge(s_tick, 1 + m * (2 * B + 1) + (2 * b + 3))
                    nc.gpsimd.tensor_tensor(tick2[:], ones2[:, 0:8], ones2[:, 0:8], ALU.add).then_inc(s_st, 1)

        @block.scalar
        def _(act):
            with act.Fori(0, M) as m:
                act.wait_ge(s_w, m * 32 + 32)
                for b in range(B):
                    for n in range(3):
                        u = 3 * b + n
                        act.wait_ge(s_p, m * (3 * B) + (u + 1))
                        if u == 0:
                            act.wait_ge(s_z, m * 1 + 1)
                        else:
                            act.wait_ge(s_tap, 1 + m * (3 * B) + u)
                        act.wait_ge(s_silu, 1 + m * (3 * B) + u)
                        nc.scalar.activation(raw[:, 4:], pp[:, u % 2, :], ACT.Identity).then_inc(s_raw, 1)
                        nc.scalar.activation(tap[:], pp[:, u % 2, :], ACT.Identity, bias=cw[:, 0, n, 4:5],
                                             scale=cw[:, 0, n, 3:4]).then_inc(s_raw, 1)
                        act.wait_ge(s_tap, 1 + m * (3 * B) + (u + 1))
                        if n == 0:
                            act.wait_ge(s_st, 1 + m * B + b)
                        nc.scalar.activation(res[:, n, :], tap[:], ACT.Silu).then_inc(s_silu, 1)
                        if n == 1:
                            act.wait_ge(s_silu, 1 + m * (3 * B) + (u + 1))
                            act.wait_ge(s_k, 1 + m * B + b)
                            nc.scalar.activation(sq[:], res[:, 1, :], ACT.Square).then_inc(s_sq, 1)
                            act.wait_ge(s_nn, m * B + (b + 1))
                            nc.scalar.activation(sq[:], pn[:], ACT.Sqrt).then_inc(s_rt, 1)

        @block.vector
        def _(dve):
            nc.vector.memset(raw[:, 0:4], 0.0).then_inc(s_z, 1)
            with dve.Fori(0, M) as m:
                dve.wait_ge(s_w, m * 32 + 32)
                for b in range(B):
                    for n in range(3):
                        u = 3 * b + n
                        dve.wait_ge(s_raw, 1 + m * (6 * B) + (2 * u + 2))
                        for i, k in enumerate((2, 1, 0)):
                            ins = nc.vector.scalar_tensor_tensor(
                                out=tap[:], in0=raw[:, 1 + k:1 + k + T], scalar=cw[:, 0, n, k:k + 1],
                                in1=tap[:], op0=ALU.mult, op1=ALU.add)
                            if i < 2:
                                ins.then_inc(s_r, 1)
                                dve.wait_ge(s_r, m * (3 * B * 2 + 2 * B) + (6 + 2) * b + 2 * n + (2 if n == 2 else 0)
                                            + i + 1)
                            elif u == 3 * B - 1:
                                ins.then_inc(s_tap, 1)
                            else:
                                ins.then_inc(s_tap, 1)
                        if n == 1:
                            dve.wait_ge(s_rt, m * B + (b + 1))
                            nc.vector.tensor_scalar(sq[:], sq[:], NORM_EPS, None, ALU.max).then_inc(s_r, 1)
                            dve.wait_ge(s_r, m * (8 * B) + (8 * b + 5))
                            nc.vector.reciprocal(sq[:], sq[:]).then_inc(s_r, 1)
                            dve.wait_ge(s_r, m * (8 * B) + (8 * b + 6))
                            nc.vector.tensor_tensor(res[:, 1, :], res[:, 1, :], sq[:], ALU.mult).then_inc(s_k, 1)
                dve.wait_ge(s_tap, 1 + m * (3 * B) + 3 * B)
                dve.wait_ge(s_k, 1 + m * B + B)
                nc.vector.memset(raw[:, 0:4], 0.0).then_inc(s_z, 1)

        @block.tensor
        def _(pe):
            pe.sem_inc(s_tap, 1)
            pe.sem_inc(s_silu, 1)
            pe.sem_inc(s_st, 1)
            pe.sem_inc(s_k, 1)
            pe.sem_inc(s_raw, 1)
            pe.sem_inc(s_tick, 1)
            with pe.Fori(0, M) as m:
                pe.wait_ge(s_w, m * 32 + 32)
                for b in range(B):
                    for n in range(3):
                        u = 3 * b + n
                        if u < 2:
                            pe.wait_ge(s_raw, 1 + m * (6 * B))
                        else:
                            pe.wait_ge(s_raw, 1 + m * (6 * B) + 2 * (u - 1))
                        for g in range(GH):
                            for dc in range(DC):
                                last = nc.tensor.matmul(pp[:, u % 2, g * G:(g + 1) * G], w[:, 0, n, dc, :],
                                                        hT[:, dc, b * T + g * G:b * T + (g + 1) * G],
                                                        start=(dc == 0), stop=(dc == DC - 1))
                        last.then_inc(s_p, 1)
                    pe.wait_ge(s_sq, m * B + (b + 1))
                    if b:
                        pe.wait_ge(s_rt, m * B + b)
                    for g in range(GH):
                        last = nc.tensor.matmul(pn[:, g * G:(g + 1) * G], ones2[:], sq[:, g * G:(g + 1) * G],
                                                start=True, stop=True)
                    last.then_inc(s_nn, 1)


def scan(nc, sem, ones2, qkv_s, ab_s, y_s):
    TB, HI = 64, DH // 2
    NBK = T // TB
    s_tick, s_st = sem("s_tick"), sem("s_block_stored")
    s_ab, s_in, s_d, s_y, s_o = sem("s_ab"), sem("s_in"), sem("s_step"), sem("s_y"), sem("s_out")
    with ExitStack() as st:
        al = st.enter_context(nc.sbuf_tensor("alpha", [P, T], F32))
        be = st.enter_context(nc.sbuf_tensor("beta", [P, T], F32))
        S = st.enter_context(nc.sbuf_tensor("state", [P, HI, DH], F32))
        W = st.enter_context(nc.sbuf_tensor("outer", [P, HI, DH], F32))
        r = st.enter_context(nc.sbuf_tensor("seen", [P, HI], F32))
        u = st.enter_context(nc.sbuf_tensor("update", [P, HI], F32))
        qb = st.enter_context(nc.sbuf_tensor("q_blk", [P, DH, TB], F32))
        kb = st.enter_context(nc.sbuf_tensor("k_blk", [P, DH, TB], F32))
        vb = st.enter_context(nc.sbuf_tensor("v_blk", [P, HI, TB], F32))
        yb = st.enter_context(nc.sbuf_tensor("y_blk", [P, HI, TB], F32))
        tick2 = st.enter_context(nc.sbuf_tensor("s_tick2", [P, 8], F32))
        tick = st.enter_context(nc.sbuf_tensor("s_tick", [P, 8], F32))
        block = st.enter_context(nc.Block())
        NS = 9

        @block.gpsimd
        def _(pool):
            for half in range(2):
                rows = slice(half * 64, half * 64 + 64)
                for b in range(B):
                    pr = slice(half * 64 + b * H, half * 64 + (b + 1) * H)
                    pool.dma_start(al[pr, :], ab_s[0:H, b, :]).then_inc(s_ab, 16)
                    pool.dma_start(be[pr, :], ab_s[H:2 * H, b, :]).then_inc(s_ab, 16)

            with pool.Fori(0, NBK) as n:
                pool.wait_ge(s_y, 1 + n)
                pool.wait_ge(s_tick, 1 + n * 3)
                nc.gpsimd.tensor_tensor(tick[:], ones2[:, 0:8], ones2[:, 0:8], ALU.add).then_inc(s_tick, 1)
                for half in range(2):
                    for b in range(B):
                        pr = slice(half * 64 + b * H, half * 64 + (b + 1) * H)
                        for dst, i in ((qb, 0), (kb, 1)):
                            pool.dma_start(dst[pr], qkv_s[i, b].rearrange("m (a j) t -> (m a) j t", a=2)
                                         [:, :, bass.ds(n * TB, TB)]).then_inc(s_in, 16)
                        pool.dma_start(vb[pr], qkv_s[2, b].rearrange("m (a j) t -> (m a) j t", a=2)
                                     [:, half * HI:(half + 1) * HI, bass.ds(n * TB, TB)]).then_inc(s_in, 16)
                pool.wait_ge(s_y, 1 + n + 1)
                pool.wait_ge(s_tick, 1 + n * 3 + 1)
                nc.gpsimd.tensor_tensor(tick[:], ones2[:, 0:8], ones2[:, 0:8], ALU.add).then_inc(s_tick, 1)
                for half in range(2):
                    for b in range(B):
                        pr = slice(half * 64 + b * H, half * 64 + (b + 1) * H)
                        pool.dma_start(y_s[b].rearrange("m (a j) t -> (m a) j t", a=2)
                                     [:, half * HI:(half + 1) * HI, bass.ds(n * TB, TB)], yb[pr]).then_inc(s_o, 16)
                pool.wait_ge(s_o, n * 128 + 128)
                pool.wait_ge(s_tick, 1 + n * 3 + 2)
                nc.gpsimd.tensor_tensor(tick[:], ones2[:, 0:8], ones2[:, 0:8], ALU.add).then_inc(s_tick, 1)
                pool.wait_ge(s_tick, 1 + n * 3 + 3)
                nc.gpsimd.tensor_tensor(tick2[:], ones2[:, 0:8], ones2[:, 0:8], ALU.add).then_inc(s_st, 1)

        @block.vector
        def _(dve):
            dve.sem_inc(s_y, 1)
            dve.sem_inc(s_st, 1)
            dve.sem_inc(s_tick, 1)
            nc.vector.memset(S[:], 0.0).then_inc(s_d, 1)
            dve.wait_ge(s_ab, 16 * 16)
            with dve.Fori(0, NBK) as n:
                dve.wait_ge(s_in, n * (24 * 16) + 24 * 16)
                dve.wait_ge(s_st, 1 + n)
                nc.vector.memset(r[:], 0.0)
                with dve.Fori(0, TB) as t:
                    tok = n * TB + t
                    base = (n * TB + t) * NS + 1
                    k_row = kb[:, :, bass.ds(t, 1)].rearrange("p j a -> p a j").broadcast_to([P, HI, DH])
                    q_row = qb[:, :, bass.ds(t, 1)].rearrange("p j a -> p a j").broadcast_to([P, HI, DH])
                    u_col = u[:, :].rearrange("p (i a) -> p i a", a=1).broadcast_to([P, HI, DH])
                    dve.wait_ge(s_d, base)
                    nc.vector.tensor_tensor(W[:], S[:], k_row, ALU.mult).then_inc(s_d, 1)
                    dve.wait_ge(s_d, base + 1)
                    nc.vector.tensor_reduce(r[:], W[:], AX_X, ALU.add).then_inc(s_d, 1)
                    dve.wait_ge(s_d, base + 2)
                    nc.vector.scalar_tensor_tensor(out=u[:], in0=r[:], scalar=al[:, bass.ds(tok, 1)],
                                                   in1=vb[:, :, bass.ds(t, 1)].rearrange("p i a -> p (i a)"),
                                                   op0=ALU.mult, op1=ALU.subtract).then_inc(s_d, 1)
                    dve.wait_ge(s_d, base + 3)
                    nc.vector.tensor_scalar(u[:], u[:], be[:, bass.ds(tok, 1)], -1.0, ALU.mult,
                                            ALU.mult).then_inc(s_d, 1)
                    dve.wait_ge(s_d, base + 4)
                    nc.vector.tensor_tensor(W[:], u_col, k_row, ALU.mult).then_inc(s_d, 1)
                    dve.wait_ge(s_d, base + 5)
                    nc.vector.scalar_tensor_tensor(out=S[:].rearrange("p i j -> p (i j)"),
                                                   in0=S[:].rearrange("p i j -> p (i j)"),
                                                   scalar=al[:, bass.ds(tok, 1)],
                                                   in1=W[:].rearrange("p i j -> p (i j)"), op0=ALU.mult,
                                                   op1=ALU.add).then_inc(s_d, 1)
                    dve.wait_ge(s_d, base + 6)
                    nc.vector.tensor_scalar(S[:], S[:], CLIP, -CLIP, ALU.min, ALU.max).then_inc(s_d, 1)
                    dve.wait_ge(s_d, base + 7)
                    nc.vector.tensor_tensor(W[:], S[:], q_row, ALU.mult).then_inc(s_d, 1)
                    dve.wait_ge(s_d, base + 8)
                    nc.vector.tensor_reduce(yb[:, :, bass.ds(t, 1)].rearrange("p i a -> p (i a)"), W[:], AX_X,
                                            ALU.add).then_inc(s_d, 1)
                dve.wait_ge(s_d, n * (TB * NS) + (TB * NS + 1))
                nc.vector.tensor_copy(r[:], u[:]).then_inc(s_y, 1)


def attn_out(nc, sem, x, y_s, wg, bg, wo, gates_s, hT, gates, x1):
    s_y = [sem("o_y_even"), sem("o_y_odd")]
    s_w, s_gp, s_g = sem("o_weights"), sem("o_gate_product"), sem("o_gate")
    s_m, s_op, s_t, s_x1 = sem("o_gated"), sem("o_product"), sem("o_scaled"), sem("o_x1")
    with ExitStack() as st:
        wg_sb = st.enter_context(nc.sbuf_tensor("wg_sb", [P, DC, C], F32))
        bg_sb = st.enter_context(nc.sbuf_tensor("bg_sb", [P, M], F32))
        wo_sb = st.enter_context(nc.sbuf_tensor("wo_sb", [P, M, D], F32))
        y = st.enter_context(nc.sbuf_tensor("y", [P, 2, M, G], F32))
        g_sb = st.enter_context(nc.sbuf_tensor("g_sb", [P, 2, G], F32))
        tmp = st.enter_context(nc.sbuf_tensor("o_tmp", [P, 2, D], F32))
        pg = st.enter_context(nc.psum_tensor("o_pg", [P, 2, G], F32))
        po = st.enter_context(nc.psum_tensor("o_po", [P, 2, G], F32))
        block = st.enter_context(nc.Block())
        NG = B * GH

        @block.sync
        def _(sp):
            sp.dma_start(wg_sb[:], wg).then_inc(s_w, 16)
            sp.dma_start(bg_sb[:], bg).then_inc(s_w, 16)
            sp.dma_start(wo_sb[:], wo).then_inc(s_w, 16)
            sp.dma_start(x1[:], x).then_inc(s_w, 16)
            sp.dma_start(gates[:].rearrange("p a b d -> p (a b d)"),
                         gates_s.broadcast_to([P, 2 * B * D])).then_inc(s_w, 16)
            for g in range(NG):
                if g >= 2:
                    sp.wait_ge(s_op, GT * (g - 1))
                sp.dma_start(y[:, g % 2], y_s[g // GH].rearrange("m p t -> p m t")
                             [:, :, (g % GH) * G:(g % GH + 1) * G]).then_inc(s_y[g % 2], 16)

        @block.scalar
        def _(act):
            act.wait_ge(s_w, 80)
            for i in range(NG * M):
                act.wait_ge(s_gp, i + 1)
                if i >= 2:
                    act.wait_ge(s_m, i - 1)
                nc.scalar.activation(g_sb[:, i % 2, :], pg[:, i % 2, :], ACT.Silu,
                                     bias=bg_sb[:, i % M:i % M + 1]).then_inc(s_g, 1)

        @block.vector
        def _(dve):
            dve.wait_ge(s_w, 80)
            for g in range(NG):
                dve.wait_ge(s_y[g % 2], 16 * (g // 2 + 1))
                for m in range(M):
                    i = g * M + m
                    dve.wait_ge(s_g, i + 1)
                    nc.vector.tensor_tensor(y[:, g % 2, m, :], y[:, g % 2, m, :], g_sb[:, i % 2, :],
                                            ALU.mult).then_inc(s_m, 1)
                for j in range(GT):
                    i = g * GT + j
                    dve.wait_ge(s_op, i + 1)
                    if i >= 2:
                        dve.wait_ge(s_x1, i - 1)
                    nc.vector.tensor_tensor(tmp[:, i % 2, :], po[:, i % 2, 0:D], gates[:, 0, g // GH, :],
                                            ALU.mult).then_inc(s_t, 1)
                    dve.wait_ge(s_t, i + 1)
                    nc.vector.tensor_tensor(x1[:, i, :], x1[:, i, :], tmp[:, i % 2, :], ALU.add).then_inc(s_x1, 1)
            dve.wait_ge(s_x1, NG * GT)

        @block.tensor
        def _(pe):
            pe.wait_ge(s_w, 80)
            for g in range(NG):
                for m in range(M):
                    i = g * M + m
                    if i >= 2:
                        pe.wait_ge(s_g, i - 1)
                    for dc in range(DC):
                        last = nc.tensor.matmul(pg[:, i % 2, :], wg_sb[:, dc, m * P:(m + 1) * P],
                                                hT[:, dc, g * G:(g + 1) * G], start=(dc == 0), stop=(dc == DC - 1))
                    last.then_inc(s_gp, 1)
                pe.wait_ge(s_m, M * (g + 1))
                for j in range(GT):
                    i = g * GT + j
                    if i >= 2:
                        pe.wait_ge(s_t, i - 1)
                    for m in range(M):
                        last = nc.tensor.matmul(po[:, i % 2, 0:D], y[:, g % 2, m, j * P:(j + 1) * P], wo_sb[:, m, :],
                                                start=(m == 0), stop=(m == M - 1))
                    last.then_inc(s_op, 1)


def norm_second(nc, sem, ident, modT, rw_sb, b2, x1, h2T, comb, acc):
    N = B * NT
    s_b, s_st, s_ag, s_sq = sem("n_loaded"), sem("n_stats"), sem("n_moments"), sem("n_root")
    s_n, s_t, s_e, s_l = sem("n_normed"), sem("n_turned"), sem("n_kept"), sem("n_logits")
    s_v, s_x, s_c, s_cc = sem("n_vector"), sem("n_exp"), sem("n_comb_turned"), sem("n_comb_kept")
    s_b2, s_a = sem("n_bias"), sem("n_acc")
    with ExitStack() as st:
        stats = st.enter_context(nc.sbuf_tensor("stats2", [P, N, 6], F32))
        mv = st.enter_context(nc.sbuf_tensor("mv2", [P, N, 2], F32))
        eps = st.enter_context(nc.sbuf_tensor("eps2", [P, 1], F32))
        sd = st.enter_context(nc.sbuf_tensor("sd2", [P, N], F32))
        rstd = st.enter_context(nc.sbuf_tensor("rstd2", [P, N], F32))
        b2_sb = st.enter_context(nc.sbuf_tensor("b2_sb", [E, D], F32))
        lg = st.enter_context(nc.sbuf_tensor("logits", [P, N, E], F32))
        rank = st.enter_context(nc.sbuf_tensor("rank", [P, N, E], F32))
        hit = st.enter_context(nc.sbuf_tensor("hit", [P, N, E], F32))
        one1 = st.enter_context(nc.sbuf_tensor("first", [P, N, E], F32))
        one2 = st.enter_context(nc.sbuf_tensor("second", [P, N, E], F32))
        best = st.enter_context(nc.sbuf_tensor("best", [P, 2, N], F32))
        pos = st.enter_context(nc.sbuf_tensor("pos", [P, N], F32))
        ex = st.enter_context(nc.sbuf_tensor("ex", [P, 4, N], F32))
        combT = st.enter_context(nc.sbuf_tensor("combT", [E, N * P], F32))
        pt = st.enter_context(nc.psum_tensor("pt2", [P, 2, DC, G], F32))
        pl = st.enter_context(nc.psum_tensor("pl2", [P, N, E], F32))
        block = st.enter_context(nc.Block())
        NG = B * GH

        def wide(ap):
            return ap.rearrange("p (n a) -> p n a", a=1).broadcast_to([P, N, E])

        @block.sync
        def _(sp):
            sp.dma_start(b2_sb[:], b2).then_inc(s_b, 16)

        @block.scalar
        def _(act):
            act.wait_ge(s_ag, N + 1)
            nc.scalar.activation(sd[:], mv[:, :, 1], ACT.Sqrt, bias=eps[:, 0:1]).then_inc(s_sq, 1)
            act.wait_ge(s_v, E + 11)
            nc.scalar.activation(ex[:, 1, :], ex[:, 0, :], ACT.Exp).then_inc(s_x, 1)

        @block.vector
        def _(dve):
            nc.vector.memset(eps[:], LN_EPS).then_inc(s_ag, 1)
            for i in range(N):
                nc.vector.bn_stats(stats[:, i, :], x1[:, i, :]).then_inc(s_st, 1)
            dve.wait_ge(s_st, N)
            for i in range(N):
                nc.vector.bn_aggr(mv[:, i, :], stats[:, i, :]).then_inc(s_ag, 1)
            dve.wait_ge(s_sq, 1)
            v = 0

            def step(ins):
                nonlocal v
                v += 1
                ins.then_inc(s_v, 1)
                dve.wait_ge(s_v, v)

            step(nc.vector.reciprocal(rstd[:], sd[:]))
            for i in range(N):
                nc.vector.tensor_scalar(acc[:, i, :], x1[:, i, :], mv[:, i, 0:1],
                                        rstd[:, i:i + 1], ALU.subtract, ALU.mult).then_inc(s_n, 1)
            for g in range(NG):
                dve.wait_ge(s_t, g + 1)
                b = g // GH
                for dc in range(DC):
                    nc.vector.tensor_scalar(h2T[:, dc, g * G:(g + 1) * G], pt[:, g % 2, dc, :],
                                            modT[:, 2 * CB + dc, b:b + 1], modT[:, 2 * SB + dc, b:b + 1],
                                            ALU.mult, ALU.add).then_inc(s_e, 1)
            for e in range(E):
                step(nc.vector.memset(rank[:, :, e], float(E - e)))
            dve.wait_ge(s_l, 1)
            step(nc.vector.tensor_copy(lg[:], pl[:]))
            for n, (one, m) in enumerate(((one1, best[:, 0, :]), (one2, best[:, 1, :]))):
                step(nc.vector.tensor_reduce(m, lg[:], AX_X, ALU.max))
                if n == 1:
                    step(nc.vector.tensor_tensor(ex[:, 0, :], best[:, 1, :], best[:, 0, :], ALU.subtract))
                step(nc.vector.tensor_tensor(hit[:], lg[:], wide(m), ALU.is_equal))
                step(nc.vector.tensor_tensor(hit[:], hit[:], rank[:], ALU.mult))
                step(nc.vector.tensor_reduce(pos[:], hit[:], AX_X, ALU.max))
                step(nc.vector.tensor_tensor(one[:], hit[:], wide(pos[:]), ALU.is_equal))
                if n == 0:
                    step(nc.vector.tensor_scalar(hit[:], one[:], -3.0e38, None, ALU.mult))
                    step(nc.vector.tensor_tensor(lg[:], lg[:], hit[:], ALU.add))
            dve.wait_ge(s_x, 1)
            step(nc.vector.tensor_scalar(ex[:, 2, :], ex[:, 1, :], 1.0, None, ALU.add))
            step(nc.vector.reciprocal(ex[:, 3, :], ex[:, 2, :]))
            step(nc.vector.tensor_tensor(ex[:, 2, :], ex[:, 1, :], ex[:, 3, :], ALU.mult))
            step(nc.vector.tensor_tensor(one1[:], one1[:], wide(ex[:, 3, :]), ALU.mult))
            step(nc.vector.tensor_tensor(one2[:], one2[:], wide(ex[:, 2, :]), ALU.mult))
            nc.vector.tensor_tensor(comb[:], one1[:], one2[:], ALU.add).then_inc(s_a, 1)
            dve.wait_ge(s_a, 1)
            for g in range(NG):
                dve.wait_ge(s_c, g + 1)
                nc.vector.tensor_copy(combT[:, g * G:(g + 1) * G], pt[0:E, g % 2, 0, :]).then_inc(s_cc, 1)
            for g in range(N // 2):
                dve.wait_ge(s_b2, g + 1)
                nc.vector.tensor_copy(acc[:, 2 * g:2 * g + 2, :],
                                      pt[:, g % 2, 1, :].rearrange("p (j d) -> p j d", j=2)).then_inc(s_a, 1)
            dve.wait_ge(s_a, 1 + N // 2)

        @block.tensor
        def _(pe):
            for g in range(NG):
                pe.wait_ge(s_n, (g + 1) * GT)
                if g >= 2:
                    pe.wait_ge(s_e, DC * (g - 1))
                for j in range(GT):
                    for dc in range(DC):
                        last = nc.tensor.transpose(pt[:, g % 2, dc, j * P:(j + 1) * P],
                                                   acc[:, g * GT + j, dc * P:(dc + 1) * P], ident[:])
                last.then_inc(s_t, 1)
            for g in range(NG):
                pe.wait_ge(s_e, DC * (g + 1))
                for j in range(g * GT, (g + 1) * GT):
                    for dc in range(DC):
                        last = nc.tensor.matmul(pl[:, j, :], h2T[:, dc, j * P:(j + 1) * P], rw_sb[:, dc, :],
                                                start=(dc == 0), stop=(dc == DC - 1))
            last.then_inc(s_l, 1)
            pe.wait_ge(s_a, 1)
            for g in range(NG):
                if g >= 2:
                    pe.wait_ge(s_cc, g - 1)
                for j in range(GT):
                    last = nc.tensor.transpose(pt[0:E, g % 2, 0, j * P:(j + 1) * P], comb[:, g * GT + j, :], ident[:])
                last.then_inc(s_c, 1)
            pe.wait_ge(s_b, 16)
            for g in range(N // 2):
                pe.wait_ge(s_cc, g // 2 + 1)
                if g >= 2:
                    pe.wait_ge(s_a, g)
                for j in range(2):
                    last = nc.tensor.matmul(pt[:, g % 2, 1, j * D:(j + 1) * D],
                                            combT[:, (2 * g + j) * P:(2 * g + j + 1) * P], b2_sb[:],
                                            start=True, stop=True)
                last.then_inc(s_b2, 1)


def experts(nc, sem, w1, b1, w2, h2T, comb, acc):
    s_w = [sem("e_weights_even"), sem("e_weights_odd")]
    s_h, s_g, s_y, s_a = sem("e_up"), sem("e_gelu"), sem("e_down"), sem("e_acc")
    with ExitStack() as st:
        w1_sb = st.enter_context(nc.sbuf_tensor("w1_sb", [P, 2, DC, F], F32))
        w2_sb = st.enter_context(nc.sbuf_tensor("w2_sb", [P, 2, FC, D], F32))
        b1_sb = st.enter_context(nc.sbuf_tensor("b1_sb", [P, 2, FC], F32))
        hm = st.enter_context(nc.sbuf_tensor("hm", [P, 2, FC, G], F32))
        ph = st.enter_context(nc.psum_tensor("ph", [P, 4, G], F32))
        py = st.enter_context(nc.psum_tensor("py", [P, 4, G], F32))
        block = st.enter_context(nc.Block())
        NG = B * GH

        @block.sync
        def _(sp):
            for e in range(E):
                if e >= 2:
                    sp.wait_ge(s_y, 1 + (e - 1) * NG * GT)
                sp.dma_start(w1_sb[:, e % 2], w1[e]).then_inc(s_w[e % 2], 16)
                sp.dma_start(w2_sb[:, e % 2], w2[e]).then_inc(s_w[e % 2], 16)
                sp.dma_start(b1_sb[:, e % 2], b1[e]).then_inc(s_w[e % 2], 16)

        @block.scalar
        def _(act):
            with act.Fori(0, E // 2) as e2:
                for p in range(2):
                    act.wait_ge(s_w[p], e2 * 48 + 48)
                    for g in range(NG):
                        i = p * NG + g
                        if i >= 2:
                            act.wait_ge(s_y, 1 + e2 * (2 * NG * GT) + (i - 1) * GT)
                        else:
                            act.wait_ge(s_y, 1 + e2 * (2 * NG * GT) + 0)
                        for f in range(FC):
                            act.wait_ge(s_h, e2 * (2 * NG * FC) + (i * FC + f + 1))
                            nc.scalar.activation(hm[:, i % 2, f, :], ph[:, f % 4, :], ACT.Gelu,
                                                 bias=b1_sb[:, p, f:f + 1]).then_inc(s_g, 1)

        @block.vector
        def _(dve):
            with dve.Fori(0, E // 2) as e2:
                for p in range(2):
                    for g in range(NG):
                        i = p * NG + g
                        for j in range(GT):
                            dve.wait_ge(s_y, 1 + e2 * (2 * NG * GT) + (i * GT + j + 1))
                            if g == 0 and j == 0:
                                dve.wait_ge(s_a, 1 + e2 * (2 * NG * GT) + i * GT)
                            nc.vector.scalar_tensor_tensor(
                                out=acc[:, g * GT + j, :], in0=py[:, j, 0:D],
                                scalar=comb[:, g * GT + j, bass.ds(e2 * 2 + p, 1)], in1=acc[:, g * GT + j, :],
                                op0=ALU.mult, op1=ALU.add).then_inc(s_a, 1)
            dve.wait_ge(s_a, 1 + E * NG * GT)

        @block.tensor
        def _(pe):
            pe.sem_inc(s_y, 1)
            pe.sem_inc(s_a, 1)
            pe.sem_inc(s_g, 1)
            def up(e2, i, p, g):
                if g == 0:
                    pe.wait_ge(s_w[p], e2 * 48 + 48)
                for f in range(FC):
                    pe.wait_ge(s_g, 1 + e2 * (2 * NG * FC) + max((i - 1) * FC + f + 1, 0))
                    for dc in range(DC):
                        last = nc.tensor.matmul(ph[:, f, :], w1_sb[:, p, dc, f * P:(f + 1) * P],
                                                h2T[:, dc, g * G:(g + 1) * G], start=(dc == 0), stop=(dc == DC - 1))
                    last.then_inc(s_h, 1)

            def down(e2, i, p, g):
                pe.wait_ge(s_g, 1 + e2 * (2 * NG * FC) + (i + 1) * FC)
                for j in range(GT):
                    pe.wait_ge(s_a, 1 + e2 * (2 * NG * GT) + max((i - 1) * GT + j + 1, 0))
                    for f in range(FC):
                        last = nc.tensor.matmul(py[:, j, 0:D], hm[:, i % 2, f, j * P:(j + 1) * P], w2_sb[:, p, f, :],
                                                start=(f == 0), stop=(f == FC - 1))
                    last.then_inc(s_y, 1)

            with pe.Fori(0, E // 2) as e2:
                for i in range(2 * NG + 1):
                    if i < 2 * NG:
                        up(e2, i, i // NG, i % NG)
                    if i >= 1:
                        down(e2, i - 1, (i - 1) // NG, (i - 1) % NG)


def finish(nc, sem, gates, x1, acc, out):
    s_m, s_a, s_o = sem("f_scaled"), sem("f_sum"), sem("f_stored")
    with ExitStack() as st:
        block = st.enter_context(nc.Block())

        @block.sync
        def _(sp):
            for b in range(B):
                sp.wait_ge(s_a, (b + 1) * NT)
                sp.dma_start(out[:, b * NT:(b + 1) * NT, :], acc[:, b * NT:(b + 1) * NT, :]).then_inc(s_o, 16)
            sp.wait_ge(s_o, 16 * B)

        @block.vector
        def _(dve):
            for i in range(B * NT):
                nc.vector.tensor_tensor(acc[:, i, :], acc[:, i, :], gates[:, 1, i // NT, :], ALU.mult).then_inc(s_m, 1)
            for i in range(B * NT):
                dve.wait_ge(s_m, i + 1)
                nc.vector.tensor_tensor(acc[:, i, :], acc[:, i, :], x1[:, i, :], ALU.add).then_inc(s_a, 1)


def kernel(**inputs):
    import numpy as np
    import concourse.bacc as bacc
    from concourse.bass_utils import run_bass_kernel_spmd

    a = {k[3:]: np.asarray(v) for k, v in inputs.items()}

    def cols(w):
        return w.T.reshape(w.shape[1] // P, P, w.shape[0]).transpose(1, 0, 2)

    wqkv = np.stack([cols(a["attn_W" + n]).reshape(P, DC, M, P) for n in "qkv"])
    convp = np.stack([np.concatenate([a[f"attn_conv_{n}_w"].reshape(C, 4), a[f"attn_conv_{n}_b"].reshape(C, 1)], 1)
                      .reshape(M, P, 5) for n in "qkv"])
    ident = np.eye(P, dtype=np.float32)
    ones2 = np.kron(np.eye(2, dtype=np.float32), np.ones((DH, DH), np.float32))
    r, c = np.arange(P)[:, None], np.arange(P)[None, :]
    same64, same32 = r // CH == c // CH, r // HB == c // HB
    tri = np.stack([same64 & (r <= c), same32 & (r <= c), same64 & (r > c), (r // CH == 0) & (c >= 0),
                    (r // CH == 1) & (c >= 0)], 1).astype(np.float32)
    c32, c64 = np.arange(HB)[None, :], np.arange(CH)[None, :]
    mask = np.concatenate([r % HB > c32, (r % HB > c32) | (r // HB % 2 == 1), r % CH <= c64], 1).astype(np.float32)
    tiles = lambda z: z.reshape(B * NT, P, D).transpose(1, 0, 2)
    arrays = {
        "x": tiles(a["attn_hidden_states"]),
        "cT": a["c"].T.reshape(DC, P, B).transpose(1, 0, 2),
        "wmod": a["wmod"].reshape(DC, P, 6 * D).transpose(1, 0, 2),
        "wqkv": wqkv.transpose(3, 1, 0, 2, 4),
        "convp": convp.transpose(1, 2, 0, 3),
        "wg": cols(a["attn_Wg"]),
        "bg": a["attn_bg"].reshape(M, P).T,
        "wab": cols(np.concatenate([a["attn_Wa"], a["attn_Wb"]], 0)),
        "bab": np.concatenate([a["attn_ba"], a["attn_bb"]]).reshape(2 * H, 1),
        "wo": cols(a["attn_Wo"]),
        "rw": cols(a["ffn_router_w"]),
        "w1": np.stack([cols(w) for w in a["ffn_w1"]]),
        "b1": a["ffn_b1"].reshape(E, FC, P).transpose(0, 2, 1),
        "w2": np.stack([cols(w) for w in a["ffn_w2"]]),
        "b2": a["ffn_b2"],
        "ident": ident,
        "ones2": ones2,
        "tri": tri,
        "mask": mask,
        "babr": np.concatenate([a["attn_ba"], a["attn_bb"]]).reshape(1, 2 * H),
    }
    nc = bacc.Bacc("TRN2", target_bir_lowering=False, num_devices=1)
    feeds, args = {}, []
    for name, v in arrays.items():
        v = np.ascontiguousarray(v)
        feeds[name + "_in"] = v
        args.append(nc.dram_tensor(name + "_in", v.shape, F32, kind="ExternalInput").ap())
    args.append(nc.dram_tensor("out_0", (P, B * NT, D), F32, kind="ExternalOutput").ap())
    args.append(nc.dram_tensor("qkv_scratch", (3, B, M, P, T), F32, kind="Internal").ap())
    args.append(nc.dram_tensor("ab_scratch", (2 * H, B, T), F32, kind="Internal").ap())
    args.append(nc.dram_tensor("y_scratch", (B, M, P, T), F32, kind="Internal").ap())
    args.append(nc.dram_tensor("gates_scratch", (1, 2 * B * D), F32, kind="Internal").ap())
    adaln_delta_moe(nc, *args)
    r = run_bass_kernel_spmd(nc, [feeds], core_ids=[0])
    got = np.asarray(r.results[0]["out_0"]).reshape(P, B * NT, D)
    return got.transpose(1, 0, 2).reshape(B, T, D)
```

```python
from contextlib import ExitStack

import concourse.bass as bass
from concourse import mybir

ALU = mybir.AluOpType
ACT = mybir.ActivationFunctionType
F32 = mybir.dt.float32
F32R = mybir.dt.float32r
AX_X = mybir.AxisListType.X

P = 128
B, T, D = 4, 1024, 256
H, DH = 16, 64
C = H * DH
E, F = 8, 512
DC = D // P
M = C // P
FC = F // P
NT = T // P
G = 512
GH = T // G
GT = G // P
CLIP = 5.0
LN_EPS = 1e-5
NORM_EPS = 1e-12
SA, CA, GA, SB, CB, GB = range(6)


def adaln_delta_moe(nc, x, cT, wmod, wqkv, convp, wg, bg, wab, bab, wo, rw, w1, b1, w2, b2,
                    ident_d, ones2_d, tri_d, mask_d, out, qkv_s, ab_s, y_s, gates_s):
    with ExitStack() as top:
        def sb_in(stack):
            return lambda name, shape: stack.enter_context(nc.sbuf_tensor(name, shape, F32))

        def ps_in(stack):
            return lambda name, shape: stack.enter_context(nc.psum_tensor(name, shape, F32))

        def sem(name):
            return top.enter_context(nc.semaphore(name))

        sb = sb_in(top)
        ident = sb("ident", [P, P])
        ones2 = sb("ones2", [P, P])
        modT = sb("modT", [P, 12, B])
        rw_sb = sb("rw_sb", [P, DC, E])

        modulation(nc, sem, cT, wmod, rw, ident_d, ones2_d, ident, ones2, modT, gates_s, rw_sb)

        hT = sb("hT", [P, DC, B * T])
        norm_first(nc, sem, x, ident, modT, hT)
        fmax = sb("fmax", [P, 1])
        flag = top.enter_context(nc.sbuf_tensor("flag", [P, 1], mybir.dt.int32))
        with ExitStack() as st:
            la, bt = sb_in(st)("log_alpha", [P, B * NT, H + 2]), sb_in(st)("beta_tok", [P, B * NT, H + 2])
            gate_scalars(nc, sem, wab, bab, ident, hT, la, bt, ab_s)
            delta_fast(nc, sem, ident, wqkv, convp, tri_d, mask_d, hT, la, bt, ab_s, y_s, fmax)
        judge(nc, sem, fmax, flag)
        clipped = nc.values_load(flag[0:1, 0:1], min_val=0, max_val=1)
        with nc.If(clipped > 0):
            project(nc, sem, wqkv, convp, ones2, hT, qkv_s)
            scan(nc, sem, ones2, qkv_s, ab_s, y_s)
        x1 = sb("x1", [P, B * NT, D])
        gates = sb("gates", [P, 2, B, D])
        h2T = hT
        attn_out(nc, sem, x, y_s, wg, bg, wo, gates_s, ident, modT, hT, gates, x1, h2T)
        comb = sb("comb", [P, B * NT, E])
        acc = sb("acc", [P, B * NT, D])
        route(nc, sem, ident, rw_sb, b2, h2T, comb, acc)
        experts(nc, sem, w1, b1, w2, h2T, comb, acc)
        finish(nc, sem, gates, x1, acc, out)


def modulation(nc, sem, cT, wmod, rw, ident_d, ones2_d, ident, ones2, modT, gates_s, rw_sb):
    s_load, s_silu, s_bc = sem("mod_loaded"), sem("mod_silu"), sem("mod_spread")
    s_col, s_row, s_v, s_o = sem("mod_columns"), sem("mod_rows"), sem("mod_vector"), sem("mod_stored")
    with ExitStack() as st:
        gates = st.enter_context(nc.sbuf_tensor("gates_made", [P, 2 * B * D], F32))
        c_sb = st.enter_context(nc.sbuf_tensor("c_sb", [P, DC, B], F32))
        sc = st.enter_context(nc.sbuf_tensor("silu_c", [P, DC, B], F32))
        scb = st.enter_context(nc.sbuf_tensor("silu_c_spread", [P, DC, B, P], F32))
        wm = st.enter_context(nc.sbuf_tensor("wmod_sb", [P, DC, 6 * D], F32))
        absg = st.enter_context(nc.sbuf_tensor("gate_size", [P, 2 * B * D], F32))
        sgn = st.enter_context(nc.sbuf_tensor("gate_sign", [P, 2 * B * D], F32))
        raw = st.enter_context(nc.sbuf_tensor("gate_raw", [P, 2 * B * D], F32))
        ones = st.enter_context(nc.sbuf_tensor("ones_row", [P, P], F32))
        pm = st.enter_context(nc.psum_tensor("pm", [P, 12, B], F32))
        pg = st.enter_context(nc.psum_tensor("pg", [P, 2 * B, D], F32))
        block = st.enter_context(nc.Block())

        @block.sync
        def _(sp):
            sp.dma_start(c_sb[:], cT).then_inc(s_load, 16)
            sp.dma_start(wm[:], wmod).then_inc(s_load, 16)
            sp.dma_start(ident[:], ident_d).then_inc(s_load, 16)
            sp.dma_start(ones2[:], ones2_d).then_inc(s_load, 16)
            sp.dma_start(rw_sb[:], rw).then_inc(s_load, 16)
            sp.wait_ge(s_load, 80)
            sp.wait_ge(s_v, 11)
            sp.dma_start(gates_s, gates[0:1, :]).then_inc(s_o, 16)
            sp.wait_ge(s_o, 16)

        @block.scalar
        def _(act):
            act.wait_ge(s_load, 80)
            nc.scalar.activation(sc[:], c_sb[:], ACT.Silu).then_inc(s_silu, 1)

        @block.vector
        def _(dve):
            nc.vector.memset(ones[:], 1.0).then_inc(s_v, 1)
            dve.wait_ge(s_v, 1)
            dve.wait_ge(s_silu, 1)
            for dc in range(DC):
                for b in range(B):
                    last = nc.vector.tensor_scalar(scb[:, dc, b, :], ones[:], sc[:, dc, b:b + 1], None, ALU.mult)
            last.then_inc(s_bc, 1)
            dve.wait_ge(s_col, 1)
            nc.vector.tensor_copy(modT[:], pm[:]).then_inc(s_v, 1)
            dve.wait_ge(s_v, 2)
            for part in (CA, CB):
                nc.vector.tensor_scalar(modT[:, 2 * part:2 * part + 2, :], modT[:, 2 * part:2 * part + 2, :], 1.0, None,
                                        ALU.add).then_inc(s_v, 1)
            dve.wait_ge(s_row, 1)
            nc.vector.tensor_copy(raw[:], pg[:].rearrange("p a d -> p (a d)")).then_inc(s_v, 1)
            dve.wait_ge(s_v, 5)
            nc.vector.tensor_scalar(sgn[:], raw[:], 0.0, 2.0, ALU.is_ge, ALU.mult).then_inc(s_v, 1)
            nc.vector.tensor_scalar(absg[:], raw[:], -1.0, None, ALU.mult).then_inc(s_v, 1)
            dve.wait_ge(s_v, 7)
            nc.vector.tensor_tensor(absg[:], absg[:], raw[:], ALU.max).then_inc(s_v, 1)
            nc.vector.tensor_scalar(sgn[:], sgn[:], -1.0, None, ALU.add).then_inc(s_v, 1)
            dve.wait_ge(s_v, 9)
            nc.vector.tensor_scalar(absg[:], absg[:], 0.25, None, ALU.max).then_inc(s_v, 1)
            dve.wait_ge(s_v, 10)
            nc.vector.tensor_tensor(gates[:], absg[:], sgn[:], ALU.mult).then_inc(s_v, 1)
            dve.wait_ge(s_v, 11)

        @block.tensor
        def _(pe):
            pe.wait_ge(s_load, 80)
            pe.wait_ge(s_silu, 1)
            for j in range(12):
                for dc in range(DC):
                    last = nc.tensor.matmul(pm[:, j, :], wm[:, dc, j * P:(j + 1) * P], sc[:, dc, :],
                                            start=(dc == 0), stop=(dc == DC - 1))
            last.then_inc(s_col, 1)
            pe.wait_ge(s_bc, 1)
            for g, part in enumerate((GA, GB)):
                for b in range(B):
                    for dc in range(DC):
                        last = nc.tensor.matmul(pg[:, g * B + b, :], scb[:, dc, b, :],
                                                wm[:, dc, part * D:(part + 1) * D],
                                                start=(dc == 0), stop=(dc == DC - 1))
            last.then_inc(s_row, 1)


def norm_first(nc, sem, x, ident, modT, hT):
    s_x = [sem(f"x_loaded_{b}") for b in range(B)]
    s_st, s_ag, s_sq = sem("x_stats"), sem("x_moments"), sem("x_root")
    s_rs, s_n, s_t, s_e = sem("x_rstd"), sem("x_normed"), sem("x_turned"), sem("x_kept")
    with ExitStack() as st:
        xs = st.enter_context(nc.sbuf_tensor("xs", [P, B * NT, D], F32))
        stats = st.enter_context(nc.sbuf_tensor("stats", [P, B * NT, 6], F32))
        mv = st.enter_context(nc.sbuf_tensor("mv", [P, B * NT, 2], F32))
        eps = st.enter_context(nc.sbuf_tensor("eps", [P, 1], F32))
        sd = st.enter_context(nc.sbuf_tensor("sd", [P, B * NT], F32))
        rstd = st.enter_context(nc.sbuf_tensor("rstd", [P, B * NT], F32))
        pt = st.enter_context(nc.psum_tensor("pt", [P, 2, DC, G], F32))
        block = st.enter_context(nc.Block())

        @block.sync
        def _(sp):
            for b in range(B):
                sp.dma_start(xs[:, b * NT:(b + 1) * NT, :], x[:, b * NT:(b + 1) * NT, :]).then_inc(s_x[b], 16)

        @block.scalar
        def _(act):
            act.wait_ge(s_ag, B * NT + 1)
            nc.scalar.activation(sd[:], mv[:, :, 1], ACT.Sqrt, bias=eps[:, 0:1]).then_inc(s_sq, 1)

        @block.vector
        def _(dve):
            nc.vector.memset(eps[:], LN_EPS).then_inc(s_ag, 1)
            for b in range(B):
                dve.wait_ge(s_x[b], 16)
                for i in range(b * NT, (b + 1) * NT):
                    nc.vector.bn_stats(stats[:, i, :], xs[:, i, :]).then_inc(s_st, 1)
            dve.wait_ge(s_st, B * NT)
            for i in range(B * NT):
                nc.vector.bn_aggr(mv[:, i, :], stats[:, i, :]).then_inc(s_ag, 1)
            dve.wait_ge(s_sq, 1)
            nc.vector.reciprocal(rstd[:], sd[:]).then_inc(s_rs, 1)
            dve.wait_ge(s_rs, 1)
            for i in range(B * NT):
                nc.vector.tensor_scalar(xs[:, i, :], xs[:, i, :], mv[:, i, 0:1], rstd[:, i:i + 1],
                                        ALU.subtract, ALU.mult).then_inc(s_n, 1)
            for g in range(B * GH):
                dve.wait_ge(s_t, g + 1)
                b = g // GH
                for dc in range(DC):
                    nc.vector.tensor_scalar(hT[:, dc, g * G:(g + 1) * G], pt[:, g % 2, dc, :],
                                            modT[:, 2 * CA + dc, b:b + 1], modT[:, 2 * SA + dc, b:b + 1],
                                            ALU.mult, ALU.add).then_inc(s_e, 1)
            dve.wait_ge(s_e, DC * B * GH)

        @block.tensor
        def _(pe):
            for g in range(B * GH):
                pe.wait_ge(s_n, (g + 1) * GT)
                if g >= 2:
                    pe.wait_ge(s_e, DC * (g - 1))
                for j in range(GT):
                    for dc in range(DC):
                        last = nc.tensor.transpose(pt[:, g % 2, dc, j * P:(j + 1) * P],
                                                   xs[:, g * GT + j, dc * P:(dc + 1) * P], ident[:])
                last.then_inc(s_t, 1)


def gate_scalars(nc, sem, wab, bab, ident, hT, la, bt, ab_s):
    s_w, s_p, s_a, s_o = sem("ab_weights"), sem("ab_product"), sem("ab_sigmoid"), sem("ab_stored")
    s_t, s_l, s_m = sem("ab_turned"), sem("ab_log_steps"), sem("ab_mins")
    N = B * NT
    with ExitStack() as st:
        w = st.enter_context(nc.sbuf_tensor("wab_sb", [P, DC, 2 * H], F32))
        bias = st.enter_context(nc.sbuf_tensor("bab_sb", [2 * H, 1], F32))
        ab = st.enter_context(nc.sbuf_tensor("ab", [2 * H, B, T], F32))
        logit = st.enter_context(nc.sbuf_tensor("ab_logit", [2 * H, B * T], F32))
        az = st.enter_context(nc.sbuf_tensor("ab_size", [P, N, H], F32))
        pa = st.enter_context(nc.psum_tensor("pa", [P, 2, G], F32))
        pz = st.enter_context(nc.psum_tensor("pz", [P, N, 2 * H], F32))
        block = st.enter_context(nc.Block())

        @block.sync
        def _(sp):
            sp.dma_start(w[:], wab).then_inc(s_w, 16)
            sp.dma_start(bias[:], bab).then_inc(s_w, 16)
            sp.wait_ge(s_a, B * GH)
            sp.dma_start(ab_s, ab[:]).then_inc(s_o, 16)
            sp.wait_ge(s_o, 16)

        @block.scalar
        def _(act):
            act.wait_ge(s_w, 32)
            for g in range(B * GH):
                act.wait_ge(s_p, g + 1)
                nc.scalar.activation(logit[:, g * G:(g + 1) * G], pa[0:2 * H, g % 2, :], ACT.Identity, bias=bias[:, 0:1])
                nc.scalar.activation(ab[:].rearrange("h b t -> h (b t)")[:, g * G:(g + 1) * G],
                                     pa[0:2 * H, g % 2, :], ACT.Sigmoid, bias=bias[:, 0:1]).then_inc(s_a, 1)
            act.wait_ge(s_t, 1)
            nc.scalar.activation(bt[:, :, 0:H], pz[:, :, H:2 * H], ACT.Sigmoid)
            nc.scalar.activation(az[:], pz[:, :, 0:H], ACT.Abs).then_inc(s_l, 1)
            act.wait_ge(s_l, 1)
            nc.scalar.activation(az[:], az[:], ACT.Exp, scale=-1.0).then_inc(s_l, 1)
            act.wait_ge(s_l, 2)
            nc.scalar.activation(az[:], az[:], ACT.Ln, bias=1.0).then_inc(s_l, 1)

        @block.vector
        def _(dve):
            dve.wait_ge(s_l, 1)
            nc.vector.tensor_scalar(la[:, :, 0:H], pz[:, :, 0:H], 0.0, None, ALU.min).then_inc(s_m, 1)
            dve.wait_ge(s_l, 3)
            dve.wait_ge(s_m, 1)
            nc.vector.tensor_tensor(la[:, :, 0:H], la[:, :, 0:H], az[:], ALU.subtract).then_inc(s_m, 1)
            dve.wait_ge(s_m, 2)

        @block.tensor
        def _(pe):
            pe.wait_ge(s_w, 32)
            for g in range(B * GH):
                if g >= 2:
                    pe.wait_ge(s_a, g - 1)
                for dc in range(DC):
                    last = nc.tensor.matmul(pa[0:2 * H, g % 2, :], w[:, dc, :], hT[:, dc, g * G:(g + 1) * G],
                                            start=(dc == 0), stop=(dc == DC - 1))
                last.then_inc(s_p, 1)
            for i in range(N):
                if i % GT == 0:
                    pe.wait_ge(s_a, i // GT + 1)
                last = nc.tensor.transpose(pz[:, i, :], logit[:, i * P:(i + 1) * P], ident[0:2 * H, 0:2 * H])
            last.then_inc(s_t, 1)


TRI64, TRI32, AFTER64, CHUNK0, CHUNK1 = range(5)
CH = 64
HB = 32
NCH = T // CH
NN = 2 * NT * 2
NG_K = 4
LIMIT = 4.99


def delta_fast(nc, sem, ident, wqkv, convp, tri_d, mask_d, hT, la, bt, ab_s, y_s, fmax):
    (s_turn, s_c, s_w, s_ar) = (sem("d_turn"), sem("d_const"), sem("d_weights"), sem("d_alpha_rows"))
    (s_proj, s_raw, s_tap, s_tp, s_silu) = (sem("d_proj"), sem("d_raw"), sem("d_taps"), sem("d_tap_part"),
                                            sem("d_silu"))
    (s_sel, s_lm, s_sm, s_pd, s_ex) = (sem("d_select"), sem("d_masked_logs"), sem("d_small_sums"), sem("d_log_sums"),
                                       sem("d_exp"))
    (s_kt, s_ktok, s_vt, s_v0, s_lmt) = (sem("d_k_turned"), sem("d_k_kept"), sem("d_v_turned"), sem("d_v0"),
                                         sem("d_masked_logs_t"))
    (s_n2, s_rt, s_sc, s_km) = (sem("d_norm2"), sem("d_norm"), sem("d_scalars"), sem("d_kmax"))
    (s_em, s_ec, s_y0) = (sem("d_masked_decay"), sem("d_decay_c"), sem("d_y0_khat"))
    (s_kk, s_T, s_kq, s_AT) = (sem("d_kk"), sem("d_T"), sem("d_kq"), sem("d_AT"))
    (s_x0, s_tq, s_sub, s_xt) = (sem("d_x_one"), sem("d_T_turned"), sem("d_subst"), sem("d_X_turned"))
    (s_p1, s_p1e, s_p2, s_p2e) = (sem("d_join1"), sem("d_join1_kept"), sem("d_join2"), sem("d_join2_kept"))
    (s_yk, s_yke, s_g, s_q) = (sem("d_yk"), sem("d_yk_kept"), sem("d_gamma_rows"), sem("d_q_decayed"))
    (s_U, s_Ue, s_S, s_Se, s_y, s_ye) = (sem("d_u"), sem("d_u_kept"), sem("d_s"), sem("d_s_kept"), sem("d_y"),
                                         sem("d_y_kept"))
    (s_ua, s_z, s_zt, s_m, s_r, s_end, s_o) = (sem("d_u_abs"), sem("d_z"), sem("d_z_turned"), sem("d_bound"),
                                               sem("d_bound_max"), sem("d_end"), sem("d_stored"))
    s_mx, s_stored = sem("d_max"), sem("d_y_stored")
    BP = B // 2
    TURNS = BP * M
    U6 = [(n, b2) for n in (1, 0, 2) for b2 in range(2)]

    with ExitStack() as st:
        def sb(name, *shape):
            return st.enter_context(nc.sbuf_tensor("d_" + name, [P, *shape], F32))

        tri = sb("tri", 5, P)
        msk = sb("msk", 2 * HB + CH)
        mask_d32, mask_o32, mask_t64 = msk[:, 0:HB], msk[:, HB:2 * HB], msk[:, 2 * HB:]
        w = sb("w", 3, DC, P)
        cw = sb("cw", 3, 5)
        raw = sb("raw", 6, 4 + T)
        tap = sb("tap", 2, T)
        qT, kT, vT = sb("qT", 2, T), sb("kT", 2, T), sb("vT", 2, T)
        res = [qT, kT, vT]
        lsu, bsu = sb("lsu", NN), sb("bsu", NN)
        ktok = sb("ktok", NN, DH)
        L = [sb("L0", NN, CH), sb("L1", NN, CH)]
        R = [sb("R0", NN, DH), sb("R1", NN, DH)]
        KG = [sb("KG0", NN, DH), sb("KG1", NN, DH)]
        QA = [sb("QA0", NN, CH), sb("QA1", NN, CH)]
        ksq = KG[0]
        Lm_t = R[0]
        Pp, Xn = sb("Pp", NN, HB), sb("Xn", NN, HB)
        Lm_d, Lm_o = Pp, Xn
        ex4 = sb("ex4", 4, NN)
        EX = sb("EX", 2, HB, HB)
        Ed, X, Eo = EX[:, 0], EX[:, 1], sb("Eo", NN, HB)
        Td, To = Ed, Eo
        Tq = sb("Tq", HB, HB)
        grow = EX[:].rearrange("p a n c -> p a (n c)")
        yT = grow
        Y0 = tap[:].rearrange("p a (n c) -> p (a n) c", c=DH)
        Ua, *Z = [raw[:, 2 * i:2 * i + 2, 4:].rearrange("p b (n c) -> p b n c", c=DH) for i in range(3)]
        tmp = Td
        arow = sb("arow", 2, T)
        n2, rt, rn, brn, cc, yc = (sb("n2", NN), sb("rt", NN), sb("rn", NN), sb("brn", NN), sb("cc", NN),
                                   sb("yc", NN))
        kmax = sb("kmax", NN, NG_K)
        zero = sb("zero", CH)
        msc = tap
        fm = sb("fm", 8)
        fone = sb("fone", 1)
        ps = st.enter_context(nc.psum_tensor("d_ps", [P, 8, G], F32))
        SA_, SB_, SC_, SD_ = ps[:, 0:2], ps[:, 2:4], ps[:, 4:6], ps[:, 6:8]

        def nview(pair, width):
            return pair.rearrange("p a (n c) -> p (a n) c", c=width)

        half = [slice(0, CH), slice(CH, P)]

        def hview(pair):
            return pair.rearrange("p h (t c) -> p t h c", c=CH)

        def by_head(ap):
            return ap.rearrange("p (t h) c -> p t h c", h=2)

        def heads_of(buf, rows, b2, t8):
            n = b2 * 16 + 2 * t8
            return buf[rows, n:n + 2, :].rearrange("p n c -> p (n c)")

        def wide(ap, n, width):
            return ap.rearrange("p (n a) -> p n a", a=1).broadcast_to([ap.shape[0], n, width])

        def mwide(ap, n):
            return ap.rearrange("p (a c) -> p a c", a=1).broadcast_to([P, n, ap.shape[1]])

        block = st.enter_context(nc.Block())

        def turns(eng, body):
            with eng.Fori(0, M) as m:
                for bp in range(BP):
                    body(bp, m, m * BP + bp)

        @block.sync
        def _(sp):
            sp.dma_start(tri[:], tri_d).then_inc(s_c, 16)
            sp.dma_start(msk[:], mask_d).then_inc(s_c, 16)
            sp.sem_inc(s_turn, 1)
            sp.sem_inc(s_stored, 1)
            sp.dma_start(w[:], wqkv[0]).then_inc(s_w, 16)
            sp.dma_start(cw[:], convp[0]).then_inc(s_w, 16)
            for su in range(TURNS):
                m, bp = su // BP, su % BP
                if bp == BP - 1:
                    sp.dma_start(w[:], wqkv[(m + 1) % M]).then_inc(s_w, 16)
                    sp.dma_start(cw[:], convp[(m + 1) % M]).then_inc(s_w, 16)
                sp.wait_ge(s_end, su + 1)
                for b2 in range(2):
                    for h in range(2):
                        sp.dma_start(arow[h * DH:(h + 1) * DH, b2, :],
                                     ab_s[2 * m + h, 2 * bp + b2:2 * bp + b2 + 1, :].broadcast_to([DH, T])
                                     ).then_inc(s_ar, 16)
                sp.wait_ge(s_ye, 4 * (su + 1))
                for b2 in range(2):
                    sp.dma_start(y_s[2 * bp + b2, m], yT[:, b2, :]).then_inc(s_o, 16)
                sp.wait_ge(s_tp, 36 * (su + 2))
                sp.wait_ge(s_silu, 6 * (su + 2))
                sp.wait_ge(s_ua, 2 * (su + 1))
                sp.sem_inc(s_turn, 1)
                sp.wait_ge(s_o, 32 * (su + 1))
                sp.sem_inc(s_stored, 1)

        @block.scalar
        def _(act):
            def keep(i, turn, pair):
                act.wait_ge(s_proj, turn * 6 + (i + 1))
                nc.scalar.activation(raw[:, i, 4:], pair.rearrange("p a c -> p (a c)"), ACT.Identity).then_inc(s_raw, 1)

            def tap_first(i, turn):
                act.wait_ge(s_raw, turn * 6 + (i + 1))
                if i >= 2:
                    act.wait_ge(s_silu, turn * 6 + (i - 1))
                nc.scalar.activation(tap[:, i % 2, :], raw[:, i, 4:], ACT.Identity, bias=cw[:, U6[i][0], 4:5],
                                     scale=cw[:, U6[i][0], 3:4]).then_inc(s_tap, 1)

            def silu(i, turn):
                act.wait_ge(s_tp, turn * 36 + 6 * (i + 1))
                nc.scalar.activation(res[U6[i][0]][:, U6[i][1], :], tap[:, i % 2, :], ACT.Silu).then_inc(s_silu, 1)

            act.wait_ge(s_w, 32)
            for i in range(6):
                keep(i, 0, (SA_, SD_)[i % 2])
            for i in range(2):
                tap_first(i, 0)
            for i in range(6):
                silu(i, 0)
                if i < 4:
                    tap_first(i + 2, 0)

            def body(bp, m, su):
                act.wait_ge(s_turn, su + 1)
                for b2, pair in enumerate((SA_, SB_)):
                    act.wait_ge(s_kt, su * 2 + (b2 + 1))
                    nc.scalar.activation(ktok[:, b2 * 16:(b2 + 1) * 16, :], nview(pair, DH), ACT.Identity)
                    nc.scalar.activation(ksq[:, b2 * 16:(b2 + 1) * 16, :], nview(pair, DH),
                                         ACT.Square).then_inc(s_ktok, 1)
                act.wait_ge(s_sm, su + 1)
                nc.scalar.activation(ex4[:].rearrange("p a n -> p (a n)"), ps[:, 0, 0:4 * NN],
                                     ACT.Exp).then_inc(s_ex, 1)
                act.wait_ge(s_stored, su + 1)
                for i, (dst, pair) in enumerate(((Ed, SB_), (Eo, SA_))):
                    act.wait_ge(s_pd, su * 4 + (i + 1))
                    nc.scalar.activation(dst[:], nview(pair, HB), ACT.Exp).then_inc(s_ex, 1)
                for b2, pair in enumerate((SB_, SA_)):
                    act.wait_ge(s_pd, su * 4 + (b2 + 3))
                    for cp in range(2):
                        last = nc.scalar.activation(QA[cp][half[cp], b2 * 16:(b2 + 1) * 16, :],
                                                    nview(pair, CH)[half[cp]], ACT.Exp)
                    last.then_inc(s_ex, 1)
                act.wait_ge(s_n2, su + 1)
                nc.scalar.activation(rt[:], n2[:], ACT.Sqrt).then_inc(s_rt, 1)
                act.wait_ge(s_end, su + 1)
                for i in range(6):
                    keep(i, su + 1, (SA_, SD_)[i % 2])
                for b2, pair in enumerate((SA_, SD_)):
                    act.wait_ge(s_p1, su * 2 + (b2 + 1))
                    for cp in range(2):
                        rows = slice(cp * CH, cp * CH + HB)
                        last = nc.scalar.activation(Pp[rows, b2 * 16:(b2 + 1) * 16, :], nview(pair, HB)[rows, 0:16, :],
                                                    ACT.Identity)
                    last.then_inc(s_p1e, 1)
                for b2, pair in enumerate((SA_, SD_)):
                    act.wait_ge(s_p2, su * 2 + (b2 + 1))
                    for cp in range(2):
                        rows = slice(cp * CH, cp * CH + HB)
                        last = nc.scalar.activation(L[cp][rows, b2 * 16:(b2 + 1) * 16, HB:CH],
                                                    nview(pair, HB)[rows, 16:32, :], ACT.Identity, scale=-1.0)
                    last.then_inc(s_p2e, 1)
                for b2, pair in enumerate((SB_, SC_)):
                    act.wait_ge(s_yk, su * 2 + (b2 + 1))
                    for cp in range(2):
                        last = nc.scalar.activation(L[cp][half[1 - cp], b2 * 16:(b2 + 1) * 16, :],
                                                    nview(pair, CH)[half[1 - cp]], ACT.Identity)
                    last.then_inc(s_yke, 1)
                def keep_y(hf):
                    act.wait_ge(s_y, su * NCH + 8 * (hf + 1))
                    for b2 in range(2):
                        nc.scalar.activation(yT[:, b2, hf * G:(hf + 1) * G], ps[:, 2 * hf + b2, :],
                                             ACT.Identity).then_inc(s_ye, 1)

                def abs_u(hf):
                    act.wait_ge(s_Ue, su * (2 * NCH) + 16 * (hf + 1))
                    ns = slice(8 * hf, 8 * hf + 8)
                    for cp in range(2):
                        last = nc.scalar.activation(
                            Ua[half[cp], :, ns, :], R[cp][half[cp]].rearrange("p (b n) c -> p b n c", b=2)[:, :, ns, :],
                            ACT.Abs)
                    last.then_inc(s_ua, 1)

                if bp == BP - 1:
                    act.wait_ge(s_w, m * 32 + 64)
                for i in range(2):
                    tap_first(i, su + 1)
                for i in range(6):
                    if i == 4:
                        abs_u(1)
                        keep_y(1)
                    silu(i, su + 1)
                    if i < 4:
                        tap_first(i + 2, su + 1)
                    if i == 3:
                        keep_y(0)
                        abs_u(0)
            turns(act, body)

        @block.gpsimd
        def _(pool):
            def logs(turn):
                pool.wait_ge(s_sel, turn * 2 + 2)
                nc.gpsimd.tensor_tensor(Lm_d[:], wide(lsu[:], NN, HB), mwide(mask_d32, NN), ALU.mult)
                nc.gpsimd.tensor_tensor(Lm_o[:], wide(lsu[:], NN, HB), mwide(mask_o32, NN), ALU.mult).then_inc(s_lm, 1)

            def z_part(g, t, ns=slice(0, NN // 2)):
                if g >= 2:
                    pool.wait_ge(s_zt, t * (2 * NG_K) + 2 * (g - 1))
                last = nc.gpsimd.tensor_tensor(
                    Z[g % 2][:, :, ns, :], Ua[:, :, ns, :],
                    kmax[:, :, g].rearrange("p (b n a) -> p b n a", b=2, a=1)[:, :, ns, :]
                    .broadcast_to([P, 2, ns.stop - ns.start, DH]), ALU.mult)
                if ns.stop == NN // 2:
                    last.then_inc(s_z, 1)

            logs(0)
            pool.wait_ge(s_silu, 6)
            z_part(0, 0)

            def body(bp, m, su):
                pool.wait_ge(s_turn, su + 1)
                z_part(1, su)
                nc.gpsimd.tensor_tensor(Lm_t[:], wide(lsu[:], NN, CH), mwide(mask_t64, NN), ALU.mult).then_inc(s_lmt, 1)
                for g in range(2, NG_K):
                    z_part(g, su)
                count = pool.compute_val(su + 1)
                pool.wait_ge(s_c, 32)
                pool.wait_ge(s_stored, count)
                nc.gpsimd.memset(X[:], 0.0).then_inc(s_x0, 1)
                count = pool.compute_val(su * 2 + 1)
                pool.wait_ge(s_c, 32)
                pool.wait_ge(s_x0, count)
                nc.gpsimd.memset(X.rearrange("p r c -> p (r c)")[:, 0:HB * HB:HB + 1], 1.0).then_inc(s_x0, 1)
                pool.wait_ge(s_ex, su * 5 + 5)
                for cp in range(2):
                    if cp:
                        pool.wait_ge(s_em, su * 2 + 1)
                    nc.gpsimd.tensor_tensor(QA[cp][half[cp]], QA[cp][half[cp]], mwide(mask_t64, NN)[half[cp]],
                                            ALU.mult).then_inc(s_em, 1)
                pool.wait_ge(s_em, su * 2 + 2)
                pool.wait_ge(s_n2, su + 1)
                for cp in range(2):
                    if cp:
                        pool.wait_ge(s_y0, su * 5 + 2)
                    nc.gpsimd.tensor_tensor(KG[cp][half[cp]], ktok[half[cp]], wide(ex4[half[cp], 1, :], NN, DH),
                                            ALU.mult).then_inc(s_y0, 1)
                    pool.wait_ge(s_y0, su * 5 + (2 * cp + 1))
                    rows = half[1 - cp]
                    nc.gpsimd.tensor_tensor(KG[cp][rows], wide(ex4[rows, 2 + cp, :], NN, DH),
                                            mwide(ident[:, rows], NN)[rows], ALU.mult).then_inc(s_y0, 1)
                pool.wait_ge(s_y0, su * 5 + 4)
                pool.wait_ge(s_sc, su * 5 + 5)
                pool.wait_ge(s_end, su + 1)
                nc.gpsimd.tensor_tensor(Y0, ktok[:], wide(yc[:], NN, DH), ALU.mult).then_inc(s_y0, 1)
                pool.wait_ge(s_p2, su * 2 + 2)
                logs(su + 1)
                for hf in range(2):
                    pool.wait_ge(s_ua, su * 2 + (hf + 1))
                    z_part(0, su + 1, slice(8 * hf, 8 * hf + 8))
            turns(pool, body)
            pool.wait_ge(s_turn, TURNS + 1)
            for g in range(1, NG_K):
                z_part(g, TURNS)

        @block.vector
        def _(dve):
            dve.wait_ge(s_c, 32)
            nc.vector.memset(raw[:, :, 0:4], 0.0).then_inc(s_mx, 1)
            nc.vector.memset(zero[:], 0.0).then_inc(s_mx, 1)
            nc.vector.memset(L[0][HB:CH, :, 0:HB], 0.0).then_inc(s_mx, 1)
            nc.vector.memset(L[1][CH + HB:P, :, 0:HB], 0.0).then_inc(s_mx, 1)
            nc.vector.memset(fmax[:], 0.0).then_inc(s_mx, 1)
            nc.vector.memset(arow[:], 0.0).then_inc(s_mx, 1)
            nc.vector.memset(kmax[:], 0.0).then_inc(s_mx, 1)
            nc.vector.memset(la[:, :, H:], 0.0).then_inc(s_mx, 1)
            nc.vector.memset(bt[:, :, H:], 0.0).then_inc(s_mx, 1)
            dve.wait_ge(s_mx, 9)

            def select(bp, heads_at):
                for dst, src in ((lsu, la), (bsu, bt)):
                    nc.vector.tensor_scalar(dst[:].rearrange("p (n h) -> p n h", h=2),
                                            src[:, bp * 16:(bp + 1) * 16, heads_at], 1.0, None,
                                            ALU.mult).then_inc(s_sel, 1)

            def bound_part(i, t):
                b2 = i % 2
                pair = (SC_, SD_)[i % 2]
                dve.wait_ge(s_zt, t * (2 * NG_K) + (i + 1))
                if i >= 2:
                    dve.wait_ge(s_r, t * (2 * NG_K) + (i - 1))
                for hf in range(2):
                    hs = slice(hf * G, (hf + 1) * G)
                    nc.vector.tensor_tensor_scan(
                        msc[:, i % 2, hs], arow[:, b2, hs], pair[:, hf, :],
                        0.0 if hf == 0 else msc[:, i % 2, G - 1:G], ALU.mult, ALU.add).then_inc(s_m, 1)
                    dve.wait_ge(s_m, t * (4 * NG_K) + (2 * i + hf + 1))
                nc.vector.tensor_reduce(fm[:, i:i + 1], msc[:, i % 2, :], AX_X, ALU.max).then_inc(s_r, 1)

            def bound_end(t):
                dve.wait_ge(s_r, t * (2 * NG_K) + 2 * NG_K)
                nc.vector.tensor_reduce(fone[:], fm[:], AX_X, ALU.max).then_inc(s_mx, 1)
                dve.wait_ge(s_mx, t + 10)
                nc.vector.tensor_tensor(fmax[:], fmax[:], fone[:], ALU.max).then_inc(s_end, 1)

            def tap_part(o, turn):
                i, j, hf = o // 6, o % 6 // 2, o % 2
                if j == 0:
                    dve.wait_ge(s_tap, turn * 6 + (i + 1))
                else:
                    dve.wait_ge(s_tp, turn * 36 + (o - 1))
                k, n = 2 - j, U6[i][0]
                hs = slice(hf * G, (hf + 1) * G)
                nc.vector.scalar_tensor_tensor(
                    out=tap[:, i % 2, hs], in0=raw[:, i, 1 + k + hf * G:1 + k + (hf + 1) * G],
                    scalar=cw[:, n, k:k + 1], in1=tap[:, i % 2, hs], op0=ALU.mult, op1=ALU.add).then_inc(s_tp, 1)

            dve.wait_ge(s_w, 32)
            select(0, slice(0, 2))
            for o in range(36):
                tap_part(o, 0)

            def body(bp, m, su):
                dve.wait_ge(s_turn, su + 1)
                dve.wait_ge(s_silu, su * 6 + 6)
                for i in range(4):
                    bound_part(i, su)
                dve.wait_ge(s_ktok, su * 2 + 2)
                nc.vector.tensor_reduce(n2[:], ksq[:], AX_X,
                                        ALU.add).then_inc(s_n2, 1)
                for i in range(4, 2 * NG_K):
                    bound_part(i, su)
                bound_end(su)
                dve.wait_ge(s_rt, su + 1)
                nc.vector.tensor_scalar(rn[:], rt[:], NORM_EPS, None, ALU.max).then_inc(s_sc, 1)
                dve.wait_ge(s_sc, su * 5 + 1)
                nc.vector.reciprocal(rn[:], rn[:]).then_inc(s_sc, 1)
                dve.wait_ge(s_sc, su * 5 + 2)
                nc.vector.tensor_tensor(brn[:], bsu[:], rn[:], ALU.mult).then_inc(s_sc, 1)
                dve.wait_ge(s_sc, su * 5 + 3)
                nc.vector.tensor_tensor(cc[:], brn[:], rn[:], ALU.mult).then_inc(s_sc, 1)
                dve.wait_ge(s_sc, su * 5 + 4)
                dve.wait_ge(s_ex, su * 5 + 1)
                nc.vector.scalar_tensor_tensor(out=yc[:], in0=cc[:], scalar=-1.0, in1=ex4[:, 0, :], op0=ALU.mult,
                                               op1=ALU.mult).then_inc(s_sc, 1)
                dve.wait_ge(s_ex, su * 5 + 3)
                nc.vector.tensor_tensor(Ed[:], Ed[:], wide(cc[:], NN, HB), ALU.mult).then_inc(s_ec, 1)
                nc.vector.tensor_tensor(Eo[:], Eo[:], wide(cc[:], NN, HB), ALU.mult).then_inc(s_ec, 1)
                dve.wait_ge(s_ec, su * 2 + 2)
                for b2, pair in enumerate((SA_, SD_)):
                    dve.wait_ge(s_kk, su * 2 + (b2 + 1))
                    ns = slice(b2 * 16, (b2 + 1) * 16)
                    for q4 in range(4):
                        rows = slice(q4 * HB, (q4 + 1) * HB)
                        c0 = (q4 % 2) * HB
                        ins = nc.vector.tensor_tensor(by_head(Td[rows, ns, :]), hview(pair)[rows, :, :, c0:c0 + HB],
                                                      by_head(Ed[rows, ns, :]), ALU.mult)
                        if q4 % 2:
                            ins = nc.vector.tensor_tensor(by_head(To[rows, ns, :]), hview(pair)[rows, :, :, 0:HB],
                                                          by_head(Eo[rows, ns, :]), ALU.mult)
                    ins.then_inc(s_T, 1)
                dve.wait_ge(s_T, su * 2 + 2)
                nc.vector.transpose(Tq[:], Td[:].rearrange("p n s -> p s n")).then_inc(s_tq, 1)
                def masked_kq(b2):
                    dve.wait_ge(s_em, su * 2 + 2)
                    dve.wait_ge(s_kq, su * 2 + (b2 + 1))
                    ns = slice(b2 * 16, (b2 + 1) * 16)
                    for cp in range(2):
                        a = by_head(QA[cp][half[cp], ns, :])
                        ins = nc.vector.tensor_tensor(a, hview((SA_, SD_)[b2])[half[cp]], a, ALU.mult)
                    ins.then_inc(s_AT, 1)

                dve.wait_ge(s_x0, su * 2 + 2)
                dve.wait_ge(s_tq, su + 1)
                for s in range(HB - 1):
                    left, known = HB - 1 - s, s + 1
                    if s:
                        dve.wait_ge(s_sub, su * 62 + 2 * s)
                    tv = tmp[:].rearrange("p a b -> p (a b)")[:, 0:left * known].rearrange("p (r c) -> p r c", c=known)
                    nc.vector.tensor_tensor(
                        tv, Tq[:, s, s + 1:].rearrange("p (r a) -> p r a", a=1).broadcast_to([P, left, known]),
                        X[:, s, 0:known].rearrange("p (a c) -> p a c", a=1).broadcast_to([P, left, known]),
                        ALU.mult).then_inc(s_sub, 1)
                    dve.wait_ge(s_sub, su * 62 + (2 * s + 1))
                    nc.vector.tensor_tensor(X[:, s + 1:, 0:known], X[:, s + 1:, 0:known], tv,
                                            ALU.subtract).then_inc(s_sub, 1)
                    if s == 4 or s == 9:
                        masked_kq(s // 5)
                dve.wait_ge(s_sub, su * 62 + 62)
                def x_turned(q4):
                    rows = slice(q4 * HB, (q4 + 1) * HB)
                    c0 = (q4 % 2) * HB
                    return nc.vector.transpose(L[q4 // 2][rows, :, c0:c0 + HB].rearrange("p n r -> p r n"), X[rows])

                x_turned(1)
                x_turned(3).then_inc(s_xt, 1)
                nc.vector.transpose(Xn[:].rearrange("p n c -> p c n"),
                                    X[:].rearrange("p r c -> p c r")).then_inc(s_xt, 1)
                x_turned(0)
                x_turned(2).then_inc(s_xt, 1)
                for b2, pair in enumerate((SB_, SC_)):
                    dve.wait_ge(s_vt, su * 2 + (b2 + 1))
                    ns = slice(b2 * 16, (b2 + 1) * 16)
                    for cp in range(2):
                        ins = nc.vector.tensor_tensor(R[cp][half[cp], ns, :], nview(pair, DH)[half[cp]],
                                                      wide(brn[half[cp], ns], 16, DH), ALU.mult)
                    ins = nc.vector.memset(R[0][half[1], b2 * 16:b2 * 16 + 2, :], 0.0)
                    ins.then_inc(s_v0, 1)
                dve.wait_ge(s_ar, su * 64 + 64)
                dve.wait_ge(s_xt, su * 3 + 3)
                for b2 in range(2):
                    for c in range(NCH):
                        ins = nc.vector.tensor_tensor_scan(grow[:, b2, c * CH:(c + 1) * CH],
                                                           arow[:, b2, c * CH:(c + 1) * CH], zero[:], 1.0,
                                                           ALU.mult, ALU.add)
                ins.then_inc(s_g, 1)
                dve.wait_ge(s_g, su + 1)
                for cp in range(2):
                    for h in range(2):
                        for b2 in range(2):
                            ins = nc.vector.tensor_tensor(
                                QA[cp][half[1 - cp], b2 * 16 + h:(b2 + 1) * 16:2, :],
                                qT[half[h], b2, :].rearrange("p (t a c) -> p t a c", a=2, c=CH)[:, :, cp, :],
                                grow[half[h], b2, :].rearrange("p (t a c) -> p t a c", a=2, c=CH)[:, :, cp, :],
                                ALU.mult)
                ins.then_inc(s_q, 1)
                dve.wait_ge(s_ktok, su * 2 + 2)
                nc.vector.tensor_reduce(kmax[:].rearrange("p n g -> p (n g)"),
                                        ktok[:].rearrange("p n (g c) -> p (n g) c", g=NG_K), AX_X, ALU.max,
                                        apply_absolute_value=True).then_inc(s_km, 1)
                select((bp + 1) % BP, bass.ds(m * 2 + (2 if bp == BP - 1 else 0), 2))
                if bp == BP - 1:
                    dve.wait_ge(s_w, m * 32 + 64)
                for c in range(NCH):
                    t8, cp = c // 2, c % 2
                    rows = half[cp]
                    for b2 in range(2):
                        dve.wait_ge(s_U, su * (2 * NCH) + (2 * c + b2 + 1))
                        nc.vector.tensor_copy(heads_of(R[cp], rows, b2, t8), ps[rows, 4 + b2, 0:2 * DH]).then_inc(s_Ue, 1)
                    tap_part(2 * c, su + 1)
                    if c < NCH - 1:
                        for b2 in range(2):
                            dve.wait_ge(s_S, su * (2 * NCH - 2) + (2 * c + b2 + 1))
                            nc.vector.tensor_copy(heads_of(R[1 - cp], rows, b2, (c + 1) // 2),
                                                  ps[rows, 6 + b2, 0:2 * DH]).then_inc(s_Se, 1)
                    tap_part(2 * c + 1, su + 1)
                for o in range(2 * NCH, 36):
                    tap_part(o, su + 1)
            turns(dve, body)
            dve.wait_ge(s_turn, TURNS + 1)
            for i in range(2 * NG_K):
                bound_part(i, TURNS)
            bound_end(TURNS)
            dve.wait_ge(s_end, TURNS + 1)

        @block.tensor
        def _(pe):
            pe.wait_ge(s_c, 32)

            def proj(i, turn, bp):
                n, b2 = U6[i]
                if i >= 2:
                    pe.wait_ge(s_raw, turn * 6 + (i - 1))
                for g in range(GH):
                    for dc in range(DC):
                        last = nc.tensor.matmul((SA_, SD_)[i % 2][:, g, :], w[:, n, dc, :],
                                                hT[:, dc, (2 * bp + b2) * T + g * G:(2 * bp + b2) * T + (g + 1) * G],
                                                start=(dc == 0), stop=(dc == DC - 1))
                last.then_inc(s_proj, 1)

            def z_turned(i, t):
                g, b2 = i // 2, i % 2
                pe.wait_ge(s_z, t * NG_K + (g + 1))
                if i >= 2:
                    pe.wait_ge(s_m, t * (4 * NG_K) + 2 * (i - 1))
                for t8 in range(NT):
                    last = nc.tensor.transpose(nview((SC_, SD_)[i % 2], P)[:, t8, :],
                                               Z[g % 2][:, b2, 2 * t8:2 * t8 + 2, :].rearrange("p h c -> p (h c)"),
                                               ident[:])
                last.then_inc(s_zt, 1)

            pe.wait_ge(s_w, 32)
            for i in range(6):
                proj(i, 0, 0)

            def body(bp, m, su):
                pe.wait_ge(s_turn, su + 1)
                def k_turned(b2):
                    pe.wait_ge(s_silu, su * 6 + (b2 + 1))
                    for t8 in range(NT):
                        last = nc.tensor.transpose(nview((SA_, SB_)[b2], P)[:, t8, :], kT[:, b2, t8 * P:(t8 + 1) * P],
                                                   ident[:])
                    last.then_inc(s_kt, 1)

                def log_sums(pair, which, src, n0):
                    for a in range(2):
                        last = nc.tensor.matmul(pair[:, a, :], tri[:, which, :],
                                                src[:, n0 + a * (G // src.shape[2]):n0 + (a + 1) * (G // src.shape[2]), :]
                                                .rearrange("p n c -> p (n c)"), start=True, stop=True)
                    last.then_inc(s_pd, 1)

                def v_turned(b2):
                    pe.wait_ge(s_silu, su * 6 + (5 + b2))
                    for t8 in range(NT):
                        last = nc.tensor.transpose(nview((SB_, SC_)[b2], P)[:, t8, :], vT[:, b2, t8 * P:(t8 + 1) * P],
                                                   ident[:])
                    last.then_inc(s_vt, 1)

                def chunk_products(other, b2, s_done, freed, kept):
                    count, count1 = pe.compute_val(kept), pe.compute_val(su + b2)
                    pe.wait_ge(s_c, 32)
                    pe.wait_ge(freed, count)
                    if b2 == 1:
                        pe.wait_ge(s_end, count1)
                    for t8 in range(NT):
                        for h in range(2):
                            for cp in range(2):
                                c = 2 * t8 + cp
                                hr, cr = slice(h * DH, (h + 1) * DH), slice(cp * CH, (cp + 1) * CH)
                                last = nc.tensor.matmul(hview((SA_, SD_)[b2])[cr, t8, h, :],
                                                        kT[hr, b2, c * CH:(c + 1) * CH],
                                                        other[hr, b2, c * CH:(c + 1) * CH], start=True, stop=True)
                    last.then_inc(s_done, 1)

                z_turned(0, su)
                k_turned(0)
                z_turned(1, su)
                k_turned(1)
                z_turned(2, su)
                pe.wait_ge(s_lm, su + 1)
                pe.wait_ge(s_ktok, su * 2 + 1)
                for i, c in enumerate((TRI64, AFTER64, CHUNK0, CHUNK1)):
                    last = nc.tensor.matmul(ps[:, 0, i * NN:(i + 1) * NN], tri[:, c, :], lsu[:], start=True,
                                            stop=True)
                last.then_inc(s_sm, 1)
                pe.wait_ge(s_ktok, su * 2 + 2)
                log_sums(SB_, TRI32, Lm_d, 0)
                z_turned(3, su)
                pe.wait_ge(s_ex, su * 5 + 1)
                log_sums(SA_, TRI64, Lm_o, 0)
                pe.wait_ge(s_ex, su * 5 + 2)
                pe.wait_ge(s_lmt, su + 1)
                log_sums(SB_, AFTER64, Lm_t, 0)
                pe.wait_ge(s_ex, su * 5 + 3)
                log_sums(SA_, AFTER64, Lm_t, 16)
                z_turned(4, su)
                pe.wait_ge(s_ex, su * 5 + 4)
                v_turned(0)
                z_turned(5, su)
                z_turned(6, su)
                chunk_products(kT, 0, s_kk, s_ex, su * 5 + 5)
                z_turned(7, su)
                chunk_products(kT, 1, s_kk, s_ex, su * 5 + 5)
                v_turned(1)
                for b2 in range(2):
                    chunk_products(qT, b2, s_kq, s_T, su * 2 + (b2 + 1))
                if bp == BP - 1:
                    pe.wait_ge(s_w, m * 32 + 64)
                for i in range(6):
                    if i < 2:
                        pe.wait_ge(s_AT, su * 2 + (i + 1))
                    proj(i, su + 1, (bp + 1) % BP)
                for b2 in range(2):
                    count, count1 = pe.compute_val(su * 3 + 1), pe.compute_val(su * 6 + (11 + b2))
                    pe.wait_ge(s_c, 32)
                    pe.wait_ge(s_xt, count)
                    pe.wait_ge(s_raw, count1)
                    for n in range(b2 * 16, (b2 + 1) * 16):
                        for cp in range(2):
                            lo, hi = slice(cp * CH, cp * CH + HB), slice(cp * CH + HB, (cp + 1) * CH)
                            last = nc.tensor.matmul(nview((SA_, SD_)[b2], HB)[lo, n % 16, :], To[hi, n, :],
                                                    L[cp][hi, n, HB:CH], start=True, stop=True)
                    last.then_inc(s_p1, 1)
                for b2 in range(2):
                    count, count1 = pe.compute_val(su * 2 + (b2 + 1)), pe.compute_val(su * 3 + 2)
                    pe.wait_ge(s_c, 32)
                    pe.wait_ge(s_p1e, count)
                    pe.wait_ge(s_xt, count1)
                    for n in range(b2 * 16, (b2 + 1) * 16):
                        for cp in range(2):
                            lo = slice(cp * CH, cp * CH + HB)
                            last = nc.tensor.matmul(nview((SA_, SD_)[b2], HB)[lo, 16 + n % 16, :], Xn[lo, n, :],
                                                    Pp[lo, n, :], start=True, stop=True)
                    last.then_inc(s_p2, 1)
                for b2, pair in enumerate((SB_, SC_)):
                    count, count1, count2, count3 = (pe.compute_val(su * 2 + (b2 + 1)), pe.compute_val(su * 5 + 5),
                                                     pe.compute_val(su * 2 + (b2 + 1)), pe.compute_val(su * 3 + 3))
                    pe.wait_ge(s_c, 32)
                    pe.wait_ge(s_xt, count3)
                    pe.wait_ge(s_p2e, count)
                    pe.wait_ge(s_y0, count1)
                    pe.wait_ge(s_v0, count2)
                    for n in range(b2 * 16, (b2 + 1) * 16):
                        for cp in range(2):
                            last = nc.tensor.matmul(nview(pair, CH)[half[1 - cp], n % 16, :], Y0[half[cp], n, :],
                                                    L[cp][half[cp], n, :], start=True, stop=True)
                    last.then_inc(s_yk, 1)
                pe.wait_ge(s_yke, su * 2 + 2)
                pe.wait_ge(s_v0, su * 2 + 2)
                pe.wait_ge(s_q, su + 1)

                def heads(c):
                    for b2 in range(2):
                        for h in range(2):
                            yield b2, h, b2 * 16 + (c // 2) * 2 + h

                def y_of(c, which):
                    for b2, h, n in heads(c):
                        if b2 == which:
                            last = nc.tensor.matmul(ps[half[h], 2 * (c // 8) + b2, (c % 8) * CH:(c % 8 + 1) * CH],
                                                    R[c % 2][:, n, :], QA[c % 2][:, n, :], start=True, stop=True)
                    if which == 1:
                        last.then_inc(s_y, 1)

                for c in range(NCH):
                    cp = c % 2
                    for b2 in range(2):
                        if c:
                            pe.wait_ge(s_Se, su * (2 * NCH - 2) + (2 * c - 1 + b2))
                        for h in range(2):
                            last = nc.tensor.matmul(ps[half[cp], 4 + b2, h * DH:(h + 1) * DH],
                                                    L[cp][:, b2 * 16 + c // 2 * 2 + h, :],
                                                    R[cp][:, b2 * 16 + c // 2 * 2 + h, :], start=True, stop=True)
                        last.then_inc(s_U, 1)
                    if c:
                        y_of(c - 1, 0)
                    for b2 in range(2):
                        if c < NCH - 1:
                            pe.wait_ge(s_Ue, su * (2 * NCH) + (2 * c + b2 + 1))
                            for h in range(2):
                                last = nc.tensor.matmul(ps[half[cp], 6 + b2, h * DH:(h + 1) * DH],
                                                        KG[cp][:, b2 * 16 + c // 2 * 2 + h, :],
                                                        R[cp][:, b2 * 16 + c // 2 * 2 + h, :], start=True, stop=True)
                            last.then_inc(s_S, 1)
                    if c:
                        y_of(c - 1, 1)
                pe.wait_ge(s_Ue, su * (2 * NCH) + 2 * NCH)
                y_of(NCH - 1, 0)
                y_of(NCH - 1, 1)
            turns(pe, body)
            pe.wait_ge(s_turn, TURNS + 1)
            for i in range(2 * NG_K):
                z_turned(i, TURNS)


def judge(nc, sem, fmax, flag):
    s_v, s_g = sem("j_vector"), sem("j_all")
    with ExitStack() as st:
        ok = st.enter_context(nc.sbuf_tensor("j_ok", [P, 1], F32))
        bad = st.enter_context(nc.sbuf_tensor("j_bad", [P, 1], F32))
        bad_all = st.enter_context(nc.sbuf_tensor("j_bad_all", [P, 1], F32))
        block = st.enter_context(nc.Block())

        @block.vector
        def _(dve):
            nc.vector.tensor_scalar(ok[:], fmax[:], LIMIT, None, ALU.is_lt).then_inc(s_v, 1)
            dve.wait_ge(s_v, 1)
            nc.vector.tensor_scalar(bad[:], ok[:], 0.5, None, ALU.is_lt).then_inc(s_v, 1)
            dve.wait_ge(s_g, 1)
            nc.vector.tensor_copy(flag[:], bad_all[:]).then_inc(s_v, 1)
            dve.wait_ge(s_v, 3)

        @block.gpsimd
        def _(pool):
            pool.wait_ge(s_v, 2)
            nc.gpsimd.partition_all_reduce(bad_all[:], bad[:], P, bass.bass_isa.ReduceOp.max).then_inc(s_g, 1)


def project(nc, sem, wqkv, convp, ones2, hT, qkv_s):
    s_w, s_p, s_raw, s_tap = sem("p_weights"), sem("p_product"), sem("p_raw"), sem("p_taps")
    s_silu, s_sq, s_nn, s_rt = sem("p_silu"), sem("p_square"), sem("p_norm2"), sem("p_norm")
    s_k, s_o, s_z = sem("p_kn"), sem("p_stored"), sem("p_zero")
    s_r, s_tick, s_st = sem("p_recip"), sem("p_tick"), sem("p_unit_stored")
    with ExitStack() as st:
        w = st.enter_context(nc.sbuf_tensor("wqkv_sb", [P, 2, 3, DC, P], F32))
        cw = st.enter_context(nc.sbuf_tensor("convp_sb", [P, 2, 3, 5], F32))
        raw = st.enter_context(nc.sbuf_tensor("raw", [P, 4 + T], F32))
        tap = st.enter_context(nc.sbuf_tensor("tap", [P, T], F32))
        res = st.enter_context(nc.sbuf_tensor("res", [P, 3, T], F32))
        sq = st.enter_context(nc.sbuf_tensor("sq", [P, T], F32))
        tick2 = st.enter_context(nc.sbuf_tensor("p_tick2", [P, 8], F32))
        tick = st.enter_context(nc.sbuf_tensor("p_tick", [P, 8], F32))
        pp = st.enter_context(nc.psum_tensor("pp", [P, 2, T], F32))
        pn = st.enter_context(nc.psum_tensor("pn", [P, T], F32))
        block = st.enter_context(nc.Block())
        NB = M * B

        @block.sync
        def _(sp):
            sp.wait_ge(s_o, M * B * 48)

        @block.gpsimd
        def _(pool):

            with pool.Fori(0, M) as m:
                pool.wait_ge(s_tap, 1 + m * (B * 3))
                pool.wait_ge(s_tick, 1 + m * (2 * B + 1))
                nc.gpsimd.tensor_tensor(tick[:], ones2[:, 0:8], ones2[:, 0:8], ALU.add).then_inc(s_tick, 1)
                pool.dma_start(w[:, 0], wqkv[bass.ds(m, 1)].rearrange("a p n c k -> (a p) n c k")).then_inc(s_w, 16)
                pool.dma_start(cw[:, 0], convp[bass.ds(m, 1)].rearrange("a p n k -> (a p) n k")).then_inc(s_w, 16)
                for b in range(B):
                    pool.wait_ge(s_silu, 1 + m * (3 * B) + 3 * (b + 1))
                    pool.wait_ge(s_k, 1 + m * B + (b + 1))
                    pool.wait_ge(s_tick, 1 + m * (2 * B + 1) + (2 * b + 1))
                    nc.gpsimd.tensor_tensor(tick[:], ones2[:, 0:8], ones2[:, 0:8], ALU.add).then_inc(s_tick, 1)
                    for n in range(3):
                        pool.dma_start(qkv_s[n, b, bass.ds(m, 1)].rearrange("a p t -> (a p) t"),
                                     res[:, n, :]).then_inc(s_o, 16)
                    pool.wait_ge(s_o, m * (48 * B) + 48 * (b + 1))
                    pool.wait_ge(s_tick, 1 + m * (2 * B + 1) + (2 * b + 2))
                    nc.gpsimd.tensor_tensor(tick[:], ones2[:, 0:8], ones2[:, 0:8], ALU.add).then_inc(s_tick, 1)
                    pool.wait_ge(s_tick, 1 + m * (2 * B + 1) + (2 * b + 3))
                    nc.gpsimd.tensor_tensor(tick2[:], ones2[:, 0:8], ones2[:, 0:8], ALU.add).then_inc(s_st, 1)

        @block.scalar
        def _(act):
            with act.Fori(0, M) as m:
                act.wait_ge(s_w, m * 32 + 32)
                for b in range(B):
                    for n in range(3):
                        u = 3 * b + n
                        act.wait_ge(s_p, m * (3 * B) + (u + 1))
                        if u == 0:
                            act.wait_ge(s_z, m * 1 + 1)
                        else:
                            act.wait_ge(s_tap, 1 + m * (3 * B) + u)
                        act.wait_ge(s_silu, 1 + m * (3 * B) + u)
                        nc.scalar.activation(raw[:, 4:], pp[:, u % 2, :], ACT.Identity).then_inc(s_raw, 1)
                        nc.scalar.activation(tap[:], pp[:, u % 2, :], ACT.Identity, bias=cw[:, 0, n, 4:5],
                                             scale=cw[:, 0, n, 3:4]).then_inc(s_raw, 1)
                        act.wait_ge(s_tap, 1 + m * (3 * B) + (u + 1))
                        if n == 0:
                            act.wait_ge(s_st, 1 + m * B + b)
                        nc.scalar.activation(res[:, n, :], tap[:], ACT.Silu).then_inc(s_silu, 1)
                        if n == 1:
                            act.wait_ge(s_silu, 1 + m * (3 * B) + (u + 1))
                            act.wait_ge(s_k, 1 + m * B + b)
                            nc.scalar.activation(sq[:], res[:, 1, :], ACT.Square).then_inc(s_sq, 1)
                            act.wait_ge(s_nn, m * B + (b + 1))
                            nc.scalar.activation(sq[:], pn[:], ACT.Sqrt).then_inc(s_rt, 1)

        @block.vector
        def _(dve):
            nc.vector.memset(raw[:, 0:4], 0.0).then_inc(s_z, 1)
            with dve.Fori(0, M) as m:
                dve.wait_ge(s_w, m * 32 + 32)
                for b in range(B):
                    for n in range(3):
                        u = 3 * b + n
                        dve.wait_ge(s_raw, 1 + m * (6 * B) + (2 * u + 2))
                        for i, k in enumerate((2, 1, 0)):
                            ins = nc.vector.scalar_tensor_tensor(
                                out=tap[:], in0=raw[:, 1 + k:1 + k + T], scalar=cw[:, 0, n, k:k + 1],
                                in1=tap[:], op0=ALU.mult, op1=ALU.add)
                            if i < 2:
                                ins.then_inc(s_r, 1)
                                dve.wait_ge(s_r, m * (3 * B * 2 + 2 * B) + (6 + 2) * b + 2 * n + (2 if n == 2 else 0)
                                            + i + 1)
                            elif u == 3 * B - 1:
                                ins.then_inc(s_tap, 1)
                            else:
                                ins.then_inc(s_tap, 1)
                        if n == 1:
                            dve.wait_ge(s_rt, m * B + (b + 1))
                            nc.vector.tensor_scalar(sq[:], sq[:], NORM_EPS, None, ALU.max).then_inc(s_r, 1)
                            dve.wait_ge(s_r, m * (8 * B) + (8 * b + 5))
                            nc.vector.reciprocal(sq[:], sq[:]).then_inc(s_r, 1)
                            dve.wait_ge(s_r, m * (8 * B) + (8 * b + 6))
                            nc.vector.tensor_tensor(res[:, 1, :], res[:, 1, :], sq[:], ALU.mult).then_inc(s_k, 1)
                dve.wait_ge(s_tap, 1 + m * (3 * B) + 3 * B)
                dve.wait_ge(s_k, 1 + m * B + B)
                nc.vector.memset(raw[:, 0:4], 0.0).then_inc(s_z, 1)

        @block.tensor
        def _(pe):
            pe.sem_inc(s_tap, 1)
            pe.sem_inc(s_silu, 1)
            pe.sem_inc(s_st, 1)
            pe.sem_inc(s_k, 1)
            pe.sem_inc(s_raw, 1)
            pe.sem_inc(s_tick, 1)
            with pe.Fori(0, M) as m:
                pe.wait_ge(s_w, m * 32 + 32)
                for b in range(B):
                    for n in range(3):
                        u = 3 * b + n
                        if u < 2:
                            pe.wait_ge(s_raw, 1 + m * (6 * B))
                        else:
                            pe.wait_ge(s_raw, 1 + m * (6 * B) + 2 * (u - 1))
                        for g in range(GH):
                            for dc in range(DC):
                                last = nc.tensor.matmul(pp[:, u % 2, g * G:(g + 1) * G], w[:, 0, n, dc, :],
                                                        hT[:, dc, b * T + g * G:b * T + (g + 1) * G],
                                                        start=(dc == 0), stop=(dc == DC - 1))
                        last.then_inc(s_p, 1)
                    pe.wait_ge(s_sq, m * B + (b + 1))
                    if b:
                        pe.wait_ge(s_rt, m * B + b)
                    for g in range(GH):
                        last = nc.tensor.matmul(pn[:, g * G:(g + 1) * G], ones2[:], sq[:, g * G:(g + 1) * G],
                                                start=True, stop=True)
                    last.then_inc(s_nn, 1)


def scan(nc, sem, ones2, qkv_s, ab_s, y_s):
    TB, HI = 64, DH // 2
    NBK = T // TB
    s_tick, s_st = sem("s_tick"), sem("s_block_stored")
    s_ab, s_in, s_d, s_y, s_o = sem("s_ab"), sem("s_in"), sem("s_step"), sem("s_y"), sem("s_out")
    with ExitStack() as st:
        al = st.enter_context(nc.sbuf_tensor("alpha", [P, T], F32))
        be = st.enter_context(nc.sbuf_tensor("beta", [P, T], F32))
        S = st.enter_context(nc.sbuf_tensor("state", [P, HI, DH], F32))
        W = st.enter_context(nc.sbuf_tensor("outer", [P, HI, DH], F32))
        r = st.enter_context(nc.sbuf_tensor("seen", [P, HI], F32))
        u = st.enter_context(nc.sbuf_tensor("update", [P, HI], F32))
        qb = st.enter_context(nc.sbuf_tensor("q_blk", [P, DH, TB], F32))
        kb = st.enter_context(nc.sbuf_tensor("k_blk", [P, DH, TB], F32))
        vb = st.enter_context(nc.sbuf_tensor("v_blk", [P, HI, TB], F32))
        yb = st.enter_context(nc.sbuf_tensor("y_blk", [P, HI, TB], F32))
        tick2 = st.enter_context(nc.sbuf_tensor("s_tick2", [P, 8], F32))
        tick = st.enter_context(nc.sbuf_tensor("s_tick", [P, 8], F32))
        block = st.enter_context(nc.Block())
        NS = 9

        @block.gpsimd
        def _(pool):
            for half in range(2):
                rows = slice(half * 64, half * 64 + 64)
                for b in range(B):
                    pr = slice(half * 64 + b * H, half * 64 + (b + 1) * H)
                    pool.dma_start(al[pr, :], ab_s[0:H, b, :]).then_inc(s_ab, 16)
                    pool.dma_start(be[pr, :], ab_s[H:2 * H, b, :]).then_inc(s_ab, 16)

            with pool.Fori(0, NBK) as n:
                pool.wait_ge(s_y, 1 + n)
                pool.wait_ge(s_tick, 1 + n * 3)
                nc.gpsimd.tensor_tensor(tick[:], ones2[:, 0:8], ones2[:, 0:8], ALU.add).then_inc(s_tick, 1)
                for half in range(2):
                    for b in range(B):
                        pr = slice(half * 64 + b * H, half * 64 + (b + 1) * H)
                        for dst, i in ((qb, 0), (kb, 1)):
                            pool.dma_start(dst[pr], qkv_s[i, b].rearrange("m (a j) t -> (m a) j t", a=2)
                                         [:, :, bass.ds(n * TB, TB)]).then_inc(s_in, 16)
                        pool.dma_start(vb[pr], qkv_s[2, b].rearrange("m (a j) t -> (m a) j t", a=2)
                                     [:, half * HI:(half + 1) * HI, bass.ds(n * TB, TB)]).then_inc(s_in, 16)
                pool.wait_ge(s_y, 1 + n + 1)
                pool.wait_ge(s_tick, 1 + n * 3 + 1)
                nc.gpsimd.tensor_tensor(tick[:], ones2[:, 0:8], ones2[:, 0:8], ALU.add).then_inc(s_tick, 1)
                for half in range(2):
                    for b in range(B):
                        pr = slice(half * 64 + b * H, half * 64 + (b + 1) * H)
                        pool.dma_start(y_s[b].rearrange("m (a j) t -> (m a) j t", a=2)
                                     [:, half * HI:(half + 1) * HI, bass.ds(n * TB, TB)], yb[pr]).then_inc(s_o, 16)
                pool.wait_ge(s_o, n * 128 + 128)
                pool.wait_ge(s_tick, 1 + n * 3 + 2)
                nc.gpsimd.tensor_tensor(tick[:], ones2[:, 0:8], ones2[:, 0:8], ALU.add).then_inc(s_tick, 1)
                pool.wait_ge(s_tick, 1 + n * 3 + 3)
                nc.gpsimd.tensor_tensor(tick2[:], ones2[:, 0:8], ones2[:, 0:8], ALU.add).then_inc(s_st, 1)

        @block.vector
        def _(dve):
            dve.sem_inc(s_y, 1)
            dve.sem_inc(s_st, 1)
            dve.sem_inc(s_tick, 1)
            nc.vector.memset(S[:], 0.0).then_inc(s_d, 1)
            dve.wait_ge(s_ab, 16 * 16)
            with dve.Fori(0, NBK) as n:
                dve.wait_ge(s_in, n * (24 * 16) + 24 * 16)
                dve.wait_ge(s_st, 1 + n)
                nc.vector.memset(r[:], 0.0)
                with dve.Fori(0, TB) as t:
                    tok = n * TB + t
                    base = (n * TB + t) * NS + 1
                    k_row = kb[:, :, bass.ds(t, 1)].rearrange("p j a -> p a j").broadcast_to([P, HI, DH])
                    q_row = qb[:, :, bass.ds(t, 1)].rearrange("p j a -> p a j").broadcast_to([P, HI, DH])
                    u_col = u[:, :].rearrange("p (i a) -> p i a", a=1).broadcast_to([P, HI, DH])
                    dve.wait_ge(s_d, base)
                    nc.vector.tensor_tensor(W[:], S[:], k_row, ALU.mult).then_inc(s_d, 1)
                    dve.wait_ge(s_d, base + 1)
                    nc.vector.tensor_reduce(r[:], W[:], AX_X, ALU.add).then_inc(s_d, 1)
                    dve.wait_ge(s_d, base + 2)
                    nc.vector.scalar_tensor_tensor(out=u[:], in0=r[:], scalar=al[:, bass.ds(tok, 1)],
                                                   in1=vb[:, :, bass.ds(t, 1)].rearrange("p i a -> p (i a)"),
                                                   op0=ALU.mult, op1=ALU.subtract).then_inc(s_d, 1)
                    dve.wait_ge(s_d, base + 3)
                    nc.vector.tensor_scalar(u[:], u[:], be[:, bass.ds(tok, 1)], -1.0, ALU.mult,
                                            ALU.mult).then_inc(s_d, 1)
                    dve.wait_ge(s_d, base + 4)
                    nc.vector.tensor_tensor(W[:], u_col, k_row, ALU.mult).then_inc(s_d, 1)
                    dve.wait_ge(s_d, base + 5)
                    nc.vector.scalar_tensor_tensor(out=S[:].rearrange("p i j -> p (i j)"),
                                                   in0=S[:].rearrange("p i j -> p (i j)"),
                                                   scalar=al[:, bass.ds(tok, 1)],
                                                   in1=W[:].rearrange("p i j -> p (i j)"), op0=ALU.mult,
                                                   op1=ALU.add).then_inc(s_d, 1)
                    dve.wait_ge(s_d, base + 6)
                    nc.vector.tensor_scalar(S[:], S[:], CLIP, -CLIP, ALU.min, ALU.max).then_inc(s_d, 1)
                    dve.wait_ge(s_d, base + 7)
                    nc.vector.tensor_tensor(W[:], S[:], q_row, ALU.mult).then_inc(s_d, 1)
                    dve.wait_ge(s_d, base + 8)
                    nc.vector.tensor_reduce(yb[:, :, bass.ds(t, 1)].rearrange("p i a -> p (i a)"), W[:], AX_X,
                                            ALU.add).then_inc(s_d, 1)
                dve.wait_ge(s_d, n * (TB * NS) + (TB * NS + 1))
                nc.vector.tensor_copy(r[:], u[:]).then_inc(s_y, 1)


def high(nc, dst, src):
    return nc.vector.tensor_copy(dst.bitcast(F32R), src)


def low(nc, dst, src, hi):
    return nc.vector.tensor_tensor(dst.bitcast(F32R), src, hi, ALU.subtract)


def three(nc, dst, lhs, rhs, first, last):
    for n, (a, b) in enumerate(((0, 0), (0, 1), (1, 0))):
        ins = nc.tensor.matmul(dst, lhs(a).bitcast(F32R), rhs(b).bitcast(F32R),
                               start=first and n == 0, stop=last and n == 2)
    return ins


def attn_out(nc, sem, x, y_s, wg, bg, wo, gates_s, ident, modT, hT, gates, x1, h2T):
    s_st, s_ag, s_sq, s_rs = sem("n_stats"), sem("n_moments"), sem("n_root"), sem("n_rstd")
    s_n, s_tn, s_e = sem("n_normed"), sem("n_turned"), sem("n_kept")
    s_y = [sem("o_y_even"), sem("o_y_odd")]
    s_w, s_l, s_gp, s_g = sem("o_weights"), sem("o_loaded"), sem("o_gate_product"), sem("o_gate")
    s_m, s_op, s_t, s_x1 = sem("o_gated"), sem("o_product"), sem("o_scaled"), sem("o_x1")
    s_hi, s_ws, s_hs, s_ys = sem("o_high"), sem("o_weights_split"), sem("o_input_split"), sem("o_gated_split")
    with ExitStack() as st:
        def sb(name, *shape):
            return st.enter_context(nc.sbuf_tensor(name, [P, *shape], F32))

        bg_sb = sb("bg_sb", M)
        wg_s, wo_s = sb("wg_split", 2, DC, C), sb("wo_split", 2, M, D)
        h_s, y_sp = sb("h_split", 2, 2, DC, G), sb("y_split", 2, M, G)
        y = sb("y", 2, M, G)
        spare = y[:, 1].rearrange("p m t -> p (m t)")
        wg_sb = spare[:, 0:DC * C].rearrange("p (c k) -> p c k", c=DC)
        wo_sb = spare[:, DC * C:].rearrange("p (m d) -> p m d", m=M)
        g_sb, tmp = sb("g_sb", 2, G), sb("o_tmp", 2, D)
        stats, mv, eps = sb("stats2", B * NT, 6), sb("mv2", B * NT, 2), sb("eps2", 1)
        sd, rstd, xn = sb("sd2", B * NT), sb("rstd2", B * NT), sb("xn", GT, D)
        pt = st.enter_context(nc.psum_tensor("pt2", [P, DC, G], F32))
        pg = st.enter_context(nc.psum_tensor("o_pg", [P, 2, G], F32))
        po = st.enter_context(nc.psum_tensor("o_po", [P, 4, G], F32))
        block = st.enter_context(nc.Block())
        NG = B * GH

        @block.sync
        def _(sp):
            def load_y(g):
                sp.dma_start(y[:, g % 2], y_s[g // GH].rearrange("m p t -> p m t")
                             [:, :, (g % GH) * G:(g % GH + 1) * G]).then_inc(s_y[g % 2], 16)

            sp.dma_start(wg_sb, wg).then_inc(s_w, 16)
            sp.dma_start(wo_sb, wo).then_inc(s_w, 16)
            sp.dma_start(bg_sb[:], bg).then_inc(s_l, 16)
            load_y(0)
            sp.dma_start(x1[:], x).then_inc(s_l, 16)
            sp.dma_start(gates[:].rearrange("p a b d -> p (a b d)"),
                         gates_s.broadcast_to([P, 2 * B * D])).then_inc(s_l, 16)
            sp.wait_ge(s_ws, 2)
            load_y(1)
            for g in range(2, NG):
                sp.wait_ge(s_ys, M * (g - 1))
                load_y(g)

        @block.scalar
        def _(act):
            act.wait_ge(s_l, 48)
            for g in range(NG + 2):
                if g >= 2:
                    act.wait_ge(s_ag, 1 + GT * (g - 1))
                    ts = slice((g - 2) * GT, (g - 1) * GT)
                    nc.scalar.activation(sd[:, ts], mv[:, ts, 1], ACT.Sqrt, bias=eps[:, 0:1]).then_inc(s_sq, 1)
                if g < NG:
                    for m in range(M):
                        i = g * M + m
                        act.wait_ge(s_gp, i + 1)
                        if i >= 2:
                            act.wait_ge(s_m, i - 1)
                        nc.scalar.activation(g_sb[:, i % 2, :], pg[:, i % 2, :], ACT.Silu,
                                             bias=bg_sb[:, m:m + 1]).then_inc(s_g, 1)

        @block.gpsimd
        def _(pool):
            for g in range(NG):
                pool.wait_ge(s_y[g % 2], 16 * (g // 2 + 1))
                for m in range(M):
                    i = g * M + m
                    pool.wait_ge(s_g, i + 1)
                    nc.gpsimd.tensor_tensor(y[:, g % 2, m, :], y[:, g % 2, m, :], g_sb[:, i % 2, :],
                                            ALU.mult).then_inc(s_m, 1)

        @block.vector
        def _(dve):
            made = 0

            def split(dst, src, s_done):
                nonlocal made
                made += 1
                high(nc, dst[0], src).then_inc(s_hi, 1)
                dve.wait_ge(s_hi, made)
                low(nc, dst[1], src, dst[0]).then_inc(s_done, 1)

            def split_h(g):
                split([h_s[:, g % 2, a] for a in range(2)], hT[:, :, g * G:(g + 1) * G], s_hs)

            def normalise(g):
                dve.wait_ge(s_sq, g + 1)
                ts = slice(g * GT, (g + 1) * GT)
                nc.vector.reciprocal(rstd[:, ts], sd[:, ts]).then_inc(s_rs, 1)
                dve.wait_ge(s_rs, g + 1)
                for j in range(GT):
                    i = g * GT + j
                    last = nc.vector.tensor_scalar(xn[:, j, :], x1[:, i, :], mv[:, i, 0:1], rstd[:, i:i + 1],
                                                   ALU.subtract, ALU.mult)
                last.then_inc(s_n, 1)

            def modulate(g):
                dve.wait_ge(s_tn, g + 1)
                b = g // GH
                for dc in range(DC):
                    last = nc.vector.tensor_scalar(h2T[:, dc, g * G:(g + 1) * G], pt[:, dc, :],
                                                   modT[:, 2 * CB + dc, b:b + 1], modT[:, 2 * SB + dc, b:b + 1],
                                                   ALU.mult, ALU.add)
                last.then_inc(s_e, 1)

            nc.vector.memset(eps[:], LN_EPS).then_inc(s_ag, 1)
            split_h(0)
            dve.wait_ge(s_w, 32)
            split([wg_s[:, a] for a in range(2)], wg_sb, s_ws)
            split([wo_s[:, a] for a in range(2)], wo_sb, s_ws)
            split_h(1)
            for g in range(NG):
                for m in range(M):
                    dve.wait_ge(s_m, g * M + m + 1)
                    split([y_sp[:, a, m, :] for a in range(2)], y[:, g % 2, m, :], s_ys)
                if g + 2 < NG:
                    dve.wait_ge(s_gp, M * (g + 1))
                    split_h(g + 2)
                if g == 0:
                    dve.wait_ge(s_l, 48)
                else:
                    normalise(g - 1)
                for j in range(GT):
                    i = g * GT + j
                    dve.wait_ge(s_op, i + 1)
                    if i >= 2:
                        dve.wait_ge(s_x1, i - 1)
                    nc.vector.tensor_tensor(tmp[:, i % 2, :], po[:, i % 4, 0:D], gates[:, 0, g // GH, :],
                                            ALU.mult).then_inc(s_t, 1)
                    dve.wait_ge(s_t, i + 1)
                    nc.vector.tensor_tensor(x1[:, i, :], x1[:, i, :], tmp[:, i % 2, :], ALU.add).then_inc(s_x1, 1)
                    dve.wait_ge(s_x1, i + 1)
                    nc.vector.bn_stats(stats[:, i, :], x1[:, i, :]).then_inc(s_st, 1)
                    dve.wait_ge(s_st, i + 1)
                    nc.vector.bn_aggr(mv[:, i, :], stats[:, i, :]).then_inc(s_ag, 1)
                if g:
                    modulate(g - 1)
            normalise(NG - 1)
            modulate(NG - 1)
            dve.wait_ge(s_e, NG)

        @block.tensor
        def _(pe):
            def gate(g):
                pe.wait_ge(s_hs, g + 1)
                for m in range(M):
                    i = g * M + m
                    if i >= 2:
                        pe.wait_ge(s_g, i - 1)
                    for dc in range(DC):
                        last = three(nc, pg[:, i % 2, :], lambda a: wg_s[:, a, dc, m * P:(m + 1) * P],
                                     lambda b: h_s[:, g % 2, b, dc, :], dc == 0, dc == DC - 1)
                    last.then_inc(s_gp, 1)

            def product(g):
                pe.wait_ge(s_ys, M * (g + 1))
                for j in range(GT):
                    i = g * GT + j
                    if i >= 4:
                        pe.wait_ge(s_t, i - 3)
                    for m in range(M):
                        last = three(nc, po[:, i % 4, 0:D], lambda a: y_sp[:, a, m, j * P:(j + 1) * P],
                                     lambda b: wo_s[:, b, m, :], m == 0, m == M - 1)
                    last.then_inc(s_op, 1)

            def turned(g):
                pe.wait_ge(s_n, g + 1)
                if g:
                    pe.wait_ge(s_e, g)
                for j in range(GT):
                    for dc in range(DC):
                        last = nc.tensor.transpose(pt[:, dc, j * P:(j + 1) * P], xn[:, j, dc * P:(dc + 1) * P],
                                                   ident[:])
                last.then_inc(s_tn, 1)

            pe.wait_ge(s_ws, 2)
            for g in range(NG + 2):
                if g < NG:
                    gate(g)
                if 1 <= g <= NG:
                    product(g - 1)
                if g >= 2:
                    turned(g - 2)


def route(nc, sem, ident, rw_sb, b2, h2T, comb, acc):
    N = B * NT
    s_b, s_l = sem("r_loaded"), sem("r_logits")
    s_v, s_x, s_c, s_cc = sem("r_vector"), sem("r_exp"), sem("r_comb_turned"), sem("r_comb_kept")
    s_b2, s_a = sem("r_bias"), sem("r_acc")
    with ExitStack() as st:
        b2_sb = st.enter_context(nc.sbuf_tensor("b2_sb", [E, D], F32))
        lg = st.enter_context(nc.sbuf_tensor("logits", [P, N, E], F32))
        rank = st.enter_context(nc.sbuf_tensor("rank", [P, N, E], F32))
        hit = st.enter_context(nc.sbuf_tensor("hit", [P, N, E], F32))
        one1 = st.enter_context(nc.sbuf_tensor("first", [P, N, E], F32))
        one2 = st.enter_context(nc.sbuf_tensor("second", [P, N, E], F32))
        best = st.enter_context(nc.sbuf_tensor("best", [P, 2, N], F32))
        pos = st.enter_context(nc.sbuf_tensor("pos", [P, N], F32))
        ex = st.enter_context(nc.sbuf_tensor("ex", [P, 4, N], F32))
        combT = st.enter_context(nc.sbuf_tensor("combT", [E, N * P], F32))
        pt = st.enter_context(nc.psum_tensor("r_pt", [P, 2, DC, G], F32))
        pl = st.enter_context(nc.psum_tensor("pl2", [P, N, E], F32))
        block = st.enter_context(nc.Block())
        NG = B * GH

        def wide(ap):
            return ap.rearrange("p (n a) -> p n a", a=1).broadcast_to([P, N, E])

        @block.sync
        def _(sp):
            sp.dma_start(b2_sb[:], b2).then_inc(s_b, 16)

        @block.scalar
        def _(act):
            act.wait_ge(s_v, E + 10)
            nc.scalar.activation(ex[:, 1, :], ex[:, 0, :], ACT.Exp).then_inc(s_x, 1)

        @block.vector
        def _(dve):
            v = 0

            def step(ins):
                nonlocal v
                v += 1
                ins.then_inc(s_v, 1)
                dve.wait_ge(s_v, v)

            for e in range(E):
                step(nc.vector.memset(rank[:, :, e], float(E - e)))
            dve.wait_ge(s_l, 1)
            step(nc.vector.tensor_copy(lg[:], pl[:]))
            for n, (one, m) in enumerate(((one1, best[:, 0, :]), (one2, best[:, 1, :]))):
                step(nc.vector.tensor_reduce(m, lg[:], AX_X, ALU.max))
                if n == 1:
                    step(nc.vector.tensor_tensor(ex[:, 0, :], best[:, 1, :], best[:, 0, :], ALU.subtract))
                step(nc.vector.tensor_tensor(hit[:], lg[:], wide(m), ALU.is_equal))
                step(nc.vector.tensor_tensor(hit[:], hit[:], rank[:], ALU.mult))
                step(nc.vector.tensor_reduce(pos[:], hit[:], AX_X, ALU.max))
                step(nc.vector.tensor_tensor(one[:], hit[:], wide(pos[:]), ALU.is_equal))
                if n == 0:
                    step(nc.vector.tensor_scalar(hit[:], one[:], -3.0e38, None, ALU.mult))
                    step(nc.vector.tensor_tensor(lg[:], lg[:], hit[:], ALU.add))
            dve.wait_ge(s_x, 1)
            step(nc.vector.tensor_scalar(ex[:, 2, :], ex[:, 1, :], 1.0, None, ALU.add))
            step(nc.vector.reciprocal(ex[:, 3, :], ex[:, 2, :]))
            step(nc.vector.tensor_tensor(ex[:, 2, :], ex[:, 1, :], ex[:, 3, :], ALU.mult))
            step(nc.vector.tensor_tensor(one1[:], one1[:], wide(ex[:, 3, :]), ALU.mult))
            step(nc.vector.tensor_tensor(one2[:], one2[:], wide(ex[:, 2, :]), ALU.mult))
            nc.vector.tensor_tensor(comb[:], one1[:], one2[:], ALU.add).then_inc(s_a, 1)
            dve.wait_ge(s_a, 1)
            for g in range(NG):
                dve.wait_ge(s_c, g + 1)
                nc.vector.tensor_copy(combT[:, g * G:(g + 1) * G], pt[0:E, g % 2, 0, :]).then_inc(s_cc, 1)
            for g in range(N // 2):
                dve.wait_ge(s_b2, g + 1)
                nc.vector.tensor_copy(acc[:, 2 * g:2 * g + 2, :],
                                      pt[:, g % 2, 1, :].rearrange("p (j d) -> p j d", j=2)).then_inc(s_a, 1)
            dve.wait_ge(s_a, 1 + N // 2)

        @block.tensor
        def _(pe):
            for g in range(NG):
                for j in range(g * GT, (g + 1) * GT):
                    for dc in range(DC):
                        last = nc.tensor.matmul(pl[:, j, :], h2T[:, dc, j * P:(j + 1) * P], rw_sb[:, dc, :],
                                                start=(dc == 0), stop=(dc == DC - 1))
            last.then_inc(s_l, 1)
            pe.wait_ge(s_a, 1)
            for g in range(NG):
                if g >= 2:
                    pe.wait_ge(s_cc, g - 1)
                for j in range(GT):
                    last = nc.tensor.transpose(pt[0:E, g % 2, 0, j * P:(j + 1) * P], comb[:, g * GT + j, :], ident[:])
                last.then_inc(s_c, 1)
            pe.wait_ge(s_b, 16)
            for g in range(N // 2):
                pe.wait_ge(s_cc, g // 2 + 1)
                if g >= 2:
                    pe.wait_ge(s_a, g)
                for j in range(2):
                    last = nc.tensor.matmul(pt[:, g % 2, 1, j * D:(j + 1) * D],
                                            combT[:, (2 * g + j) * P:(2 * g + j + 1) * P], b2_sb[:],
                                            start=True, stop=True)
                last.then_inc(s_b2, 1)


def experts(nc, sem, w1, b1, w2, h2T, comb, acc):
    s_w1, s_w2, s_b1 = sem("e_w1_loaded"), sem("e_w2_loaded"), [sem("e_b1_even"), sem("e_b1_odd")]
    s_ws1, s_ws2 = sem("e_w1_split"), sem("e_w2_split")
    s_h, s_g, s_y, s_a = sem("e_up"), sem("e_gelu"), sem("e_down"), sem("e_acc")
    s_hi, s_in, s_gs = sem("e_high"), sem("e_input_split"), sem("e_gelu_split")
    with ExitStack() as st:
        def sb(name, *shape):
            return st.enter_context(nc.sbuf_tensor(name, [P, *shape], F32))

        w1_s, w2_s = sb("w1_split", 2, DC, F), sb("w2_split", 2, FC, D)
        h2_s = sb("h2_split", 2, DC, B * T)
        hm_s = sb("hm_split", 2, FC, G)
        w1_sb, b1_sb = sb("w1_sb", DC, F), sb("b1_sb", 2, FC)
        spare = h2T[:].rearrange("p a t -> p (a t)")
        w2_sb = spare[:, 0:FC * D].rearrange("p (f d) -> p f d", f=FC)
        hm = spare[:, FC * D:FC * D + 2 * FC * G].rearrange("p (i f t) -> p i f t", i=2, f=FC)
        ph = st.enter_context(nc.psum_tensor("ph", [P, 4, G], F32))
        py = st.enter_context(nc.psum_tensor("py", [P, 4, G], F32))
        block = st.enter_context(nc.Block())
        NG = B * GH
        SPLITS = 2 * NG * FC + 4

        @block.sync
        def _(sp):
            for e in range(E):
                if e:
                    sp.wait_ge(s_ws1, e)
                sp.dma_start(w1_sb[:], w1[e]).then_inc(s_w1, 16)
                if e >= 2:
                    sp.wait_ge(s_g, 1 + (e - 1) * NG * FC)
                sp.dma_start(b1_sb[:, e % 2], b1[e]).then_inc(s_b1[e % 2], 16)
                if e:
                    sp.wait_ge(s_ws2, e)
                else:
                    sp.wait_ge(s_in, NG)
                sp.dma_start(w2_sb, w2[e]).then_inc(s_w2, 16)

        @block.scalar
        def _(act):
            act.wait_ge(s_in, NG)
            with act.Fori(0, E // 2) as e2:
                for p in range(2):
                    act.wait_ge(s_b1[p], e2 * 16 + 16)
                    for g in range(NG):
                        i = p * NG + g
                        act.wait_ge(s_gs, 1 + e2 * (2 * NG * FC) + max(i - 1, 0) * FC)
                        for f in range(FC):
                            act.wait_ge(s_h, e2 * (2 * NG * FC) + (i * FC + f + 1))
                            nc.scalar.activation(hm[:, i % 2, f, :], ph[:, f, :], ACT.Gelu,
                                                 bias=b1_sb[:, p, f:f + 1]).then_inc(s_g, 1)

        @block.vector
        def _(dve):
            for g in range(NG):
                gs = slice(g * G, (g + 1) * G)
                high(nc, h2_s[:, 0, :, gs], h2T[:, :, gs]).then_inc(s_hi, 1)
                dve.wait_ge(s_hi, g + 1)
                low(nc, h2_s[:, 1, :, gs], h2T[:, :, gs], h2_s[:, 0, :, gs]).then_inc(s_in, 1)

            with dve.Fori(0, E // 2) as e2:
                made = 0

                def split(dst, src, s_done):
                    nonlocal made
                    made += 1
                    high(nc, dst[0], src).then_inc(s_hi, 1)
                    dve.wait_ge(s_hi, e2 * SPLITS + (NG + made))
                    low(nc, dst[1], src, dst[0]).then_inc(s_done, 1)

                def split_w1(p):
                    dve.wait_ge(s_w1, e2 * 32 + 16 * (p + 1))
                    if p == 1:
                        dve.wait_ge(s_h, e2 * (2 * NG * FC) + NG * FC)
                    split((w1_s[:, 0], w1_s[:, 1]), w1_sb[:], s_ws1)

                for i in range(2 * NG + 1):
                    if i == 0:
                        split_w1(0)
                    if i == NG - 1:
                        split_w1(1)
                    if i >= 1:
                        p, g = (i - 1) // NG, (i - 1) % NG
                        for j in range(GT):
                            dve.wait_ge(s_y, 1 + e2 * (2 * NG * GT) + ((i - 1) * GT + j + 1))
                            if g == 0 and j == 0:
                                dve.wait_ge(s_a, 1 + e2 * (2 * NG * GT) + (i - 1) * GT)
                            nc.vector.scalar_tensor_tensor(
                                out=acc[:, g * GT + j, :], in0=py[:, j, 0:D],
                                scalar=comb[:, g * GT + j, bass.ds(e2 * 2 + p, 1)], in1=acc[:, g * GT + j, :],
                                op0=ALU.mult, op1=ALU.add).then_inc(s_a, 1)
                    if i in (0, NG):
                        dve.wait_ge(s_w2, e2 * 32 + 16 * (i // NG + 1))
                        split((w2_s[:, 0], w2_s[:, 1]), w2_sb, s_ws2)
                    if i < 2 * NG:
                        for f in range(FC):
                            dve.wait_ge(s_g, 1 + e2 * (2 * NG * FC) + (i * FC + f + 1))
                            split((hm_s[:, 0, f, :], hm_s[:, 1, f, :]), hm[:, i % 2, f, :], s_gs)
            dve.wait_ge(s_a, 1 + E * NG * GT)

        @block.tensor
        def _(pe):
            pe.sem_inc(s_y, 1)
            pe.sem_inc(s_a, 1)
            pe.sem_inc(s_g, 1)
            pe.sem_inc(s_gs, 1)

            def up(e2, i, p, g):
                if g == 0:
                    pe.wait_ge(s_ws1, e2 * 2 + (p + 1))
                if p == 0:
                    pe.wait_ge(s_in, g + 1)
                gs = slice(g * G, (g + 1) * G)
                for f in range(FC):
                    pe.wait_ge(s_g, 1 + e2 * (2 * NG * FC) + max((i - 1) * FC + f + 1, 0))
                    fs = slice(f * P, (f + 1) * P)
                    for dc in range(DC):
                        last = three(nc, ph[:, f, :], lambda a: w1_s[:, a, dc, fs], lambda b: h2_s[:, b, dc, gs],
                                     dc == 0, dc == DC - 1)
                    last.then_inc(s_h, 1)

            def down(e2, i, p, g):
                if g == 0:
                    pe.wait_ge(s_ws2, e2 * 2 + (p + 1))
                pe.wait_ge(s_gs, 1 + e2 * (2 * NG * FC) + (i + 1) * FC)
                for j in range(GT):
                    pe.wait_ge(s_a, 1 + e2 * (2 * NG * GT) + max((i - 1) * GT + j + 1, 0))
                    js = slice(j * P, (j + 1) * P)
                    for f in range(FC):
                        last = three(nc, py[:, j, 0:D], lambda a: hm_s[:, a, f, js], lambda b: w2_s[:, b, f, :],
                                     f == 0, f == FC - 1)
                    last.then_inc(s_y, 1)

            with pe.Fori(0, E // 2) as e2:
                for i in range(2 * NG + 1):
                    if i < 2 * NG:
                        up(e2, i, i // NG, i % NG)
                    if i >= 1:
                        down(e2, i - 1, (i - 1) // NG, (i - 1) % NG)


def finish(nc, sem, gates, x1, acc, out):
    s_m, s_a, s_o = sem("f_scaled"), sem("f_sum"), sem("f_stored")
    with ExitStack() as st:
        block = st.enter_context(nc.Block())

        @block.sync
        def _(sp):
            for b in range(B):
                sp.wait_ge(s_a, (b + 1) * NT)
                sp.dma_start(out[:, b * NT:(b + 1) * NT, :], acc[:, b * NT:(b + 1) * NT, :]).then_inc(s_o, 16)
            sp.wait_ge(s_o, 16 * B)

        @block.vector
        def _(dve):
            for i in range(B * NT):
                nc.vector.tensor_tensor(acc[:, i, :], acc[:, i, :], gates[:, 1, i // NT, :], ALU.mult).then_inc(s_m, 1)
            for i in range(B * NT):
                dve.wait_ge(s_m, i + 1)
                nc.vector.tensor_tensor(acc[:, i, :], acc[:, i, :], x1[:, i, :], ALU.add).then_inc(s_a, 1)


def kernel(**inputs):
    import numpy as np
    import concourse.bacc as bacc
    from concourse.bass_utils import run_bass_kernel_spmd

    a = {k[3:]: np.asarray(v) for k, v in inputs.items()}

    def cols(w):
        return w.T.reshape(w.shape[1] // P, P, w.shape[0]).transpose(1, 0, 2)

    wqkv = np.stack([cols(a["attn_W" + n]).reshape(P, DC, M, P) for n in "qkv"])
    convp = np.stack([np.concatenate([a[f"attn_conv_{n}_w"].reshape(C, 4), a[f"attn_conv_{n}_b"].reshape(C, 1)], 1)
                      .reshape(M, P, 5) for n in "qkv"])
    ident = np.eye(P, dtype=np.float32)
    ones2 = np.kron(np.eye(2, dtype=np.float32), np.ones((DH, DH), np.float32))
    r, c = np.arange(P)[:, None], np.arange(P)[None, :]
    same64, same32 = r // CH == c // CH, r // HB == c // HB
    tri = np.stack([same64 & (r <= c), same32 & (r <= c), same64 & (r > c), (r // CH == 0) & (c >= 0),
                    (r // CH == 1) & (c >= 0)], 1).astype(np.float32)
    c32, c64 = np.arange(HB)[None, :], np.arange(CH)[None, :]
    mask = np.concatenate([r % HB > c32, (r % HB > c32) | (r // HB % 2 == 1), r % CH <= c64], 1).astype(np.float32)
    tiles = lambda z: z.reshape(B * NT, P, D).transpose(1, 0, 2)
    arrays = {
        "x": tiles(a["attn_hidden_states"]),
        "cT": a["c"].T.reshape(DC, P, B).transpose(1, 0, 2),
        "wmod": a["wmod"].reshape(DC, P, 6 * D).transpose(1, 0, 2),
        "wqkv": wqkv.transpose(3, 1, 0, 2, 4),
        "convp": convp.transpose(1, 2, 0, 3),
        "wg": cols(a["attn_Wg"]),
        "bg": a["attn_bg"].reshape(M, P).T,
        "wab": cols(np.concatenate([a["attn_Wa"], a["attn_Wb"]], 0)),
        "bab": np.concatenate([a["attn_ba"], a["attn_bb"]]).reshape(2 * H, 1),
        "wo": cols(a["attn_Wo"]),
        "rw": cols(a["ffn_router_w"]),
        "w1": np.stack([cols(w) for w in a["ffn_w1"]]),
        "b1": a["ffn_b1"].reshape(E, FC, P).transpose(0, 2, 1),
        "w2": np.stack([cols(w) for w in a["ffn_w2"]]),
        "b2": a["ffn_b2"],
        "ident": ident,
        "ones2": ones2,
        "tri": tri,
        "mask": mask,
    }
    nc = bacc.Bacc("TRN2", target_bir_lowering=False, num_devices=1)
    feeds, args = {}, []
    for name, v in arrays.items():
        v = np.ascontiguousarray(v)
        feeds[name + "_in"] = v
        args.append(nc.dram_tensor(name + "_in", v.shape, F32, kind="ExternalInput").ap())
    args.append(nc.dram_tensor("out_0", (P, B * NT, D), F32, kind="ExternalOutput").ap())
    args.append(nc.dram_tensor("qkv_scratch", (3, B, M, P, T), F32, kind="Internal").ap())
    args.append(nc.dram_tensor("ab_scratch", (2 * H, B, T), F32, kind="Internal").ap())
    args.append(nc.dram_tensor("y_scratch", (B, M, P, T), F32, kind="Internal").ap())
    args.append(nc.dram_tensor("gates_scratch", (1, 2 * B * D), F32, kind="Internal").ap())
    adaln_delta_moe(nc, *args)
    r = run_bass_kernel_spmd(nc, [feeds], core_ids=[0])
    got = np.asarray(r.results[0]["out_0"]).reshape(P, B * NT, D)
    return got.transpose(1, 0, 2).reshape(B, T, D)
```
